# Optimizing a Trainium2 kernel written in Bass

```python
import numpy as np
import jax
import jax.numpy as jnp

def _softmax(x, axis=-1):
    return jax.nn.softmax(x, axis=axis)

def _gelu(x):
    return jax.nn.gelu(x, approximate=True)

def _silu(x):
    return jax.nn.silu(x)

def _sigmoid(x):
    return jax.nn.sigmoid(x)

def _layernorm(x, axis=-1, eps=1e-05):
    m = jnp.mean(x, axis=axis, keepdims=True)
    v = jnp.var(x, axis=axis, keepdims=True)
    return (x - m) / jnp.sqrt(v + eps)

def _scatter_add(tgt, idx, src, axis=0):
    return tgt.at[idx].add(src)

def _segment_sum(src, seg, n):
    return jax.ops.segment_sum(src, seg, n)
kernel_name = 'mk_adaln_d1_jaxref_r8_c11021'

def setup_inputs(seed: int=0):
    np.random.seed(seed)
    _w = jnp.asarray

    def _L0_attn_setup():
        import jax, jax.numpy as jnp
        import numpy as np
        H = 4
        M = 64
        EPS = 1e-05
        CLAMP = 32.0

        def _rope(x):
            B, T, Hh, D = x.shape
            half = D // 2
            inv_freq = 1.0 / 10000.0 ** (jnp.arange(half, dtype=jnp.float32) / half)
            ang = jnp.arange(T, dtype=jnp.float32)[:, None] * inv_freq[None, :]
            cos = jnp.cos(ang)[None, :, None, :]
            sin = jnp.sin(ang)[None, :, None, :]
            x1, x2 = (x[..., :half], x[..., half:])
            return jnp.concatenate([x1 * cos - x2 * sin, x2 * cos + x1 * sin], axis=-1)

        def _forward(hidden_states, Wq, Wk, Wv, Wg, Wo, sk_w1, sk_w2, sk_b2, sv_w1, sv_w2, sv_b2, gnorm_w):
            x = hidden_states
            B, T, D = x.shape
            Dk = D // H
            Dv = D // H
            q = (x @ Wq).reshape(B, T, H, Dk)
            k = (x @ Wk).reshape(B, T, H, Dk)
            v = (x @ Wv).reshape(B, T, H, Dv)
            q = _rope(q)
            k = _rope(k)
            q = q.transpose(0, 2, 1, 3)
            k = k.transpose(0, 2, 1, 3)
            v = v.transpose(0, 2, 1, 3)
            sk = jnp.clip(x @ sk_w1 @ sk_w2 + sk_b2, -CLAMP, CLAMP).reshape(B, T, H, M).transpose(0, 2, 1, 3)
            sv = jnp.clip(x @ sv_w1 @ sv_w2 + sv_b2, -CLAMP, CLAMP).reshape(B, T, H, M).transpose(0, 2, 1, 3)
            scale = Dk ** (-0.5)
            mask = jnp.tril(jnp.ones((T, T), dtype=bool))
            wk = jnp.exp(sk)
            zk = jnp.cumsum(wk, axis=2)
            S = jnp.einsum('bhtd,bhsd->bhts', q, k)
            S = jnp.where(mask, S, 0.0)
            logits = jnp.einsum('bhts,bhsm->bhtm', S, wk) * scale / zk
            p = jax.nn.softmax(logits, axis=-1)
            wv = jnp.exp(sv)
            zv = jnp.cumsum(wv, axis=2)
            A = jnp.einsum('bhtm,bhsm->bhts', p / zv, wv)
            A = jnp.where(mask, A, 0.0)
            o = jnp.einsum('bhts,bhsd->bhtd', A, v)
            o = o.transpose(0, 2, 1, 3)
            g = (x @ Wg).reshape(B, T, H, Dv)
            on = o * jax.lax.rsqrt(jnp.mean(o * o, axis=-1, keepdims=True) + EPS) * gnorm_w
            o = on * g * jax.nn.sigmoid(g)
            return o.reshape(B, T, H * Dv) @ Wo
        key = jax.random.key(seed)
        ks = jax.random.split(key, 10)
        B, T, D = (2, 256, 128)
        low = 16

        def w(k, shape, s=0.02):
            return jax.random.normal(k, shape, dtype=jnp.float32) * s
        return {'hidden_states': jax.random.normal(ks[0], (B, T, D), dtype=jnp.float32), 'Wq': w(ks[1], (D, D)), 'Wk': w(ks[2], (D, D)), 'Wv': w(ks[3], (D, D)), 'Wg': w(ks[4], (D, D)), 'Wo': w(ks[5], (D, D)), 'sk_w1': w(ks[6], (D, low)), 'sk_w2': w(ks[7], (low, H * M)), 'sk_b2': jnp.zeros((H * M,), dtype=jnp.float32), 'sv_w1': w(ks[8], (D, low)), 'sv_w2': w(ks[9], (low, H * M)), 'sv_b2': jnp.zeros((H * M,), dtype=jnp.float32), 'gnorm_w': jnp.ones((D // H,), dtype=jnp.float32)}
    _L0_attn_in = _L0_attn_setup()

    def _L0_ffn_setup():
        import jax, jax.numpy as jnp
        import numpy as np
        EPS = 1e-05

        def _ln_stats(x):
            mu = jnp.mean(x, axis=-1, keepdims=True)
            var = jnp.mean((x - mu) ** 2, axis=-1, keepdims=True)
            return (x - mu) * jax.lax.rsqrt(var + EPS)
        B, S, H, I, E = (2, 256, 128, 512, 8)
        key = jax.random.key(seed)
        ks = jax.random.split(key, 8)
        inp = {'hidden_states': jax.random.normal(ks[0], (B, S, H), dtype=jnp.float32), 'router_ln_w': jnp.ones((H,), jnp.float32), 'router_ln_b': jnp.zeros((H,), jnp.float32), 'router_w': jax.random.normal(ks[1], (H, E), dtype=jnp.float32) * 0.02, 'router_b': jnp.zeros((E,), jnp.float32), 'exp_ln_w': jnp.ones((E, H), jnp.float32), 'exp_ln_b': jnp.zeros((E, H), jnp.float32), 'w1': jax.random.normal(ks[2], (E, H, I), dtype=jnp.float32) * 0.02, 'b1': jnp.zeros((E, I), jnp.float32), 'w2': jax.random.normal(ks[3], (E, I, H), dtype=jnp.float32) * 0.02, 'b2': jnp.zeros((E, H), jnp.float32), 'out_ln_w': jnp.ones((H,), jnp.float32), 'out_ln_b': jnp.zeros((H,), jnp.float32)}
        return inp
    _L0_ffn_in = _L0_ffn_setup()
    _L0_c = _w((lambda *s: np.random.randn(*s).astype(np.float32) * 0.05)(16, 128))
    _L0_wmod = _w((lambda *s: np.random.randn(*s).astype(np.float32) * 0.05)(128, 6 * 128) * 128 ** (-0.5))
    _d = {'L0_attn_hidden_states': _L0_attn_in['hidden_states'], 'L0_attn_Wq': _L0_attn_in['Wq'], 'L0_attn_Wk': _L0_attn_in['Wk'], 'L0_attn_Wv': _L0_attn_in['Wv'], 'L0_attn_Wg': _L0_attn_in['Wg'], 'L0_attn_Wo': _L0_attn_in['Wo'], 'L0_attn_sk_w1': _L0_attn_in['sk_w1'], 'L0_attn_sk_w2': _L0_attn_in['sk_w2'], 'L0_attn_sk_b2': _L0_attn_in['sk_b2'], 'L0_attn_sv_w1': _L0_attn_in['sv_w1'], 'L0_attn_sv_w2': _L0_attn_in['sv_w2'], 'L0_attn_sv_b2': _L0_attn_in['sv_b2'], 'L0_attn_gnorm_w': _L0_attn_in['gnorm_w'], 'L0_ffn_router_ln_w': _L0_ffn_in['router_ln_w'], 'L0_ffn_router_ln_b': _L0_ffn_in['router_ln_b'], 'L0_ffn_router_w': _L0_ffn_in['router_w'], 'L0_ffn_router_b': _L0_ffn_in['router_b'], 'L0_ffn_exp_ln_w': _L0_ffn_in['exp_ln_w'], 'L0_ffn_exp_ln_b': _L0_ffn_in['exp_ln_b'], 'L0_ffn_w1': _L0_ffn_in['w1'], 'L0_ffn_b1': _L0_ffn_in['b1'], 'L0_ffn_w2': _L0_ffn_in['w2'], 'L0_ffn_b2': _L0_ffn_in['b2'], 'L0_ffn_out_ln_w': _L0_ffn_in['out_ln_w'], 'L0_ffn_out_ln_b': _L0_ffn_in['out_ln_b'], 'L0_c': _L0_c, 'L0_wmod': _L0_wmod}
    _x0 = _d['L0_attn_hidden_states']
    _d['L0_attn_hidden_states'] = jax.random.normal(jax.random.fold_in(jax.random.key(seed), 1), (16, 256, 128), dtype=_x0.dtype)
    del _x0
    return _d

def reference(L0_attn_hidden_states, L0_attn_Wq, L0_attn_Wk, L0_attn_Wv, L0_attn_Wg, L0_attn_Wo, L0_attn_sk_w1, L0_attn_sk_w2, L0_attn_sk_b2, L0_attn_sv_w1, L0_attn_sv_w2, L0_attn_sv_b2, L0_attn_gnorm_w, L0_ffn_router_ln_w, L0_ffn_router_ln_b, L0_ffn_router_w, L0_ffn_router_b, L0_ffn_exp_ln_w, L0_ffn_exp_ln_b, L0_ffn_w1, L0_ffn_b1, L0_ffn_w2, L0_ffn_b2, L0_ffn_out_ln_w, L0_ffn_out_ln_b, L0_c, L0_wmod):

    def _L0_attn_ref(hidden_states, Wq, Wk, Wv, Wg, Wo, sk_w1, sk_w2, sk_b2, sv_w1, sv_w2, sv_b2, gnorm_w):
        import jax, jax.numpy as jnp
        import numpy as np
        H = 4
        M = 64
        EPS = 1e-05
        CLAMP = 32.0

        def _rope(x):
            B, T, Hh, D = x.shape
            half = D // 2
            inv_freq = 1.0 / 10000.0 ** (jnp.arange(half, dtype=jnp.float32) / half)
            ang = jnp.arange(T, dtype=jnp.float32)[:, None] * inv_freq[None, :]
            cos = jnp.cos(ang)[None, :, None, :]
            sin = jnp.sin(ang)[None, :, None, :]
            x1, x2 = (x[..., :half], x[..., half:])
            return jnp.concatenate([x1 * cos - x2 * sin, x2 * cos + x1 * sin], axis=-1)

        def _forward(hidden_states, Wq, Wk, Wv, Wg, Wo, sk_w1, sk_w2, sk_b2, sv_w1, sv_w2, sv_b2, gnorm_w):
            x = hidden_states
            B, T, D = x.shape
            Dk = D // H
            Dv = D // H
            q = (x @ Wq).reshape(B, T, H, Dk)
            k = (x @ Wk).reshape(B, T, H, Dk)
            v = (x @ Wv).reshape(B, T, H, Dv)
            q = _rope(q)
            k = _rope(k)
            q = q.transpose(0, 2, 1, 3)
            k = k.transpose(0, 2, 1, 3)
            v = v.transpose(0, 2, 1, 3)
            sk = jnp.clip(x @ sk_w1 @ sk_w2 + sk_b2, -CLAMP, CLAMP).reshape(B, T, H, M).transpose(0, 2, 1, 3)
            sv = jnp.clip(x @ sv_w1 @ sv_w2 + sv_b2, -CLAMP, CLAMP).reshape(B, T, H, M).transpose(0, 2, 1, 3)
            scale = Dk ** (-0.5)
            mask = jnp.tril(jnp.ones((T, T), dtype=bool))
            wk = jnp.exp(sk)
            zk = jnp.cumsum(wk, axis=2)
            S = jnp.einsum('bhtd,bhsd->bhts', q, k)
            S = jnp.where(mask, S, 0.0)
            logits = jnp.einsum('bhts,bhsm->bhtm', S, wk) * scale / zk
            p = jax.nn.softmax(logits, axis=-1)
            wv = jnp.exp(sv)
            zv = jnp.cumsum(wv, axis=2)
            A = jnp.einsum('bhtm,bhsm->bhts', p / zv, wv)
            A = jnp.where(mask, A, 0.0)
            o = jnp.einsum('bhts,bhsd->bhtd', A, v)
            o = o.transpose(0, 2, 1, 3)
            g = (x @ Wg).reshape(B, T, H, Dv)
            on = o * jax.lax.rsqrt(jnp.mean(o * o, axis=-1, keepdims=True) + EPS) * gnorm_w
            o = on * g * jax.nn.sigmoid(g)
            return o.reshape(B, T, H * Dv) @ Wo
        return _forward(hidden_states, Wq, Wk, Wv, Wg, Wo, sk_w1, sk_w2, sk_b2, sv_w1, sv_w2, sv_b2, gnorm_w)

    def _L0_ffn_ref(hidden_states, router_ln_w, router_ln_b, router_w, router_b, exp_ln_w, exp_ln_b, w1, b1, w2, b2, out_ln_w, out_ln_b):
        import jax, jax.numpy as jnp
        import numpy as np
        EPS = 1e-05

        def _ln_stats(x):
            mu = jnp.mean(x, axis=-1, keepdims=True)
            var = jnp.mean((x - mu) ** 2, axis=-1, keepdims=True)
            return (x - mu) * jax.lax.rsqrt(var + EPS)
        K = 2
        x = hidden_states
        xhat = _ln_stats(x)
        router_logits = (xhat * router_ln_w + router_ln_b) @ router_w + router_b
        routing_weights, selected = jax.lax.top_k(router_logits, K)
        routing_weights = jax.nn.softmax(routing_weights, axis=-1)
        xn = xhat[None] * exp_ln_w[:, None, None, :] + exp_ln_b[:, None, None, :]
        h = jnp.einsum('ebsh,ehi->ebsi', xn, w1) + b1[:, None, None, :]
        h = jax.nn.gelu(h, approximate=False)
        eo = jnp.einsum('ebsi,eih->ebsh', h, w2) + b2[:, None, None, :]
        eo = jnp.moveaxis(eo, 0, 2)
        gathered = jnp.take_along_axis(eo, selected[..., None], axis=2)
        combined = jnp.sum(routing_weights[..., None] * gathered, axis=2)
        return _ln_stats(combined) * out_ln_w + out_ln_b
    x = L0_attn_hidden_states
    mod = (_silu(L0_c) @ L0_wmod).reshape(L0_c.shape[0], 6, 1, -1)
    sa, ca, ga, sb, cb, gb = (mod[:, 0], mod[:, 1], mod[:, 2], mod[:, 3], mod[:, 4], mod[:, 5])
    ga = (2 * (ga >= 0) - 1) * jnp.maximum(jnp.abs(ga), 0.25)
    gb = (2 * (gb >= 0) - 1) * jnp.maximum(jnp.abs(gb), 0.25)
    h = _layernorm(x, axis=-1) * (1 + ca) + sa
    x = x + ga * _L0_attn_ref(h, L0_attn_Wq, L0_attn_Wk, L0_attn_Wv, L0_attn_Wg, L0_attn_Wo, L0_attn_sk_w1, L0_attn_sk_w2, L0_attn_sk_b2, L0_attn_sv_w1, L0_attn_sv_w2, L0_attn_sv_b2, L0_attn_gnorm_w)
    h = _layernorm(x, axis=-1) * (1 + cb) + sb
    x = x + gb * _L0_ffn_ref(h, L0_ffn_router_ln_w, L0_ffn_router_ln_b, L0_ffn_router_w, L0_ffn_router_b, L0_ffn_exp_ln_w, L0_ffn_exp_ln_b, L0_ffn_w1, L0_ffn_b1, L0_ffn_w2, L0_ffn_b2, L0_ffn_out_ln_w, L0_ffn_out_ln_b)
    return x

_drawn_inputs = setup_inputs


def setup_inputs(seed=0):
    import zlib

    import numpy as np

    out = dict(_drawn_inputs(seed))
    spreads = {'L0_attn_sk_b2': (0.0, 0.8),
     'L0_attn_sv_b2': (0.0, 0.8),
     'L0_attn_gnorm_w': (1.0, 0.6),
     'L0_ffn_router_ln_w': (1.0, 0.2),
     'L0_ffn_router_ln_b': (0.0, 0.1),
     'L0_ffn_router_b': (0.0, 0.1),
     'L0_ffn_exp_ln_w': (1.0, 0.6),
     'L0_ffn_exp_ln_b': (0.0, 0.662),
     'L0_ffn_b1': (0.0, 0.1),
     'L0_ffn_b2': (0.0, 0.1),
     'L0_ffn_out_ln_w': (1.0, 0.2),
     'L0_ffn_out_ln_b': (0.0, 0.339)}
    factors = {'L0_attn_Wq': 8.0,
     'L0_attn_Wk': 8.0,
     'L0_attn_Wv': 2.851,
     'L0_attn_Wg': 2.966,
     'L0_attn_Wo': 2.755,
     'L0_attn_sk_w1': 8.0,
     'L0_attn_sk_w2': 8.0,
     'L0_attn_sv_w1': 8.0,
     'L0_attn_sv_w2': 8.0}
    for name, (base, spread) in spreads.items():
        noise = np.random.default_rng([zlib.crc32(name.encode()), seed]).standard_normal(out[name].shape)
        drawn = base * np.exp(spread * noise) if base else spread * noise
        out[name] = jnp.asarray(drawn.astype(out[name].dtype))
    for name, factor in factors.items():
        out[name] = (out[name] * factor).astype(out[name].dtype)
    return out
```

```python
import numpy as np
from contextlib import ExitStack

import concourse.bass as bass
from concourse import mybir

F32 = mybir.dt.float32
BF16 = mybir.dt.bfloat16
U32 = mybir.dt.uint32
ACT = mybir.ActivationFunctionType
ALU = mybir.AluOpType
AX = mybir.AxisListType

P = 128
NB = 16
T = 256
D = 128
H = 4
HD = D // H
M = 64
LOW = 16
NE = 8
FF = 512
NC = FF // P
NT = NB * T // P
EPS = 1e-5
CLAMP = 32.0
UNROLL = 4
PEEL = 4
LAST_LAG = 4


def build(nc, inp, out, debug=None):
    with ExitStack() as ctx:
        def sb(name, shape, dt=F32):
            return ctx.enter_context(nc.sbuf_tensor(name, shape, dt))

        def sem(name):
            return ctx.enter_context(nc.semaphore(name))

        banks = [ctx.enter_context(nc.psum_tensor(f"bank{i}", [P, 512], F32)) for i in range(8)]
        b3, b4, b5, b6, b7 = banks[3:]

        x_sb = sb("x_sb", [P, NT, D])
        Wq, Wqr, Wk, Wkr, Wv, Wg, Wo, Wog = [sb(n, [P, D]) for n in ("Wq", "Wqr", "Wk", "Wkr", "Wv", "Wg", "Wo", "Wog")]
        low1 = sb("low1", [P, 2 * LOW])
        low2 = sb("low2", [P, 4, P])
        cosT, sinT = sb("cosT", [P, T]), sb("sinT", [P, T])
        ident = sb("ident", [P, P])
        headmean = sb("headmean", [P, P])
        ones = sb("ones", [P, T])
        halves = sb("halves", [P, 2])
        vec_rows = sb("vec_rows", [P, D])
        vecT = sb("vecT", [P, 96])
        cT = sb("cT", [P, 4, NB])
        wmod = sb("wmod", [P, 6 * D])
        saT, caT = sb("saT", [P, NB]), sb("caT", [P, NB])
        mod_rows = sb("mod_rows", [NB, 4 * D])
        mod_tmp = sb("mod_tmp", [NB, 2, 2, D])
        modb = sb("modb", [P, 4, 3 * D])
        routw = sb("routw", [P, NE])
        routwg = sb("routwg", [P, NE])
        mod_dram = nc.dram_tensor("mod_dram", [NB, 4 * D], F32, kind="Internal").ap()
        R_LNW, R_LNB, R_RW, R_RB, R_GN, R_C, R_B1 = 0, 8, 16, 17, 18, 32, 48
        NROW = R_B1 + NE * NC
        GA, SB_, CB, GB = 0, 1, 2, 3

        w1s = sb("w1s", [P, NE, FF])
        w2s = sb("w2s", [P, NE, NC, D])
        rbias = sb("rbias", [P, NE])
        rlog = sb("rlog", [P, NT, NE])
        xT_all = sb("xT_all", [P, NB, T])
        outer, ctx = ctx, ExitStack()
        mv1 = sb("mv1", [P, 2, 2]); st1 = sb("st1", [P, 2, 6]); ve1 = sb("ve1", [P, 2]); rs1 = sb("rs1", [P, 2])
        mv2 = sb("mv2", [P, 2, 2]); st2 = sb("st2", [P, 2, 6]); ve2 = sb("ve2", [P, 2]); rs2 = sb("rs2", [P, 2])
        mv3 = sb("mv3", [P, 2, 2]); st3 = sb("st3", [P, 2, 6]); ve3 = sb("ve3", [P, 2]); rs3 = sb("rs3", [P, 2])
        xn = sb("xn", [P, 2, 2, D])
        hT = sb("hT", [P, 2, T])
        rot = sb("rot", [P, 2, 4, T])
        Qx = sb("Qx", [P, 2, H, T])
        qT = sb("qT", [P, T])
        headmask = sb("headmask", [P, H, 2])
        kT = sb("kT", [P, 2, T])
        lT = sb("lT", [P, 2, T])
        v_tok = sb("v_tok", [P, 4, 2, D])
        g_sb, eg = sb("g_sb", [P, 2, T]), sb("eg", [P, 2, T])
        gate = sb("gate", [P, 4, T])
        wkT = sb("wkT", [P, 2, 2, T])
        wvT = sb("wvT", [P, 4, 2, T])
        z = sb("z", [P, 2, 4, T])
        r0 = sb("r0", [P, 4, T])
        rz = sb("rz", [P, 2, 4, T])
        wk_tok = sb("wk_tok", [P, 2, 2, H * M])
        S_sb = sb("S_sb", [P, 3, 512])
        A_sb = sb("A_sb", [P, 3, 512])
        eps_col = sb("eps_col", [P, 1])[:]
        lg2 = sb("lg2", [P, 2, 2, T])
        mx = sb("mx", [P, 2, H]); rsum = sb("rsum", [P, 2, H])
        lgs = sb("lgs", [P, 2, 2, H * M])
        Px = sb("Px", [P, 2, H, T])
        sq = sb("sq", [P, T]); rs = sb("rs", [P, T]); onT1 = sb("onT1", [P, T]); onT = sb("onT", [P, 2, T])
        Wob = sb("Wob", [P, 2, D])
        xn2 = sb("xn2", [P, 2, D]); h2 = sb("h2", [P, 2, D]); h2a = sb("h2a", [P, 2, D])
        xhat = sb("xhat", [P, 2, 2, D])
        xhatT = sb("xhatT", [P, 2, T])

        names = """ld_x ld_w ld_rows ld_ffn set_pool set_dve set_zero low2_ld vec_tp vec_rdy silu_e silu_rdy mod_mm mod_rdy mod_st q_rdy modb_ld0 modb_ld1 modb_ld2 modb_ld3
            wkT_tp out_mm pT_tp s_mm xT_tp xhatT_tp qk_mm v_mm rlog_mm lg_mm a_mm glt_mm lgtok_tp oT_mm skv_mm ms_mm
            lnz_rdy r0_rdy wk_tok_rdy s_copied hT_rdy xhatT_rdy v_rdy rlog_rdy a_copied lT_rdy eg_rdy sq_rdy wexp_rdy pexp_rdy
            rsln_rdy rs_rdy sigln_rdy sig_rdy
            st1_rdy mv1_rdy ve1_rdy xn_rdy px_rdy nu_rdy rz_rdy x1_rdy st2_rdy mv2_rdy ve2_rdy xn2_rdy h2a_rdy h2_rdy st3_rdy mv3_rdy ve3_rdy
            xhat_rdy ropemul_rdy lg2_rdy mx_rdy lgsub_rdy t1_rdy on_rdy sum_rdy rsum_rdy clip_rdy z_rdy
            rstd1_rdy gate_rdy wob_rdy rstd2_rdy s_masked rope_rdy rstd3_rdy a_masked egc_rdy pnorm_rdy xhat_kept dve_chain dbg""".split()
        S = {n: sem(n) for n in names}

        def need(eng, name, batch):
            if isinstance(batch, int) and not 0 <= batch < NB:
                return
            eng.wait_ge(S[name], batch + 1)

        def need_apart(eng, name, batch):
            eng.wait_ge(S["vec_tp"], 1)
            need(eng, name, batch)

        def live(batch):
            return not isinstance(batch, int) or 0 <= batch < NB

        def pipeline(eng, iteration):
            for i in range(PEEL):
                iteration(i, i % UNROLL)
            with eng.Fori(PEEL // UNROLL, NB // UNROLL) as n:
                for k in range(UNROLL):
                    iteration(n * UNROLL + k, k)
            for i in range(NB, NB + LAST_LAG + 1):
                iteration(i, i % UNROLL)

        def slot_loads(batch, slot):
            if isinstance(batch, int):
                return 16 * (batch // 4 + 1)
            return (batch - slot + 4) * 4

        block = ctx.enter_context(nc.Block())

        @block.sync
        def _(sp):
            xv = inp["x"].rearrange("b (c p) d -> p (b c) d", p=P)
            for n, sl in ((0, slice(0, 4)), (1, slice(4, NT))):
                sp.dma_start(x_sb[:, sl, :], xv[:, sl, :]).then_inc(S["ld_x"], 16)
            for dst, name in ((Wq, "Wq"), (Wk, "Wk")):
                sp.dma_start(dst[:], inp[name]).then_inc(S["ld_w"], 16)
            for dst, name in ((Wqr, "Wq"), (Wkr, "Wk")):
                dv = dst[:].rearrange("p (h two c) -> p h two c", h=H, two=2)
                sv = inp[name].rearrange("p (h two c) -> p h two c", h=H, two=2)
                for half in range(2):
                    sp.dma_start(dv[:, :, half, :], sv[:, :, 1 - half, :]).then_inc(S["ld_w"], 16)
            for dst, name in ((Wv, "Wv"), (Wg, "Wg"), (Wo, "Wo"), (cosT, "cosT"), (sinT, "sinT"), (routw, "router_w")):
                sp.dma_start(dst[:], inp[name]).then_inc(S["ld_w"], 16)
            sp.dma_start(low1[:, 0:LOW], inp["sk_w1"]).then_inc(S["ld_w"], 16)
            sp.dma_start(low1[:, LOW:2 * LOW], inp["sv_w1"]).then_inc(S["ld_w"], 16)
            sp.dma_start(rbias[:], inp["router_b"].partition_broadcast(P)).then_inc(S["ld_w"], 16)
            sp.dma_start(w1s[:], inp["w1"].rearrange("e d i -> d e i")).then_inc(S["ld_ffn"], 16)
            sp.dma_start(w2s[:], inp["w2"].rearrange("e (c p) d -> p e c d", p=P)).then_inc(S["ld_ffn"], 16)
            sp.wait_ge(S["mod_rdy"], 1)
            sp.dma_start(mod_dram, mod_rows[:]).then_inc(S["mod_st"], 16)
            sp.wait_ge(S["mod_st"], 16)
            def iteration(i, k):
                if live(i):
                    need(sp, "h2_rdy", i - 4)
                    if isinstance(i, int):
                        src = mod_dram[i, 0:3 * D]
                    else:
                        src = mod_dram[bass.ds(i, 1), 0:3 * D].squeeze(0)
                    sp.dma_start(modb[:, k, :], src.partition_broadcast(P)).then_inc(S[f"modb_ld{k}"], 16)
            pipeline(sp, iteration)
        N_W = 15

        @block.gpsimd
        def _(pool):
            def gate_step(a, k):
                need(pool, "sig_rdy", a)
                nc.gpsimd.tensor_tensor(gate[:, k, :], g_sb[:, k % 2, :], eg[:, k % 2, :], ALU.mult).then_inc(S["gate_rdy"], 1)

            nc.gpsimd.memset(ident[:], 1.0).then_inc(S["set_pool"], 1)
            nc.gpsimd.memset(headmean[:], 1.0 / HD).then_inc(S["set_pool"], 1)
            nc.gpsimd.memset(halves[:], -0.5).then_inc(S["set_pool"], 1)
            nc.gpsimd.memset(headmask[:], 1.0).then_inc(S["set_pool"], 1)
            nc.gpsimd.memset(rs1[:], 1.0).then_inc(S["xhat_kept"], 2)
            pool.wait_ge(S["set_pool"], 4)
            nc.gpsimd.affine_select(out=ident[:], in_=ident[:], compare_op=ALU.is_equal, fill=0.0, base=0,
                                    pattern=[[-1, P]], channel_multiplier=1).then_inc(S["set_pool"], 1)
            for n, hm in enumerate((headmean[:].rearrange("p (h c) -> p h c", h=H), headmask[:])):
                w = hm.shape[2]
                nc.gpsimd.affine_select(out=hm, in_=hm, compare_op=ALU.is_ge, fill=0.0, base=0,
                                        pattern=[[-HD, H], [0, w]], channel_multiplier=1).then_inc(S["set_pool"], 1)
                pool.wait_ge(S["set_pool"], 6 + 2 * n)
                nc.gpsimd.affine_select(out=hm, in_=hm, compare_op=ALU.is_ge, fill=0.0, base=HD - 1,
                                        pattern=[[HD, H], [0, w]], channel_multiplier=-1).then_inc(S["set_pool"], 1)

            def iteration(i, k):
                a, b, c, e, d = i, i - 1, i - 2, i - 3, i - 4
                kb, kc, ke, kd = (k - 1) % 4, (k - 2) % 4, (k - 3) % 4, (k - 4) % 4
                if live(a):
                    need(pool, "ve1_rdy", a)
                    nc.gpsimd.tensor_tensor(rs1[:], ve1[:], halves[:], ALU.pow).then_inc(S["rstd1_rdy"], 1)
                if live(b):
                    gate_step(b, kb)
                if live(c):
                    pool.wait_ge(S[f"modb_ld{kc}"], slot_loads(c, kc))
                    if isinstance(c, int) and c == 0:
                        pool.wait_ge(S["vec_rdy"], 2)
                    need(pool, "out_mm", c - 2)
                    nc.gpsimd.tensor_tensor(Wob[:, kc % 2, :], Wog[:], modb[:, kc, GA * D:(GA + 1) * D],
                                            ALU.mult).then_inc(S["wob_rdy"], 1)
                if live(e):
                    need(pool, "ve2_rdy", e)
                    nc.gpsimd.tensor_tensor(rs2[:], ve2[:], halves[:], ALU.pow).then_inc(S["rstd2_rdy"], 1)
                if live(b):
                    need_apart(pool, "s_copied", b)
                    causal(S_sb, "s_masked")
                if live(a):
                    need(pool, "ropemul_rdy", a)
                    need(pool, "s_mm", a - 2)
                    nc.gpsimd.tensor_tensor(qT[:], rot[:, k % 2, 0, :], rot[:, k % 2, 1, :], ALU.add).then_inc(S["q_rdy"], 1)
                    need_apart(pool, "q_rdy", a)
                    for h in range(H):
                        nc.gpsimd.tensor_scalar(Qx[:, k % 2, h, :], qT[:], headmask[:, h, 0:1], 1.0, ALU.mult, ALU.mult)
                    nc.gpsimd.tensor_tensor(kT[:, k % 2, :], rot[:, k % 2, 2, :], rot[:, k % 2, 3, :],
                                            ALU.add).then_inc(S["rope_rdy"], 1)
                if live(e):
                    need(pool, "ve3_rdy", e)
                    nc.gpsimd.tensor_tensor(rs3[:], ve3[:], halves[:], ALU.pow).then_inc(S["rstd3_rdy"], 1)
                if live(c):
                    need_apart(pool, "a_copied", c)
                    causal(A_sb, "a_masked")
                if live(a):
                    need_apart(pool, "eg_rdy", a)
                    nc.gpsimd.tensor_scalar(eg[:, k % 2, :], eg[:, k % 2, :], 1e18, 0.0, ALU.min, ALU.max).then_inc(S["egc_rdy"], 1)
                if live(b):
                    need(pool, "rsum_rdy", b)
                    for tile in range(2):
                        v = lgs[:, kb % 2, tile, :].rearrange("p (h m) -> p h m", h=H)
                        last = nc.gpsimd.tensor_tensor(v, v, rsum[:, tile, :].unsqueeze(2).broadcast_to([P, H, M]), ALU.mult)
                    last.then_inc(S["pnorm_rdy"], 1)
                if live(d):
                    need(pool, "xhatT_rdy", d)
                    nc.gpsimd.tensor_copy(xT_all[:, bass.ds(d, 1), :].squeeze(1), xhatT[:, kd % 2, :]).then_inc(S["xhat_kept"], 1)

            def causal(buf, name):
                d0 = buf[:, 0:2, :].rearrange("p two (h t) -> p (two h) t", h=2)[:, :, 0:P]
                d1 = buf[:, 2, :].rearrange("p (h t) -> p h t", h=H)
                for d in (d0, d1):
                    last = nc.gpsimd.affine_select(out=d, in_=d, compare_op=ALU.is_ge, fill=0.0, base=0,
                                                   pattern=[[0, H], [1, P]], channel_multiplier=-1)
                last.then_inc(S[name], 1)

            pipeline(pool, iteration)

        @block.scalar
        def _(act):
            nc.scalar.preload_act_table_set("natural_log_exp_and_others")
            act.wait_ge(S["set_zero"], 1)
            rows = ((R_LNW, NE, "exp_ln_w"), (R_LNB, NE, "exp_ln_b"), (R_B1, NE * NC, "b1"), (R_RW, 1, "router_ln_w"), (R_RB, 1, "router_ln_b"), (R_C, NB, "c"))
            for r, n, name in rows:
                src = inp[name] if n > 1 else inp[name].unsqueeze(0)
                if name == "b1":
                    src = src.rearrange("e (c p) -> (e c) p", p=P)
                act.dma_start(vec_rows[r:r + n, :], src).then_inc(S["ld_rows"], 16)
            for h in range(H):
                act.dma_start(vec_rows[R_GN:R_GN + 1, h * HD:(h + 1) * HD], inp["gnorm_w"].unsqueeze(0)).then_inc(S["ld_rows"], 16)
            act.dma_start(wmod[:], inp["wmod"]).then_inc(S["ld_rows"], 16)
            for n, w2, bias in ((0, "sk_w2", "sk_b2"), (1, "sv_w2", "sv_b2")):
                act.dma_start(low2[n * LOW:(n + 1) * LOW, 2 * n:2 * n + 2, :],
                              inp[w2].rearrange("r (a c) -> r a c", a=2)).then_inc(S["low2_ld"], 16)
                act.dma_start(low2[2 * LOW:2 * LOW + 1, 2 * n:2 * n + 2, :],
                              inp[bias].unsqueeze(0).rearrange("o (a c) -> o a c", a=2)).then_inc(S["low2_ld"], 16)
            act.wait_ge(S["vec_rdy"], 1)
            nc.scalar.activation(cT[:, 1, :], cT[:, 0, :], ACT.Exp, scale=-1.0).then_inc(S["silu_e"], 1)

            def iteration(i, k):
                a, b, c, e, d = i, i - 1, i - 2, i - 3, i - 4
                kb, kc, kd = (k - 1) % 4, (k - 2) % 4, (k - 4) % 4
                if live(b):
                    need(act, "z_rdy", b)
                    need(act, "rz_rdy", b - 1)
                    nc.scalar.activation(r0[:], z[:, kb % 2, :, :], ACT.Ln).then_inc(S["lnz_rdy"], 1)
                    need(act, "wkT_tp", b)
                    need(act, "lg_mm", b - 2)
                    nc.scalar.copy(wk_tok[:, kb % 2, :, :], b3[:].rearrange("p (c n) -> p c n", c=2)).then_inc(S["wk_tok_rdy"], 1)
                    need(act, "lnz_rdy", b)
                    nc.scalar.activation(r0[:], r0[:], ACT.Exp, scale=-1.0).then_inc(S["r0_rdy"], 1)
                    need(act, "s_mm", b)
                    for n in range(3):
                        last = nc.scalar.copy(S_sb[:, n, :], banks[n][:])
                    last.then_inc(S["s_copied"], 1)
                if live(a):
                    if isinstance(a, int) and a == 0:
                        act.wait_ge(S["mod_rdy"], 1)
                    need(act, "xT_tp", a)
                    need(act, "glt_mm", a - 2)
                    nc.scalar.activation(hT[:, k % 2, :], b3[:, 0:T], ACT.Identity, bias=saT[:, bass.ds(a, 1)],
                                         scale=caT[:, bass.ds(a, 1)]).then_inc(S["hT_rdy"], 1)
                if live(d):
                    need(act, "xhatT_tp", d)
                    act.wait_ge(S["xhat_kept"], d - 2 + 1 + 2)
                    nc.scalar.copy(xhatT[:, kd % 2, :], b3[:, T:2 * T]).then_inc(S["xhatT_rdy"], 1)
                if live(a):
                    need(act, "v_mm", a)
                    need(act, "oT_mm", a - 4)
                    nc.scalar.copy(v_tok[:, k, :, :], b3[:, 0:T].rearrange("p (c n) -> p c n", c=2)).then_inc(S["v_rdy"], 1)
                if live(d):
                    need(act, "rlog_mm", d)
                    nc.scalar.copy(rlog[:, bass.ds(d * 2, 2), :], b3[:, T:T + 2 * NE].rearrange("p (c n) -> p c n", c=2)).then_inc(S["rlog_rdy"], 1)
                if live(c):
                    need(act, "a_mm", c)
                    need(act, "oT_mm", c - 2)
                    for n in range(3):
                        last = nc.scalar.copy(A_sb[:, n, :], banks[n][:])
                    last.then_inc(S["a_copied"], 1)
                if live(a):
                    need(act, "glt_mm", a)
                    need(act, "skv_mm", a - 2)
                    nc.scalar.copy(lT[0:2 * LOW, k % 2, :], b3[0:2 * LOW, T:2 * T]).then_inc(S["lT_rdy"], 1)
                    need(act, "gate_rdy", a - 2)
                    nc.scalar.copy(g_sb[:, k % 2, :], b3[:, 0:T])
                    nc.scalar.activation(eg[:, k % 2, :], b3[:, 0:T], ACT.Exp, scale=-1.0).then_inc(S["eg_rdy"], 1)
                if live(c):
                    need(act, "oT_mm", c)
                    need(act, "ms_mm", c - 1)
                    nc.scalar.activation(sq[:], b7[:, 0:T], ACT.Square).then_inc(S["sq_rdy"], 1)
                if live(a):
                    need(act, "skv_mm", a)
                    need(act, "a_mm", a - 4)
                    nc.scalar.activation(wkT[:, k % 2, :, :], b4[:].rearrange("p (c n) -> p c n", c=2), ACT.Exp)
                    nc.scalar.activation(wvT[:, k, :, :], b5[:].rearrange("p (c n) -> p c n", c=2), ACT.Exp).then_inc(S["wexp_rdy"], 1)
                if live(b):
                    need(act, "lgsub_rdy", b)
                    nc.scalar.activation(lgs[:, kb % 2, :, :], lgs[:, kb % 2, :, :], ACT.Exp).then_inc(S["pexp_rdy"], 1)
                if live(c):
                    need(act, "ms_mm", c)
                    need(act, "t1_rdy", c - 1)
                    nc.scalar.activation(rs[:], b6[:, 0:T], ACT.Ln, bias=eps_col).then_inc(S["rsln_rdy"], 1)
                    need(act, "rsln_rdy", c)
                    nc.scalar.activation(rs[:], rs[:], ACT.Exp, scale=-0.5).then_inc(S["rs_rdy"], 1)
                if live(a):
                    need(act, "egc_rdy", a)
                    nc.scalar.activation(eg[:, k % 2, :], eg[:, k % 2, :], ACT.Ln, bias=1.0).then_inc(S["sigln_rdy"], 1)
                    need(act, "sigln_rdy", a)
                    nc.scalar.activation(eg[:, k % 2, :], eg[:, k % 2, :], ACT.Exp, scale=-1.0).then_inc(S["sig_rdy"], 1)

            pipeline(act, iteration)

        @block.vector
        def _(dve):
            chain = [0]

            def link(ins):
                chain[0] += 1
                ins.then_inc(S["dve_chain"], 1)
                dve.wait_ge(S["dve_chain"], chain[0])

            link(nc.vector.memset(vec_rows[:], 0.0))
            nc.vector.memset(low2[:], 0.0).then_inc(S["set_zero"], 1)
            nc.vector.memset(ones[:], 1.0)
            nc.vector.memset(eps_col, EPS)
            nc.vector.memset(Qx[:], 0.0)
            nc.vector.memset(Px[:], 0.0)
            link(nc.vector.memset(lT[:], 0.0))
            nc.vector.memset(lT[2 * LOW:2 * LOW + 1, :, :], 1.0).then_inc(S["set_dve"], 1)
            dve.wait_ge(S["vec_tp"], 1)
            link(nc.vector.tensor_copy(vecT[:, 0:NROW], b3[:, 0:NROW]))
            nc.vector.tensor_copy(cT[:, 0, :], vecT[:, R_C:R_C + NB]).then_inc(S["vec_rdy"], 1)
            dve.wait_ge(S["ld_w"], 16 * N_W)
            nc.vector.tensor_scalar(Wog[:], Wo[:], vecT[:, R_GN:R_GN + 1], None, ALU.mult)
            nc.vector.tensor_scalar(routwg[:], routw[:], vecT[:, R_RW:R_RW + 1], None, ALU.mult).then_inc(S["vec_rdy"], 1)
            dve.wait_ge(S["silu_e"], 1)
            link(nc.vector.tensor_scalar(cT[:, 1, :], cT[:, 1, :], 1.0, None, ALU.add))
            link(nc.vector.reciprocal(cT[:, 2, :], cT[:, 1, :]))
            nc.vector.tensor_tensor(cT[:, 3, :], cT[:, 0, :], cT[:, 2, :], ALU.mult).then_inc(S["silu_rdy"], 1)
            dve.wait_ge(S["mod_mm"], 1)
            nc.vector.tensor_copy(saT[:], b3[:, 0:NB])
            nc.vector.tensor_scalar(caT[:], b3[:, NB:2 * NB], 1.0, None, ALU.add)
            for n, m in ((0, GA), (1, GB)):
                g = b4[0:NB, m * D:(m + 1) * D]
                link(nc.vector.tensor_copy(mod_tmp[:, n, 0, :], g))
                link(nc.vector.scalar_tensor_tensor(out=mod_tmp[:, n, 1, :], in0=mod_tmp[:, n, 0, :], scalar=-1.0,
                                                    in1=mod_tmp[:, n, 0, :], op0=ALU.mult, op1=ALU.max))
                nc.vector.tensor_scalar(mod_tmp[:, n, 1, :], mod_tmp[:, n, 1, :], 0.25, None, ALU.max)
                link(nc.vector.tensor_scalar(mod_tmp[:, n, 0, :], mod_tmp[:, n, 0, :], 0.0, 2.0, ALU.is_ge, ALU.mult))
                nc.vector.scalar_tensor_tensor(out=mod_rows[:, m * D:(m + 1) * D], in0=mod_tmp[:, n, 0, :], scalar=-1.0,
                                               in1=mod_tmp[:, n, 1, :], op0=ALU.add, op1=ALU.mult)
            nc.vector.tensor_copy(mod_rows[:, SB_ * D:(SB_ + 1) * D], b4[0:NB, SB_ * D:(SB_ + 1) * D])
            nc.vector.tensor_scalar(mod_rows[:, CB * D:(CB + 1) * D], b4[0:NB, CB * D:(CB + 1) * D], 1.0, None,
                                    ALU.add).then_inc(S["mod_rdy"], 1)

            def ln_sums(src2, st, n):
                for tile in range(2):
                    last = nc.vector.bn_stats(st[:, tile, :], src2[tile])
                last.then_inc(S[f"st{n}_rdy"], 1)

            def ln_moments(st, mv, ve, b, n):
                for tile in range(2):
                    last = nc.vector.bn_aggr(mv[:, tile, :], st[:, tile, :])
                last.then_inc(S[f"mv{n}_rdy"], 1)
                need(dve, f"mv{n}_rdy", b)
                nc.vector.tensor_scalar(ve[:], mv[:, :, 1], EPS, None, ALU.add).then_inc(S[f"ve{n}_rdy"], 1)

            def ln_stats(src2, st, mv, ve, b, n):
                ln_sums(src2, st, n)
                need_apart(dve, f"st{n}_rdy", b)
                ln_moments(st, mv, ve, b, n)

            def normalize(dst2, src2, mv, r, name):
                for tile in range(2):
                    last = nc.vector.tensor_scalar(dst2[tile], src2[tile], mv[:, tile, 0:1], r[:, tile:tile + 1],
                                                   ALU.subtract, ALU.mult)
                last.then_inc(S[name], 1)

            def x_tile(b, tile):
                return x_sb[:, bass.ds(b * 2 + tile, 1), :].squeeze(1) if not isinstance(b, int) else x_sb[:, b * 2 + tile, :]

            def iteration(i, k):
                a, b, c, e = i, i - 1, i - 2, i - 3
                kb, kc, ke = (k - 1) % 4, (k - 2) % 4, (k - 3) % 4
                if live(a):
                    if isinstance(a, int) and a == 0:
                        dve.wait_ge(S["ld_x"], 32)
                    ln_sums([x_tile(a, 0), x_tile(a, 1)], st1, 1)
                    need(dve, "st1_rdy", a)
                if live(c):
                    need(dve, "pT_tp", c)
                    need(dve, "a_mm", c - 2)
                    for pair in range(2):
                        for half in range(2):
                            q = slice(half * M, (half + 1) * M)
                            last = nc.vector.scalar_tensor_tensor(
                                out=Px[q, kc % 2, 2 * pair + half, :], in0=b6[q, pair * T:(pair + 1) * T], scalar=-1.0,
                                in1=rz[q, kc % 2, 2 + pair, :], op0=ALU.mult, op1=ALU.mult)
                    last.then_inc(S["px_rdy"], 1)
                if live(a):
                    ln_moments(st1, mv1, ve1, a, 1)
                    need(dve, "rstd1_rdy", a)
                    need(dve, "xT_tp", a - 2)
                    normalize([xn[:, k % 2, t, :] for t in range(2)], [x_tile(a, 0), x_tile(a, 1)], mv1, rs1, "xn_rdy")
                if live(b):
                    need(dve, "r0_rdy", b)
                    nc.vector.tensor_tensor(z[:, kb % 2, :, :], z[:, kb % 2, :, :], r0[:], ALU.mult).then_inc(S["nu_rdy"], 1)
                    need(dve, "nu_rdy", b)
                    nc.vector.scalar_tensor_tensor(out=rz[:, kb % 2, :, :], in0=z[:, kb % 2, :, :], scalar=-2.0, in1=r0[:],
                                                   op0=ALU.add, op1=ALU.mult).then_inc(S["rz_rdy"], 1)
                if live(e):
                    need(dve, "out_mm", e)
                    xe = x_sb[:, bass.ds(e * 2, 2), :]
                    nc.vector.tensor_tensor(xe, xe, b7[:, 0:T].rearrange("p (c n) -> p c n", c=2), ALU.add).then_inc(S["x1_rdy"], 1)
                    need_apart(dve, "x1_rdy", e)
                    ln_stats([x_tile(e, 0), x_tile(e, 1)], st2, mv2, ve2, e, 2)
                if live(a):
                    need(dve, "qk_mm", a)
                    need(dve, "rope_rdy", a - 2)
                    for n, bank in ((0, b4), (2, b5)):
                        nc.vector.tensor_tensor(rot[:, k % 2, n, :], bank[:, 0:T], cosT[:], ALU.mult)
                        last = nc.vector.tensor_tensor(rot[:, k % 2, n + 1, :], bank[:, T:2 * T], sinT[:], ALU.mult)
                    last.then_inc(S["ropemul_rdy"], 1)
                if live(e):
                    need(dve, "rstd2_rdy", e)
                    normalize([xn2[:, t, :] for t in range(2)], [x_tile(e, 0), x_tile(e, 1)], mv2, rs2, "xn2_rdy")
                    need(dve, "xn2_rdy", e)
                    cb = modb[:, ke, CB * D:(CB + 1) * D].unsqueeze(1).broadcast_to([P, 2, D])
                    sbb = modb[:, ke, SB_ * D:(SB_ + 1) * D].unsqueeze(1).broadcast_to([P, 2, D])
                    nc.vector.tensor_tensor(h2a[:], xn2[:], cb, ALU.mult).then_inc(S["h2a_rdy"], 1)
                    need(dve, "h2a_rdy", e)
                    nc.vector.tensor_tensor(h2[:], h2a[:], sbb, ALU.add).then_inc(S["h2_rdy"], 1)
                    need_apart(dve, "h2_rdy", e)
                    ln_stats([h2[:, t, :] for t in range(2)], st3, mv3, ve3, e, 3)
                if live(b):
                    need(dve, "lg_mm", b)
                    need(dve, "lgtok_tp", b - 2)
                    need(dve, "rz_rdy", b)
                    nc.vector.scalar_tensor_tensor(out=lg2[:, kb % 2, :, :], in0=b7[:].rearrange("p (c n) -> p c n", c=2),
                                                   scalar=-float(HD) ** -0.5, in1=rz[:, kb % 2, 0:2, :],
                                                   op0=ALU.mult, op1=ALU.mult).then_inc(S["lg2_rdy"], 1)
                if live(e):
                    need(dve, "rstd3_rdy", e)
                    normalize([xhat[:, ke % 2, t, :] for t in range(2)], [h2[:, t, :] for t in range(2)], mv3, rs3, "xhat_rdy")
                if live(b):
                    need(dve, "lgtok_tp", b)
                    need(dve, "pT_tp", b - 2)
                    lgv = b6[:].rearrange("p (g m) -> p g m", m=M)
                    nc.vector.tensor_reduce(mx[:].rearrange("p c h -> p (c h)"), lgv, AX.X, ALU.max).then_inc(S["mx_rdy"], 1)
                    need(dve, "mx_rdy", b)
                    nc.vector.tensor_tensor(lgs[:, kb % 2, :, :].rearrange("p c (h m) -> p (c h) m", h=H), lgv,
                                            mx[:].rearrange("p c h -> p (c h)").unsqueeze(2).broadcast_to([P, 2 * H, M]),
                                            ALU.subtract).then_inc(S["lgsub_rdy"], 1)
                if live(a):
                    need(dve, "wexp_rdy", a)
                    for w in (wkT[:, k % 2, :, :], wvT[:, k, :, :]):
                        last = nc.vector.tensor_scalar(w, w, float(np.exp(CLAMP)), float(np.exp(-CLAMP)), ALU.min, ALU.max)
                    last.then_inc(S["clip_rdy"], 1)
                if live(b):
                    need(dve, "pexp_rdy", b)
                    need(dve, "pnorm_rdy", b - 1)
                    nc.vector.tensor_reduce(mx[:].rearrange("p c h -> p (c h)"),
                                            lgs[:, kb % 2, :, :].rearrange("p c (h m) -> p (c h) m", h=H), AX.X,
                                            ALU.add).then_inc(S["sum_rdy"], 1)
                    need(dve, "sum_rdy", b)
                    nc.vector.reciprocal(rsum[:], mx[:]).then_inc(S["rsum_rdy"], 1)
                if live(c):
                    need(dve, "rs_rdy", c)
                    need(dve, "out_mm", c - 2)
                    nc.vector.tensor_tensor(onT1[:], b7[:, 0:T], rs[:], ALU.mult).then_inc(S["t1_rdy"], 1)
                    need(dve, "t1_rdy", c)
                    need(dve, "gate_rdy", c)
                    nc.vector.tensor_tensor(onT[:, kc % 2, :], onT1[:], gate[:, kc, :], ALU.mult).then_inc(S["on_rdy"], 1)
                if live(a):
                    need(dve, "clip_rdy", a)
                    for j in range(4):
                        w = wkT[:, k % 2, j, :] if j < 2 else wvT[:, k, j - 2, :]
                        last = nc.vector.tensor_tensor_scan(z[:, k % 2, j, :], ones[:], w, 0.0, ALU.mult, ALU.add)
                    last.then_inc(S["z_rdy"], 1)

            pipeline(dve, iteration)

        @block.tensor
        def _(pe):
            mm, tp = nc.tensor.matmul, nc.tensor.transpose
            pe.wait_ge(S["set_pool"], 9)
            pe.wait_ge(S["ld_rows"], 16 * 11)
            tp(b3[:, 0:P], vec_rows[:], ident[:]).then_inc(S["vec_tp"], 1)
            pe.wait_ge(S["silu_rdy"], 1)
            mm(b3[:, 0:NB], wmod[:, 0:D], cT[:, 3, :], start=True, stop=True)
            mm(b3[:, NB:2 * NB], wmod[:, D:2 * D], cT[:, 3, :], start=True, stop=True)
            mm(b4[0:NB, :], cT[:, 3, :], wmod[:, 2 * D:6 * D], start=True, stop=True).then_inc(S["mod_mm"], 1)
            pe.wait_ge(S["ld_w"], 16 * N_W)
            pe.wait_ge(S["low2_ld"], 64)
            pe.wait_ge(S["set_dve"], 1)
            pe.wait_ge(S["mod_rdy"], 1)

            def iteration(i, k):
                a, b, c, e, d = i, i - 1, i - 2, i - 3, i - 4
                kb, kc, ke, kd = (k - 1) % 4, (k - 2) % 4, (k - 3) % 4, (k - 4) % 4
                if live(b):
                    need(pe, "clip_rdy", b)
                    need(pe, "eg_rdy", b)
                    for ch in range(2):
                        for pair in range(2):
                            last = tp(b3[:, ch * T + pair * P:ch * T + (pair + 1) * P],
                                      wkT[:, kb % 2, pair, ch * P:(ch + 1) * P], ident[:])
                    last.then_inc(S["wkT_tp"], 1)
                if live(e):
                    need(pe, "on_rdy", e)
                    need(pe, "wob_rdy", e)
                    for tile in range(2):
                        last = mm(b7[:, tile * D:(tile + 1) * D], onT[:, ke % 2, tile * P:(tile + 1) * P], Wob[:, ke % 2, :],
                                  start=True, stop=True)
                    last.then_inc(S["out_mm"], 1)
                if live(c):
                    need(pe, "pnorm_rdy", c)
                    need(pe, "rsln_rdy", c - 1)
                    for pair in range(2):
                        for tile in range(2):
                            last = tp(b6[:, pair * T + tile * P:pair * T + (tile + 1) * P],
                                      lgs[:, kc % 2, tile, pair * P:(pair + 1) * P], ident[:])
                    last.then_inc(S["pT_tp"], 1)
                if live(b):
                    need(pe, "rope_rdy", b)
                    need(pe, "a_copied", b - 2)
                    kk = kT[:, kb % 2, :]
                    for n in range(2):
                        mm(banks[n][:], kk[:, 0:P], Qx[:, kb % 2, 2 * n:2 * n + 2, :], start=True, stop=True)
                    mm(banks[2][:], kk[:, P:T], Qx[:, kb % 2, :, P:T], start=True, stop=True).then_inc(S["s_mm"], 1)
                if live(d):
                    need(pe, "xhat_rdy", d)
                    need(pe, "wk_tok_rdy", b)
                    if isinstance(d, int):
                        need(pe, "rlog_rdy", d - 1)
                    for tile in range(2):
                        last = tp(b3[:, T + tile * P:T + (tile + 1) * P], xhat[:, kd % 2, tile, :], ident[:])
                    last.then_inc(S["xhatT_tp"], 1)
                if live(a):
                    need(pe, "xn_rdy", a)
                    need(pe, "wk_tok_rdy", b)
                    for tile in range(2):
                        last = tp(b3[:, tile * P:(tile + 1) * P], xn[:, k % 2, tile, :], ident[:])
                    last.then_inc(S["xT_tp"], 1)
                    need(pe, "hT_rdy", a)
                    need(pe, "wexp_rdy", a - 1)
                    hh = hT[:, k % 2, :]
                    for bank, w, wr in ((b4, Wq, Wqr), (b5, Wk, Wkr)):
                        mm(bank[:, 0:T], w[:], hh, start=True, stop=True)
                        last = mm(bank[:, T:2 * T], wr[:], hh, start=True, stop=True)
                    last.then_inc(S["qk_mm"], 1)
                if live(d):
                    need(pe, "xhatT_rdy", d)
                    for tile in range(2):
                        last = mm(b3[:, T + tile * NE:T + (tile + 1) * NE], xhatT[:, kd % 2, tile * P:(tile + 1) * P], routwg[:],
                                  start=True, stop=True)
                    last.then_inc(S["rlog_mm"], 1)
                if live(a):
                    need(pe, "xhatT_rdy", d)
                    for tile in range(2):
                        last = mm(b3[:, tile * D:(tile + 1) * D], hT[:, k % 2, tile * P:(tile + 1) * P], Wv[:], start=True, stop=True)
                    last.then_inc(S["v_mm"], 1)
                if live(b):
                    need(pe, "s_masked", b)
                    need(pe, "wk_tok_rdy", b)
                    need(pe, "x1_rdy", e)
                    for pair in range(2):
                        for ch in range(2):
                            for half in range(2):
                                h = 2 * pair + half
                                w = wk_tok[:, kb % 2, ch, h * M:(h + 1) * M]
                                o = b7[half * M:(half + 1) * M, pair * T + ch * P:(pair + 1) * T]
                                r = S_sb[:, pair, half * T:(half + 1) * T] if ch == 0 else \
                                    S_sb[:, 2, h * P:(h + 1) * P]
                                last = mm(o, w, r, start=ch == 0, stop=ch == 1)
                    last.then_inc(S["lg_mm"], 1)
                if live(c):
                    need(pe, "px_rdy", c)
                    need(pe, "s_copied", b)
                    for pair in range(2):
                        mm(banks[pair][:], wvT[:, kc, pair, 0:P], Px[:, kc % 2, 2 * pair:2 * pair + 2, :], start=True, stop=True)
                        last = mm(banks[2][:, pair * T:(pair + 1) * T], wvT[:, kc, pair, P:T],
                                  Px[:, kc % 2, 2 * pair:2 * pair + 2, P:T], start=True, stop=True)
                    last.then_inc(S["a_mm"], 1)
                if live(a):
                    need(pe, "v_rdy", a)
                    need(pe, "rlog_rdy", d)
                    mm(b3[0:2 * LOW, T:2 * T], low1[:], hT[:, k % 2, :], start=True, stop=True)
                    mm(b3[:, 0:T], Wg[:], hT[:, k % 2, :], start=True, stop=True).then_inc(S["glt_mm"], 1)
                if live(b):
                    need(pe, "lg2_rdy", b)
                    need(pe, "px_rdy", c)
                    for tile in range(2):
                        for pair in range(2):
                            last = tp(b6[:, tile * T + pair * P:tile * T + (pair + 1) * P],
                                      lg2[:, kb % 2, pair, tile * P:(tile + 1) * P], ident[:])
                    last.then_inc(S["lgtok_tp"], 1)
                if live(c):
                    need(pe, "a_masked", c)
                    need(pe, "lg2_rdy", b)
                    need(pe, "x1_rdy", e)
                    for ch in range(2):
                        for h in range(H):
                            r = A_sb[:, h // 2, (h % 2) * T:(h % 2 + 1) * T] if ch == 0 else A_sb[:, 2, h * P:(h + 1) * P]
                            last = mm(b7[h * HD:(h + 1) * HD, ch * P:T], v_tok[:, kc, ch, h * HD:(h + 1) * HD], r,
                                      start=ch == 0, stop=ch == 1)
                    last.then_inc(S["oT_mm"], 1)
                if live(a):
                    need(pe, "lT_rdy", a)
                    need(pe, "ropemul_rdy", a)
                    for n in range(4):
                        last = mm((b4, b5)[n // 2][:, (n % 2) * T:(n % 2 + 1) * T], low2[:, n, :], lT[:, k % 2, :], start=True, stop=True)
                    last.then_inc(S["skv_mm"], 1)
                if live(c):
                    need(pe, "sq_rdy", c)
                    need(pe, "lgsub_rdy", b)
                    need(pe, "px_rdy", c)
                    mm(b6[:, 0:T], headmean[:], sq[:], start=True, stop=True).then_inc(S["ms_mm"], 1)

            pipeline(pe, iteration)

        ctx.close()
        ctx = outer
        GROUP = 4
        NG = NT // GROUP
        b1T = sb("b1T", [P, NE * NC])
        b2b = sb("b2b", [P, NE, D])
        olw, olb = sb("olw", [P, D]), sb("olb", [P, D])
        gbb = sb("gbb", [P, NB, D])
        iota_e = sb("iota_e", [P, NE])
        top, topi = sb("top", [P, NT, 8]), sb("topi", [P, NT, 8], U32)
        topf = sb("topf", [P, NT, 2])
        pw = sb("pw", [P, NT, 4])
        comb = sb("comb", [P, NT, NE]); comb2 = sb("comb2", [P, NT, NE])
        hid = sb("hid", [P, 2, NC, GROUP * P])
        acc = sb("acc", [P, 2, GROUP, D])
        st4, mv4, ve4, rs4 = sb("st4", [P, GROUP, 6]), sb("mv4", [P, GROUP, 2]), sb("ve4", [P, GROUP]), sb("rs4", [P, GROUP])
        halves4 = sb("halves4", [P, GROUP])
        yn = sb("yn", [P, GROUP, D]); yo = sb("yo", [P, GROUP, D]); yp = sb("yp", [P, GROUP, D])
        names = """f_ld f_ops f_w1 f_b1mm f_b1 f_iota f_comb f_s up_mm hid_rdy down_mm acc_rdy st4_rdy mv4_rdy ve4_rdy rs4_rdy yn_rdy y1_rdy y2_rdy y3_rdy out_rdy out_st""".split()
        S.update({n: sem(n) for n in names})
        block = ctx.enter_context(nc.Block())
        up_banks, down_banks = banks[0:4], banks[4:6]

        @block.sync
        def _(sp):
            sp.dma_start(b2b[:], inp["b2"].rearrange("e d -> (e d)").partition_broadcast(P).rearrange("p (e d) -> p e d", e=NE)).then_inc(S["f_ld"], 16)
            sp.dma_start(olw[:], inp["out_ln_w"].partition_broadcast(P)).then_inc(S["f_ld"], 16)
            sp.dma_start(olb[:], inp["out_ln_b"].partition_broadcast(P)).then_inc(S["f_ld"], 16)
            sp.dma_start(gbb[:], mod_dram[:, GB * D:(GB + 1) * D].partition_broadcast(P)).then_inc(S["f_ld"], 16)
            ov = out.rearrange("b (c p) d -> p (b c) d", p=P)
            with sp.Fori(0, NG) as g:
                sp.wait_ge(S["out_rdy"], g + 1)
                sp.dma_start(ov[:, bass.ds(g * GROUP, GROUP), :], x_sb[:, bass.ds(g * GROUP, GROUP), :]).then_inc(S["out_st"], 16)
            sp.wait_ge(S["out_st"], 16 * NG)

        @block.gpsimd
        def _(pool):
            nc.gpsimd.iota(iota_e[:], pattern=[[1, NE]], base=0, channel_multiplier=0, allow_small_or_imprecise_dtypes=True)
            nc.gpsimd.memset(halves4[:], -0.5).then_inc(S["f_iota"], 1)
            pool.wait_ge(S["f_iota"], 1)
            with pool.Fori(0, NG) as g:
                pool.wait_ge(S["ve4_rdy"], g + 1)
                nc.gpsimd.tensor_tensor(rs4[:], ve4[:], halves4[:], ALU.pow).then_inc(S["rs4_rdy"], 1)

        @block.scalar
        def _(act):
            act.wait_ge(S["f_comb"], 1)
            nc.scalar.activation(pw[:, :, 1], pw[:, :, 0], ACT.Exp).then_inc(S["f_s"], 1)
            act.wait_ge(S["f_b1"], 1)
            with act.Fori(0, NG) as g:
                for e in range(NE):
                    for j in range(NC):
                        act.wait_ge(S["up_mm"], g * (NE * NC) + e * NC + j + 1)
                        if j == 0 and e >= 2:
                            act.wait_ge(S["down_mm"], g * NE + e - 1)
                        ins = nc.scalar.activation(hid[:, e % 2, j, :], up_banks[j][:], ACT.Gelu, bias=b1T[:, e * NC + j:e * NC + j + 1])
                        ins.then_inc(S["hid_rdy"], 1)

        @block.vector
        def _(dve):
            n = [0]

            def link(ins):
                n[0] += 1
                ins.then_inc(S["f_ops"], 1)
                dve.wait_ge(S["f_ops"], n[0])

            dve.wait_ge(S["ld_ffn"], 32)
            dve.wait_ge(S["f_b1mm"], 1)
            nc.vector.tensor_tensor(b1T[:], banks[6][:, 0:NE * NC], vecT[:, R_B1:R_B1 + NE * NC], ALU.add).then_inc(S["f_b1"], 1)
            for e in range(NE):
                last = nc.vector.tensor_scalar(w1s[:, e, :], w1s[:, e, :], vecT[:, R_LNW + e:R_LNW + e + 1], None, ALU.mult)
            last.then_inc(S["f_w1"], 1)
            link(nc.vector.tensor_tensor(rbias[:], banks[7][:, 0:NE], rbias[:], ALU.add))
            link(nc.vector.tensor_tensor(rlog[:], rlog[:], rbias[:].unsqueeze(1).broadcast_to([P, NT, NE]), ALU.add))
            for j in range(NT):
                nc.vector.max(top[:, j, :], rlog[:, j, :])
            link(nc.vector.memset(pw[:], 1.0))
            nc.vector.memset(ve4[:], 1.0).then_inc(S["acc_rdy"], 2 * NE)
            for j in range(NT):
                last = nc.vector.max_index(topi[:, j, :], top[:, j, :], rlog[:, j, :])
            link(last)
            nc.vector.tensor_copy(topf[:], topi[:, :, 0:2])
            nc.vector.tensor_tensor(pw[:, :, 0], top[:, :, 1], top[:, :, 0], ALU.subtract).then_inc(S["f_comb"], 1)
            dve.wait_ge(S["f_s"], 1)
            link(nc.vector.tensor_scalar(pw[:, :, 2], pw[:, :, 1], 1.0, None, ALU.add))
            link(nc.vector.reciprocal(pw[:, :, 2], pw[:, :, 2]))
            link(nc.vector.tensor_tensor(pw[:, :, 3], pw[:, :, 1], pw[:, :, 2], ALU.mult))
            dve.wait_ge(S["f_iota"], 1)
            for dst, k in ((comb, 0), (comb2, 1)):
                link(nc.vector.tensor_tensor(dst[:], iota_e[:].unsqueeze(1).broadcast_to([P, NT, NE]),
                                             topf[:, :, k:k + 1].broadcast_to([P, NT, NE]), ALU.is_equal))
                link(nc.vector.tensor_tensor(dst[:], dst[:], pw[:, :, 2 + k:3 + k].broadcast_to([P, NT, NE]), ALU.mult))
            link(nc.vector.tensor_tensor(comb[:], comb[:], comb2[:], ALU.add))
            dve.wait_ge(S["f_ld"], 64)
            with dve.Fori(0, NG) as g:
                for e in range(NE):
                    dve.wait_ge(S["down_mm"], g * NE + e + 1)
                    for t in range(GROUP):
                        w = comb[:, bass.ds(g * GROUP + t, 1), e:e + 1].squeeze(1)
                        o = down_banks[e % 2][:, t * D:(t + 1) * D]
                        if e == 0:
                            last = nc.vector.tensor_scalar(acc[:, 0, t, :], o, w, None, ALU.mult)
                        else:
                            last = nc.vector.scalar_tensor_tensor(out=acc[:, e % 2, t, :], in0=o, scalar=w, in1=acc[:, 1 - e % 2, t, :], op0=ALU.mult, op1=ALU.add)
                    last.then_inc(S["acc_rdy"], 1)
                    dve.wait_ge(S["acc_rdy"], (g + 1) * 2 * NE + 2 * e + 1)
                    for t in range(GROUP):
                        w = comb[:, bass.ds(g * GROUP + t, 1), e:e + 1].squeeze(1)
                        last = nc.vector.scalar_tensor_tensor(out=acc[:, e % 2, t, :], in0=b2b[:, e, :], scalar=w, in1=acc[:, e % 2, t, :], op0=ALU.mult, op1=ALU.add)
                    last.then_inc(S["acc_rdy"], 1)
                    dve.wait_ge(S["acc_rdy"], (g + 1) * 2 * NE + 2 * e + 2)
                src = acc[:, 1, :, :]
                for t in range(GROUP):
                    last = nc.vector.bn_stats(st4[:, t, :], src[:, t, :])
                last.then_inc(S["st4_rdy"], 1)
                dve.wait_ge(S["st4_rdy"], g + 1)
                nc.vector.tensor_copy(yo[:], src)
                for t in range(GROUP):
                    last = nc.vector.bn_aggr(mv4[:, t, :], st4[:, t, :])
                last.then_inc(S["mv4_rdy"], 1)
                dve.wait_ge(S["mv4_rdy"], g + 1)
                nc.vector.tensor_scalar(ve4[:], mv4[:, :, 1], EPS, None, ALU.add).then_inc(S["ve4_rdy"], 1)
                dve.wait_ge(S["rs4_rdy"], g + 1)
                for t in range(GROUP):
                    last = nc.vector.tensor_scalar(yn[:, t, :], src[:, t, :], mv4[:, t, 0:1], rs4[:, t:t + 1], ALU.subtract, ALU.mult)
                last.then_inc(S["yn_rdy"], 1)
                dve.wait_ge(S["yn_rdy"], g + 1)
                nc.vector.tensor_tensor(yo[:], yn[:], olw[:].unsqueeze(1).broadcast_to([P, GROUP, D]), ALU.mult).then_inc(S["y1_rdy"], 1)
                dve.wait_ge(S["y1_rdy"], g + 1)
                nc.vector.tensor_tensor(yp[:], yo[:], olb[:].unsqueeze(1).broadcast_to([P, GROUP, D]), ALU.add).then_inc(S["y2_rdy"], 1)
                dve.wait_ge(S["y2_rdy"], g + 1)
                gv = gbb[:, bass.ds(g * (GROUP // 2), GROUP // 2), :].unsqueeze(2).broadcast_to([P, GROUP // 2, 2, D])
                nc.vector.tensor_tensor(yo[:].rearrange("p (b c) d -> p b c d", c=2), yp[:].rearrange("p (b c) d -> p b c d", c=2), gv, ALU.mult).then_inc(S["y3_rdy"], 1)
                dve.wait_ge(S["y3_rdy"], g + 1)
                xg = x_sb[:, bass.ds(g * GROUP, GROUP), :]
                nc.vector.tensor_tensor(xg, xg, yo[:], ALU.add).then_inc(S["out_rdy"], 1)

        @block.tensor
        def _(pe):
            mm = nc.tensor.matmul
            pe.wait_ge(S["ld_ffn"], 32)
            mm(banks[7][:, 0:NE], vecT[:, R_RB:R_RB + 1].broadcast_to([P, P]), routw[:], start=True, stop=True)
            for e in range(NE):
                for j in range(NC):
                    last = mm(banks[6][:, e * NC + j:e * NC + j + 1], w1s[:, e, j * P:(j + 1) * P], vecT[:, R_LNB + e:R_LNB + e + 1], start=True, stop=True)
            last.then_inc(S["f_b1mm"], 1)
            pe.wait_ge(S["f_w1"], 1)
            with pe.Fori(0, NG) as g:
                def up(e):
                    for j in range(NC):
                        if e >= 1:
                            pe.wait_ge(S["hid_rdy"], g * (NE * NC) + (e - 1) * NC + j + 1)
                        mm(up_banks[j][:], w1s[:, e, j * P:(j + 1) * P], xT_all[:, bass.ds(g * 2, 2), :], start=True, stop=True).then_inc(S["up_mm"], 1)

                def down(e):
                    for t in range(GROUP):
                        for j in range(NC):
                            if t == 0:
                                pe.wait_ge(S["hid_rdy"], g * (NE * NC) + e * NC + j + 1)
                            if t == 0 and j == 0:
                                pe.wait_ge(S["acc_rdy"], (g + 1) * 2 * NE + 2 * (e - 2) + 1)
                            last = mm(down_banks[e % 2][:, t * D:(t + 1) * D], hid[:, e % 2, j, t * P:(t + 1) * P], w2s[:, e, j, :], start=j == 0, stop=j == NC - 1)
                    last.then_inc(S["down_mm"], 1)
                up(0)
                for e in range(NE):
                    if e + 1 < NE:
                        up(e + 1)
                    down(e)


_INS = dict(x="L0_attn_hidden_states", Wq="L0_attn_Wq", Wk="L0_attn_Wk", Wv="L0_attn_Wv", Wg="L0_attn_Wg", Wo="L0_attn_Wo",
            sk_w1="L0_attn_sk_w1", sk_w2="L0_attn_sk_w2", sk_b2="L0_attn_sk_b2", sv_w1="L0_attn_sv_w1", sv_w2="L0_attn_sv_w2",
            sv_b2="L0_attn_sv_b2", gnorm_w="L0_attn_gnorm_w", router_ln_w="L0_ffn_router_ln_w", router_ln_b="L0_ffn_router_ln_b",
            router_w="L0_ffn_router_w", router_b="L0_ffn_router_b", exp_ln_w="L0_ffn_exp_ln_w", exp_ln_b="L0_ffn_exp_ln_b",
            w1="L0_ffn_w1", b1="L0_ffn_b1", w2="L0_ffn_w2", b2="L0_ffn_b2", out_ln_w="L0_ffn_out_ln_w", out_ln_b="L0_ffn_out_ln_b",
            c="L0_c", wmod="L0_wmod")


def rope_tables():
    half = HD // 2
    inv_freq = (1.0 / 10000.0 ** (np.arange(half, dtype=np.float32) / half)).astype(np.float32)
    ang = np.arange(T, dtype=np.float32)[None, :] * inv_freq[:, None]
    cos, sin = np.cos(ang), np.sin(ang)
    return (np.ascontiguousarray(np.tile(np.concatenate([cos, cos]), (H, 1))),
            np.ascontiguousarray(np.tile(np.concatenate([-sin, sin]), (H, 1))))


def kernel(**inputs):
    import concourse.bacc as bacc
    from concourse.bass_utils import run_bass_kernel_spmd

    nc = bacc.Bacc("TRN2", target_bir_lowering=False, num_devices=1)
    arrays = {n: np.ascontiguousarray(inputs[full]) for n, full in _INS.items()}
    arrays["cosT"], arrays["sinT"] = rope_tables()
    aps = {n: nc.dram_tensor(f"in_{n}", a.shape, F32, kind="ExternalInput").ap() for n, a in arrays.items()}
    out = nc.dram_tensor("out", [NB, T, D], F32, kind="ExternalOutput").ap()
    build(nc, aps, out)
    r = run_bass_kernel_spmd(nc, [{f"in_{n}": a for n, a in arrays.items()}], core_ids=[0])
    return r.results[0]["out"]
```

```python
import numpy as np
from contextlib import ExitStack

import concourse.bass as bass
from concourse import mybir

F32 = mybir.dt.float32
BF16 = mybir.dt.bfloat16
U32 = mybir.dt.uint32
ACT = mybir.ActivationFunctionType
ALU = mybir.AluOpType
AX = mybir.AxisListType

P = 128
NB = 16
T = 256
D = 128
H = 4
HD = D // H
M = 64
LOW = 16
NE = 8
FF = 512
NC = FF // P
NT = NB * T // P
EPS = 1e-5
CLAMP = 32.0
UNROLL = 4
PEEL = 4
LAST_LAG = 4


def build(nc, inp, out, debug=None):
    with ExitStack() as ctx:
        def sb(name, shape, dt=F32):
            return ctx.enter_context(nc.sbuf_tensor(name, shape, dt))

        def sem(name):
            return ctx.enter_context(nc.semaphore(name))

        banks = [ctx.enter_context(nc.psum_tensor(f"bank{i}", [P, 512], F32)) for i in range(8)]
        b3, b4, b5, b6, b7 = banks[3:]

        x_sb = sb("x_sb", [P, NT, D])
        Wq, Wqr, Wk, Wkr, Wv, Wg, Wo, Wog = [sb(n, [P, D]) for n in ("Wq", "Wqr", "Wk", "Wkr", "Wv", "Wg", "Wo", "Wog")]
        low1 = sb("low1", [P, 2 * LOW])
        low2 = sb("low2", [P, 4, P])
        cosT, sinT = sb("cosT", [P, T]), sb("sinT", [P, T])
        ident = sb("ident", [P, P])
        headmean = sb("headmean", [P, P])
        ones = sb("ones", [P, T])
        halves = sb("halves", [P, 2])
        vec_rows = sb("vec_rows", [P, D])
        vecT = sb("vecT", [P, 96])
        cT = sb("cT", [P, 4, NB])
        wmod = sb("wmod", [P, 6 * D])
        saT, caT = sb("saT", [P, NB]), sb("caT", [P, NB])
        mod_rows = sb("mod_rows", [NB, 4 * D])
        mod_tmp = sb("mod_tmp", [NB, 2, 2, D])
        modb = sb("modb", [P, 4, 3 * D])
        routw = sb("routw", [P, NE])
        routwg = sb("routwg", [P, NE])
        mod_dram = nc.dram_tensor("mod_dram", [NB, 4 * D], F32, kind="Internal").ap()
        R_LNW, R_LNB, R_RW, R_RB, R_GN, R_C, R_B1 = 0, 8, 16, 17, 18, 32, 48
        NROW = R_B1 + NE * NC
        GA, SB_, CB, GB = 0, 1, 2, 3

        w1s = sb("w1s", [P, NE, FF])
        w2s = sb("w2s", [P, NE, NC, D])
        rbias = sb("rbias", [P, NE])
        rlog = sb("rlog", [P, NT, NE])
        xhat_dram = nc.dram_tensor("xhat_dram", [P * NT, D], F32, kind="Internal").ap()
        outer, ctx = ctx, ExitStack()
        mv1 = sb("mv1", [P, 2, 2]); st1 = sb("st1", [P, 2, 6]); ve1 = sb("ve1", [P, 2]); rs1 = sb("rs1", [P, 2])
        mv2 = sb("mv2", [P, 2, 2]); st2 = sb("st2", [P, 2, 6]); ve2 = sb("ve2", [P, 2]); rs2 = sb("rs2", [P, 2])
        mv3 = sb("mv3", [P, 2, 2]); st3 = sb("st3", [P, 2, 6]); ve3 = sb("ve3", [P, 2]); rs3 = sb("rs3", [P, 2])
        xn = sb("xn", [P, 2, 2, D])
        hT = sb("hT", [P, 2, T])
        rot = sb("rot", [P, 2, 4, T])
        Qx = sb("Qx", [P, 2, H, T])
        qT = sb("qT", [P, T])
        headmask = sb("headmask", [P, H, 2])
        kT = sb("kT", [P, 2, T])
        lT = sb("lT", [P, 2, T])
        v_tok = sb("v_tok", [P, 4, 2, D])
        g_sb, eg = sb("g_sb", [P, 2, T]), sb("eg", [P, 2, T])
        gate = sb("gate", [P, 4, T])
        wkT = sb("wkT", [P, 2, 2, T])
        wvT = sb("wvT", [P, 4, 2, T])
        z = sb("z", [P, 2, 4, T])
        r0 = sb("r0", [P, 4, T])
        rz = sb("rz", [P, 2, 4, T])
        wk_tok = sb("wk_tok", [P, 2, 2, H * M])
        S_sb = sb("S_sb", [P, 3, 512])
        A_sb = sb("A_sb", [P, 3, 512])
        eps_col = sb("eps_col", [P, 1])[:]
        lg2 = sb("lg2", [P, 2, 2, T])
        mx = sb("mx", [P, 2, H]); rsum = sb("rsum", [P, 2, H])
        lgs = sb("lgs", [P, 2, 2, H * M])
        Px = sb("Px", [P, 2, H, T])
        sq = sb("sq", [P, T]); rs = sb("rs", [P, T]); onT1 = sb("onT1", [P, T]); onT = sb("onT", [P, 2, T])
        Wob = sb("Wob", [P, 2, D])
        xn2 = sb("xn2", [P, 2, D]); h2 = sb("h2", [P, 2, D]); h2a = sb("h2a", [P, 2, D])
        xhat = sb("xhat", [P, 2, 2, D])
        xhatT = sb("xhatT", [P, 2, T])

        names = """ld_x ld_w ld_rows ld_ffn set_pool set_dve set_zero low2_ld vec_tp vec_rdy silu_e silu_rdy mod_mm mod_rdy mod_st q_rdy modb_ld0 modb_ld1 modb_ld2 modb_ld3
            wkT_tp out_mm pT_tp s_mm xT_tp xhatT_tp qk_mm v_mm rlog_mm lg_mm a_mm glt_mm lgtok_tp oT_mm skv_mm ms_mm
            lnz_rdy r0_rdy wk_tok_rdy s_copied hT_rdy xhatT_rdy v_rdy rlog_rdy a_copied lT_rdy eg_rdy sq_rdy wexp_rdy pexp_rdy
            rsln_rdy rs_rdy sigln_rdy sig_rdy
            st1_rdy mv1_rdy ve1_rdy xn_rdy px_rdy nu_rdy rz_rdy x1_rdy st2_rdy mv2_rdy ve2_rdy xn2_rdy h2a_rdy h2_rdy st3_rdy mv3_rdy ve3_rdy
            xhat_rdy ropemul_rdy lg2_rdy mx_rdy lgsub_rdy t1_rdy on_rdy sum_rdy rsum_rdy clip_rdy z_rdy
            rstd1_rdy gate_rdy wob_rdy rstd2_rdy s_masked rope_rdy rstd3_rdy a_masked egc_rdy pnorm_rdy xhat_st0 xhat_st1 dve_chain""".split()
        S = {n: sem(n) for n in names}

        def need(eng, name, batch):
            if isinstance(batch, int) and not 0 <= batch < NB:
                return
            eng.wait_ge(S[name], batch + 1)

        def need_apart(eng, name, batch):
            eng.wait_ge(S["vec_tp"], 1)
            need(eng, name, batch)

        def live(batch):
            return not isinstance(batch, int) or 0 <= batch < NB

        def pipeline(eng, iteration):
            for i in range(PEEL):
                iteration(i, i % UNROLL)
            with eng.Fori(PEEL // UNROLL, NB // UNROLL) as n:
                for k in range(UNROLL):
                    iteration(n * UNROLL + k, k)
            for i in range(NB, NB + LAST_LAG + 1):
                iteration(i, i % UNROLL)

        def slot_loads(batch, slot):
            if isinstance(batch, int):
                return 16 * (batch // 4 + 1)
            return (batch - slot + 4) * 4

        block = ctx.enter_context(nc.Block())

        @block.sync
        def _(sp):
            xv = inp["x"].rearrange("b (c p) d -> p (b c) d", p=P)
            for n, sl in ((0, slice(0, 4)), (1, slice(4, NT))):
                sp.dma_start(x_sb[:, sl, :], xv[:, sl, :]).then_inc(S["ld_x"], 16)
            for dst, name in ((Wq, "Wq"), (Wk, "Wk")):
                sp.dma_start(dst[:], inp[name]).then_inc(S["ld_w"], 16)
            for dst, name in ((Wqr, "Wq"), (Wkr, "Wk")):
                dv = dst[:].rearrange("p (h two c) -> p h two c", h=H, two=2)
                sv = inp[name].rearrange("p (h two c) -> p h two c", h=H, two=2)
                for half in range(2):
                    sp.dma_start(dv[:, :, half, :], sv[:, :, 1 - half, :]).then_inc(S["ld_w"], 16)
            for dst, name in ((Wv, "Wv"), (Wg, "Wg"), (Wo, "Wo"), (cosT, "cosT"), (sinT, "sinT"), (routw, "router_w")):
                sp.dma_start(dst[:], inp[name]).then_inc(S["ld_w"], 16)
            sp.dma_start(low1[:, 0:LOW], inp["sk_w1"]).then_inc(S["ld_w"], 16)
            sp.dma_start(low1[:, LOW:2 * LOW], inp["sv_w1"]).then_inc(S["ld_w"], 16)
            sp.dma_start(rbias[:], inp["router_b"].partition_broadcast(P)).then_inc(S["ld_w"], 16)
            sp.dma_start(w1s[:], inp["w1"].rearrange("e d i -> d e i")).then_inc(S["ld_ffn"], 16)
            sp.dma_start(w2s[:], inp["w2"].rearrange("e (c p) d -> p e c d", p=P)).then_inc(S["ld_ffn"], 16)
            sp.wait_ge(S["mod_rdy"], 1)
            sp.dma_start(mod_dram, mod_rows[:]).then_inc(S["mod_st"], 16)
            sp.wait_ge(S["mod_st"], 16)
            xrows = xhat_dram.rearrange("(p b c) d -> p b (c d)", p=P, c=2)

            def iteration(i, k):
                if live(i):
                    need(sp, "h2_rdy", i - 4)
                    if isinstance(i, int):
                        src = mod_dram[i, 0:3 * D]
                    else:
                        src = mod_dram[bass.ds(i, 1), 0:3 * D].squeeze(0)
                    sp.dma_start(modb[:, k, :], src.partition_broadcast(P)).then_inc(S[f"modb_ld{k}"], 16)
                if live(i - 4):
                    need(sp, "xhat_rdy", i - 4)
                    sp.dma_start(xrows[:, bass.ds(i - 4, 1), :].squeeze(1), xhat[:, k % 2, :, :].rearrange("p c d -> p (c d)")).then_inc(S[f"xhat_st{k % 2}"], 16)
            pipeline(sp, iteration)
        N_W = 15

        @block.gpsimd
        def _(pool):
            def gate_step(a, k):
                need(pool, "sig_rdy", a)
                nc.gpsimd.tensor_tensor(gate[:, k, :], g_sb[:, k % 2, :], eg[:, k % 2, :], ALU.mult).then_inc(S["gate_rdy"], 1)

            nc.gpsimd.memset(ident[:], 1.0).then_inc(S["set_pool"], 1)
            nc.gpsimd.memset(headmean[:], 1.0 / HD).then_inc(S["set_pool"], 1)
            nc.gpsimd.memset(halves[:], -0.5).then_inc(S["set_pool"], 1)
            nc.gpsimd.memset(headmask[:], 1.0).then_inc(S["set_pool"], 1)
            pool.wait_ge(S["set_pool"], 4)
            nc.gpsimd.affine_select(out=ident[:], in_=ident[:], compare_op=ALU.is_equal, fill=0.0, base=0,
                                    pattern=[[-1, P]], channel_multiplier=1).then_inc(S["set_pool"], 1)
            for n, hm in enumerate((headmean[:].rearrange("p (h c) -> p h c", h=H), headmask[:])):
                w = hm.shape[2]
                nc.gpsimd.affine_select(out=hm, in_=hm, compare_op=ALU.is_ge, fill=0.0, base=0,
                                        pattern=[[-HD, H], [0, w]], channel_multiplier=1).then_inc(S["set_pool"], 1)
                pool.wait_ge(S["set_pool"], 6 + 2 * n)
                nc.gpsimd.affine_select(out=hm, in_=hm, compare_op=ALU.is_ge, fill=0.0, base=HD - 1,
                                        pattern=[[HD, H], [0, w]], channel_multiplier=-1).then_inc(S["set_pool"], 1)

            def iteration(i, k):
                a, b, c, e, d = i, i - 1, i - 2, i - 3, i - 4
                kb, kc, ke, kd = (k - 1) % 4, (k - 2) % 4, (k - 3) % 4, (k - 4) % 4
                if live(a):
                    need(pool, "ve1_rdy", a)
                    nc.gpsimd.tensor_tensor(rs1[:], ve1[:], halves[:], ALU.pow).then_inc(S["rstd1_rdy"], 1)
                if live(b):
                    gate_step(b, kb)
                if live(c):
                    pool.wait_ge(S[f"modb_ld{kc}"], slot_loads(c, kc))
                    if isinstance(c, int) and c == 0:
                        pool.wait_ge(S["vec_rdy"], 2)
                    need(pool, "out_mm", c - 2)
                    nc.gpsimd.tensor_tensor(Wob[:, kc % 2, :], Wog[:], modb[:, kc, GA * D:(GA + 1) * D],
                                            ALU.mult).then_inc(S["wob_rdy"], 1)
                if live(e):
                    need(pool, "ve2_rdy", e)
                    nc.gpsimd.tensor_tensor(rs2[:], ve2[:], halves[:], ALU.pow).then_inc(S["rstd2_rdy"], 1)
                if live(b):
                    need_apart(pool, "s_copied", b)
                    causal(S_sb, "s_masked")
                if live(a):
                    need(pool, "ropemul_rdy", a)
                    need(pool, "s_mm", a - 2)
                    nc.gpsimd.tensor_tensor(qT[:], rot[:, k % 2, 0, :], rot[:, k % 2, 1, :], ALU.add).then_inc(S["q_rdy"], 1)
                    need_apart(pool, "q_rdy", a)
                    for h in range(H):
                        nc.gpsimd.tensor_scalar(Qx[:, k % 2, h, :], qT[:], headmask[:, h, 0:1], 1.0, ALU.mult, ALU.mult)
                    nc.gpsimd.tensor_tensor(kT[:, k % 2, :], rot[:, k % 2, 2, :], rot[:, k % 2, 3, :],
                                            ALU.add).then_inc(S["rope_rdy"], 1)
                if live(e):
                    need(pool, "ve3_rdy", e)
                    nc.gpsimd.tensor_tensor(rs3[:], ve3[:], halves[:], ALU.pow).then_inc(S["rstd3_rdy"], 1)
                if live(c):
                    need_apart(pool, "a_copied", c)
                    causal(A_sb, "a_masked")
                if live(a):
                    need_apart(pool, "eg_rdy", a)
                    nc.gpsimd.tensor_scalar(eg[:, k % 2, :], eg[:, k % 2, :], 1e18, 0.0, ALU.min, ALU.max).then_inc(S["egc_rdy"], 1)
                if live(b):
                    need(pool, "rsum_rdy", b)
                    for tile in range(2):
                        v = lgs[:, kb % 2, tile, :].rearrange("p (h m) -> p h m", h=H)
                        last = nc.gpsimd.tensor_tensor(v, v, rsum[:, tile, :].unsqueeze(2).broadcast_to([P, H, M]), ALU.mult)
                    last.then_inc(S["pnorm_rdy"], 1)

            def causal(buf, name):
                d0 = buf[:, 0:2, :].rearrange("p two (h t) -> p (two h) t", h=2)[:, :, 0:P]
                d1 = buf[:, 2, :].rearrange("p (h t) -> p h t", h=H)
                for d in (d0, d1):
                    last = nc.gpsimd.affine_select(out=d, in_=d, compare_op=ALU.is_ge, fill=0.0, base=0,
                                                   pattern=[[0, H], [1, P]], channel_multiplier=-1)
                last.then_inc(S[name], 1)

            pipeline(pool, iteration)

        @block.scalar
        def _(act):
            nc.scalar.preload_act_table_set("natural_log_exp_and_others")
            act.wait_ge(S["set_zero"], 1)
            rows = ((R_LNW, NE, "exp_ln_w"), (R_LNB, NE, "exp_ln_b"), (R_B1, NE * NC, "b1"), (R_RW, 1, "router_ln_w"), (R_RB, 1, "router_ln_b"), (R_C, NB, "c"))
            for r, n, name in rows:
                src = inp[name] if n > 1 else inp[name].unsqueeze(0)
                if name == "b1":
                    src = src.rearrange("e (c p) -> (e c) p", p=P)
                act.dma_start(vec_rows[r:r + n, :], src).then_inc(S["ld_rows"], 16)
            for h in range(H):
                act.dma_start(vec_rows[R_GN:R_GN + 1, h * HD:(h + 1) * HD], inp["gnorm_w"].unsqueeze(0)).then_inc(S["ld_rows"], 16)
            act.dma_start(wmod[:], inp["wmod"]).then_inc(S["ld_rows"], 16)
            for n, w2, bias in ((0, "sk_w2", "sk_b2"), (1, "sv_w2", "sv_b2")):
                act.dma_start(low2[n * LOW:(n + 1) * LOW, 2 * n:2 * n + 2, :],
                              inp[w2].rearrange("r (a c) -> r a c", a=2)).then_inc(S["low2_ld"], 16)
                act.dma_start(low2[2 * LOW:2 * LOW + 1, 2 * n:2 * n + 2, :],
                              inp[bias].unsqueeze(0).rearrange("o (a c) -> o a c", a=2)).then_inc(S["low2_ld"], 16)
            act.wait_ge(S["vec_rdy"], 1)
            nc.scalar.activation(cT[:, 1, :], cT[:, 0, :], ACT.Exp, scale=-1.0).then_inc(S["silu_e"], 1)

            def iteration(i, k):
                a, b, c, e, d = i, i - 1, i - 2, i - 3, i - 4
                kb, kc, kd = (k - 1) % 4, (k - 2) % 4, (k - 4) % 4
                if live(b):
                    need(act, "z_rdy", b)
                    need(act, "rz_rdy", b - 1)
                    nc.scalar.activation(r0[:], z[:, kb % 2, :, :], ACT.Ln).then_inc(S["lnz_rdy"], 1)
                    need(act, "wkT_tp", b)
                    need(act, "lg_mm", b - 2)
                    nc.scalar.copy(wk_tok[:, kb % 2, :, :], b3[:].rearrange("p (c n) -> p c n", c=2)).then_inc(S["wk_tok_rdy"], 1)
                    need(act, "lnz_rdy", b)
                    nc.scalar.activation(r0[:], r0[:], ACT.Exp, scale=-1.0).then_inc(S["r0_rdy"], 1)
                    need(act, "s_mm", b)
                    for n in range(3):
                        last = nc.scalar.copy(S_sb[:, n, :], banks[n][:])
                    last.then_inc(S["s_copied"], 1)
                if live(a):
                    if isinstance(a, int) and a == 0:
                        act.wait_ge(S["mod_rdy"], 1)
                    need(act, "xT_tp", a)
                    need(act, "glt_mm", a - 2)
                    nc.scalar.activation(hT[:, k % 2, :], b3[:, 0:T], ACT.Identity, bias=saT[:, bass.ds(a, 1)],
                                         scale=caT[:, bass.ds(a, 1)]).then_inc(S["hT_rdy"], 1)
                if live(d):
                    need(act, "xhatT_tp", d)
                    nc.scalar.copy(xhatT[:, kd % 2, :], b3[:, T:2 * T]).then_inc(S["xhatT_rdy"], 1)
                if live(a):
                    need(act, "v_mm", a)
                    need(act, "oT_mm", a - 4)
                    nc.scalar.copy(v_tok[:, k, :, :], b3[:, 0:T].rearrange("p (c n) -> p c n", c=2)).then_inc(S["v_rdy"], 1)
                if live(d):
                    need(act, "rlog_mm", d)
                    nc.scalar.copy(rlog[:, bass.ds(d * 2, 2), :], b3[:, T:T + 2 * NE].rearrange("p (c n) -> p c n", c=2)).then_inc(S["rlog_rdy"], 1)
                if live(c):
                    need(act, "a_mm", c)
                    need(act, "oT_mm", c - 2)
                    for n in range(3):
                        last = nc.scalar.copy(A_sb[:, n, :], banks[n][:])
                    last.then_inc(S["a_copied"], 1)
                if live(a):
                    need(act, "glt_mm", a)
                    need(act, "skv_mm", a - 2)
                    nc.scalar.copy(lT[0:2 * LOW, k % 2, :], b3[0:2 * LOW, T:2 * T]).then_inc(S["lT_rdy"], 1)
                    need(act, "gate_rdy", a - 2)
                    nc.scalar.copy(g_sb[:, k % 2, :], b3[:, 0:T])
                    nc.scalar.activation(eg[:, k % 2, :], b3[:, 0:T], ACT.Exp, scale=-1.0).then_inc(S["eg_rdy"], 1)
                if live(c):
                    need(act, "oT_mm", c)
                    need(act, "ms_mm", c - 1)
                    nc.scalar.activation(sq[:], b7[:, 0:T], ACT.Square).then_inc(S["sq_rdy"], 1)
                if live(a):
                    need(act, "skv_mm", a)
                    need(act, "a_mm", a - 4)
                    nc.scalar.activation(wkT[:, k % 2, :, :], b4[:].rearrange("p (c n) -> p c n", c=2), ACT.Exp)
                    nc.scalar.activation(wvT[:, k, :, :], b5[:].rearrange("p (c n) -> p c n", c=2), ACT.Exp).then_inc(S["wexp_rdy"], 1)
                if live(b):
                    need(act, "lgsub_rdy", b)
                    nc.scalar.activation(lgs[:, kb % 2, :, :], lgs[:, kb % 2, :, :], ACT.Exp).then_inc(S["pexp_rdy"], 1)
                if live(c):
                    need(act, "ms_mm", c)
                    need(act, "t1_rdy", c - 1)
                    nc.scalar.activation(rs[:], b6[:, 0:T], ACT.Ln, bias=eps_col).then_inc(S["rsln_rdy"], 1)
                    need(act, "rsln_rdy", c)
                    nc.scalar.activation(rs[:], rs[:], ACT.Exp, scale=-0.5).then_inc(S["rs_rdy"], 1)
                if live(a):
                    need(act, "egc_rdy", a)
                    nc.scalar.activation(eg[:, k % 2, :], eg[:, k % 2, :], ACT.Ln, bias=1.0).then_inc(S["sigln_rdy"], 1)
                    need(act, "sigln_rdy", a)
                    nc.scalar.activation(eg[:, k % 2, :], eg[:, k % 2, :], ACT.Exp, scale=-1.0).then_inc(S["sig_rdy"], 1)

            pipeline(act, iteration)

        @block.vector
        def _(dve):
            chain = [0]

            def link(ins):
                chain[0] += 1
                ins.then_inc(S["dve_chain"], 1)
                dve.wait_ge(S["dve_chain"], chain[0])

            link(nc.vector.memset(vec_rows[:], 0.0))
            nc.vector.memset(low2[:], 0.0).then_inc(S["set_zero"], 1)
            nc.vector.memset(ones[:], 1.0)
            nc.vector.memset(eps_col, EPS)
            nc.vector.memset(Qx[:], 0.0)
            nc.vector.memset(Px[:], 0.0)
            link(nc.vector.memset(lT[:], 0.0))
            nc.vector.memset(lT[2 * LOW:2 * LOW + 1, :, :], 1.0).then_inc(S["set_dve"], 1)
            dve.wait_ge(S["vec_tp"], 1)
            link(nc.vector.tensor_copy(vecT[:, 0:NROW], b3[:, 0:NROW]))
            nc.vector.tensor_copy(cT[:, 0, :], vecT[:, R_C:R_C + NB]).then_inc(S["vec_rdy"], 1)
            dve.wait_ge(S["ld_w"], 16 * N_W)
            nc.vector.tensor_scalar(Wog[:], Wo[:], vecT[:, R_GN:R_GN + 1], None, ALU.mult)
            nc.vector.tensor_scalar(routwg[:], routw[:], vecT[:, R_RW:R_RW + 1], None, ALU.mult).then_inc(S["vec_rdy"], 1)
            dve.wait_ge(S["silu_e"], 1)
            link(nc.vector.tensor_scalar(cT[:, 1, :], cT[:, 1, :], 1.0, None, ALU.add))
            link(nc.vector.reciprocal(cT[:, 2, :], cT[:, 1, :]))
            nc.vector.tensor_tensor(cT[:, 3, :], cT[:, 0, :], cT[:, 2, :], ALU.mult).then_inc(S["silu_rdy"], 1)
            dve.wait_ge(S["mod_mm"], 1)
            nc.vector.tensor_copy(saT[:], b3[:, 0:NB])
            nc.vector.tensor_scalar(caT[:], b3[:, NB:2 * NB], 1.0, None, ALU.add)
            for n, m in ((0, GA), (1, GB)):
                g = b4[0:NB, m * D:(m + 1) * D]
                link(nc.vector.tensor_copy(mod_tmp[:, n, 0, :], g))
                link(nc.vector.scalar_tensor_tensor(out=mod_tmp[:, n, 1, :], in0=mod_tmp[:, n, 0, :], scalar=-1.0,
                                                    in1=mod_tmp[:, n, 0, :], op0=ALU.mult, op1=ALU.max))
                nc.vector.tensor_scalar(mod_tmp[:, n, 1, :], mod_tmp[:, n, 1, :], 0.25, None, ALU.max)
                link(nc.vector.tensor_scalar(mod_tmp[:, n, 0, :], mod_tmp[:, n, 0, :], 0.0, 2.0, ALU.is_ge, ALU.mult))
                nc.vector.scalar_tensor_tensor(out=mod_rows[:, m * D:(m + 1) * D], in0=mod_tmp[:, n, 0, :], scalar=-1.0,
                                               in1=mod_tmp[:, n, 1, :], op0=ALU.add, op1=ALU.mult)
            nc.vector.tensor_copy(mod_rows[:, SB_ * D:(SB_ + 1) * D], b4[0:NB, SB_ * D:(SB_ + 1) * D])
            nc.vector.tensor_scalar(mod_rows[:, CB * D:(CB + 1) * D], b4[0:NB, CB * D:(CB + 1) * D], 1.0, None,
                                    ALU.add).then_inc(S["mod_rdy"], 1)

            def ln_sums(src2, st, n):
                for tile in range(2):
                    last = nc.vector.bn_stats(st[:, tile, :], src2[tile])
                last.then_inc(S[f"st{n}_rdy"], 1)

            def ln_moments(st, mv, ve, b, n):
                for tile in range(2):
                    last = nc.vector.bn_aggr(mv[:, tile, :], st[:, tile, :])
                last.then_inc(S[f"mv{n}_rdy"], 1)
                need(dve, f"mv{n}_rdy", b)
                nc.vector.tensor_scalar(ve[:], mv[:, :, 1], EPS, None, ALU.add).then_inc(S[f"ve{n}_rdy"], 1)

            def ln_stats(src2, st, mv, ve, b, n):
                ln_sums(src2, st, n)
                need_apart(dve, f"st{n}_rdy", b)
                ln_moments(st, mv, ve, b, n)

            def normalize(dst2, src2, mv, r, name):
                for tile in range(2):
                    last = nc.vector.tensor_scalar(dst2[tile], src2[tile], mv[:, tile, 0:1], r[:, tile:tile + 1],
                                                   ALU.subtract, ALU.mult)
                last.then_inc(S[name], 1)

            def x_tile(b, tile):
                return x_sb[:, bass.ds(b * 2 + tile, 1), :].squeeze(1) if not isinstance(b, int) else x_sb[:, b * 2 + tile, :]

            def iteration(i, k):
                a, b, c, e = i, i - 1, i - 2, i - 3
                kb, kc, ke = (k - 1) % 4, (k - 2) % 4, (k - 3) % 4
                if live(a):
                    if isinstance(a, int) and a == 0:
                        dve.wait_ge(S["ld_x"], 32)
                    ln_sums([x_tile(a, 0), x_tile(a, 1)], st1, 1)
                    need(dve, "st1_rdy", a)
                if live(c):
                    need(dve, "pT_tp", c)
                    need(dve, "a_mm", c - 2)
                    for pair in range(2):
                        for half in range(2):
                            q = slice(half * M, (half + 1) * M)
                            last = nc.vector.scalar_tensor_tensor(
                                out=Px[q, kc % 2, 2 * pair + half, :], in0=b6[q, pair * T:(pair + 1) * T], scalar=-1.0,
                                in1=rz[q, kc % 2, 2 + pair, :], op0=ALU.mult, op1=ALU.mult)
                    last.then_inc(S["px_rdy"], 1)
                if live(a):
                    ln_moments(st1, mv1, ve1, a, 1)
                    need(dve, "rstd1_rdy", a)
                    need(dve, "xT_tp", a - 2)
                    normalize([xn[:, k % 2, t, :] for t in range(2)], [x_tile(a, 0), x_tile(a, 1)], mv1, rs1, "xn_rdy")
                if live(b):
                    need(dve, "r0_rdy", b)
                    nc.vector.tensor_tensor(z[:, kb % 2, :, :], z[:, kb % 2, :, :], r0[:], ALU.mult).then_inc(S["nu_rdy"], 1)
                    need(dve, "nu_rdy", b)
                    nc.vector.scalar_tensor_tensor(out=rz[:, kb % 2, :, :], in0=z[:, kb % 2, :, :], scalar=-2.0, in1=r0[:],
                                                   op0=ALU.add, op1=ALU.mult).then_inc(S["rz_rdy"], 1)
                if live(e):
                    need(dve, "out_mm", e)
                    xe = x_sb[:, bass.ds(e * 2, 2), :]
                    nc.vector.tensor_tensor(xe, xe, b7[:, 0:T].rearrange("p (c n) -> p c n", c=2), ALU.add).then_inc(S["x1_rdy"], 1)
                    need_apart(dve, "x1_rdy", e)
                    ln_stats([x_tile(e, 0), x_tile(e, 1)], st2, mv2, ve2, e, 2)
                if live(a):
                    need(dve, "qk_mm", a)
                    need(dve, "rope_rdy", a - 2)
                    for n, bank in ((0, b4), (2, b5)):
                        nc.vector.tensor_tensor(rot[:, k % 2, n, :], bank[:, 0:T], cosT[:], ALU.mult)
                        last = nc.vector.tensor_tensor(rot[:, k % 2, n + 1, :], bank[:, T:2 * T], sinT[:], ALU.mult)
                    last.then_inc(S["ropemul_rdy"], 1)
                if live(e):
                    need(dve, "rstd2_rdy", e)
                    normalize([xn2[:, t, :] for t in range(2)], [x_tile(e, 0), x_tile(e, 1)], mv2, rs2, "xn2_rdy")
                    need(dve, "xn2_rdy", e)
                    cb = modb[:, ke, CB * D:(CB + 1) * D].unsqueeze(1).broadcast_to([P, 2, D])
                    sbb = modb[:, ke, SB_ * D:(SB_ + 1) * D].unsqueeze(1).broadcast_to([P, 2, D])
                    nc.vector.tensor_tensor(h2a[:], xn2[:], cb, ALU.mult).then_inc(S["h2a_rdy"], 1)
                    need(dve, "h2a_rdy", e)
                    nc.vector.tensor_tensor(h2[:], h2a[:], sbb, ALU.add).then_inc(S["h2_rdy"], 1)
                    need_apart(dve, "h2_rdy", e)
                    ln_stats([h2[:, t, :] for t in range(2)], st3, mv3, ve3, e, 3)
                if live(b):
                    need(dve, "lg_mm", b)
                    need(dve, "lgtok_tp", b - 2)
                    need(dve, "rz_rdy", b)
                    nc.vector.scalar_tensor_tensor(out=lg2[:, kb % 2, :, :], in0=b7[:].rearrange("p (c n) -> p c n", c=2),
                                                   scalar=-float(HD) ** -0.5, in1=rz[:, kb % 2, 0:2, :],
                                                   op0=ALU.mult, op1=ALU.mult).then_inc(S["lg2_rdy"], 1)
                if live(e):
                    need(dve, "rstd3_rdy", e)
                    if not (isinstance(e, int) and e < 2):
                        dve.wait_ge(S[f"xhat_st{ke % 2}"], (e - ke % 2) * 8)
                    normalize([xhat[:, ke % 2, t, :] for t in range(2)], [h2[:, t, :] for t in range(2)], mv3, rs3, "xhat_rdy")
                if live(b):
                    need(dve, "lgtok_tp", b)
                    need(dve, "pT_tp", b - 2)
                    lgv = b6[:].rearrange("p (g m) -> p g m", m=M)
                    nc.vector.tensor_reduce(mx[:].rearrange("p c h -> p (c h)"), lgv, AX.X, ALU.max).then_inc(S["mx_rdy"], 1)
                    need(dve, "mx_rdy", b)
                    nc.vector.tensor_tensor(lgs[:, kb % 2, :, :].rearrange("p c (h m) -> p (c h) m", h=H), lgv,
                                            mx[:].rearrange("p c h -> p (c h)").unsqueeze(2).broadcast_to([P, 2 * H, M]),
                                            ALU.subtract).then_inc(S["lgsub_rdy"], 1)
                if live(a):
                    need(dve, "wexp_rdy", a)
                    for w in (wkT[:, k % 2, :, :], wvT[:, k, :, :]):
                        last = nc.vector.tensor_scalar(w, w, float(np.exp(CLAMP)), float(np.exp(-CLAMP)), ALU.min, ALU.max)
                    last.then_inc(S["clip_rdy"], 1)
                if live(b):
                    need(dve, "pexp_rdy", b)
                    need(dve, "pnorm_rdy", b - 1)
                    nc.vector.tensor_reduce(mx[:].rearrange("p c h -> p (c h)"),
                                            lgs[:, kb % 2, :, :].rearrange("p c (h m) -> p (c h) m", h=H), AX.X,
                                            ALU.add).then_inc(S["sum_rdy"], 1)
                    need(dve, "sum_rdy", b)
                    nc.vector.reciprocal(rsum[:], mx[:]).then_inc(S["rsum_rdy"], 1)
                if live(c):
                    need(dve, "rs_rdy", c)
                    need(dve, "out_mm", c - 2)
                    nc.vector.tensor_tensor(onT1[:], b7[:, 0:T], rs[:], ALU.mult).then_inc(S["t1_rdy"], 1)
                    need(dve, "t1_rdy", c)
                    need(dve, "gate_rdy", c)
                    nc.vector.tensor_tensor(onT[:, kc % 2, :], onT1[:], gate[:, kc, :], ALU.mult).then_inc(S["on_rdy"], 1)
                if live(a):
                    need(dve, "clip_rdy", a)
                    for j in range(4):
                        w = wkT[:, k % 2, j, :] if j < 2 else wvT[:, k, j - 2, :]
                        last = nc.vector.tensor_tensor_scan(z[:, k % 2, j, :], ones[:], w, 0.0, ALU.mult, ALU.add)
                    last.then_inc(S["z_rdy"], 1)

            pipeline(dve, iteration)

        @block.tensor
        def _(pe):
            mm, tp = nc.tensor.matmul, nc.tensor.transpose
            pe.wait_ge(S["set_pool"], 9)
            pe.wait_ge(S["ld_rows"], 16 * 11)
            tp(b3[:, 0:P], vec_rows[:], ident[:]).then_inc(S["vec_tp"], 1)
            pe.wait_ge(S["silu_rdy"], 1)
            mm(b3[:, 0:NB], wmod[:, 0:D], cT[:, 3, :], start=True, stop=True)
            mm(b3[:, NB:2 * NB], wmod[:, D:2 * D], cT[:, 3, :], start=True, stop=True)
            mm(b4[0:NB, :], cT[:, 3, :], wmod[:, 2 * D:6 * D], start=True, stop=True).then_inc(S["mod_mm"], 1)
            pe.wait_ge(S["ld_w"], 16 * N_W)
            pe.wait_ge(S["low2_ld"], 64)
            pe.wait_ge(S["set_dve"], 1)
            pe.wait_ge(S["mod_rdy"], 1)

            def iteration(i, k):
                a, b, c, e, d = i, i - 1, i - 2, i - 3, i - 4
                kb, kc, ke, kd = (k - 1) % 4, (k - 2) % 4, (k - 3) % 4, (k - 4) % 4
                if live(b):
                    need(pe, "clip_rdy", b)
                    need(pe, "eg_rdy", b)
                    for ch in range(2):
                        for pair in range(2):
                            last = tp(b3[:, ch * T + pair * P:ch * T + (pair + 1) * P],
                                      wkT[:, kb % 2, pair, ch * P:(ch + 1) * P], ident[:])
                    last.then_inc(S["wkT_tp"], 1)
                if live(e):
                    need(pe, "on_rdy", e)
                    need(pe, "wob_rdy", e)
                    for tile in range(2):
                        last = mm(b7[:, tile * D:(tile + 1) * D], onT[:, ke % 2, tile * P:(tile + 1) * P], Wob[:, ke % 2, :],
                                  start=True, stop=True)
                    last.then_inc(S["out_mm"], 1)
                if live(c):
                    need(pe, "pnorm_rdy", c)
                    need(pe, "rsln_rdy", c - 1)
                    for pair in range(2):
                        for tile in range(2):
                            last = tp(b6[:, pair * T + tile * P:pair * T + (tile + 1) * P],
                                      lgs[:, kc % 2, tile, pair * P:(pair + 1) * P], ident[:])
                    last.then_inc(S["pT_tp"], 1)
                if live(b):
                    need(pe, "rope_rdy", b)
                    need(pe, "a_copied", b - 2)
                    kk = kT[:, kb % 2, :]
                    for n in range(2):
                        mm(banks[n][:], kk[:, 0:P], Qx[:, kb % 2, 2 * n:2 * n + 2, :], start=True, stop=True)
                    mm(banks[2][:], kk[:, P:T], Qx[:, kb % 2, :, P:T], start=True, stop=True).then_inc(S["s_mm"], 1)
                if live(d):
                    need(pe, "xhat_rdy", d)
                    need(pe, "wk_tok_rdy", b)
                    if isinstance(d, int):
                        need(pe, "rlog_rdy", d - 1)
                    for tile in range(2):
                        last = tp(b3[:, T + tile * P:T + (tile + 1) * P], xhat[:, kd % 2, tile, :], ident[:])
                    last.then_inc(S["xhatT_tp"], 1)
                if live(a):
                    need(pe, "xn_rdy", a)
                    need(pe, "wk_tok_rdy", b)
                    for tile in range(2):
                        last = tp(b3[:, tile * P:(tile + 1) * P], xn[:, k % 2, tile, :], ident[:])
                    last.then_inc(S["xT_tp"], 1)
                    need(pe, "hT_rdy", a)
                    need(pe, "wexp_rdy", a - 1)
                    hh = hT[:, k % 2, :]
                    for bank, w, wr in ((b4, Wq, Wqr), (b5, Wk, Wkr)):
                        mm(bank[:, 0:T], w[:], hh, start=True, stop=True)
                        last = mm(bank[:, T:2 * T], wr[:], hh, start=True, stop=True)
                    last.then_inc(S["qk_mm"], 1)
                if live(d):
                    need(pe, "xhatT_rdy", d)
                    for tile in range(2):
                        last = mm(b3[:, T + tile * NE:T + (tile + 1) * NE], xhatT[:, kd % 2, tile * P:(tile + 1) * P], routwg[:],
                                  start=True, stop=True)
                    last.then_inc(S["rlog_mm"], 1)
                if live(a):
                    need(pe, "xhatT_rdy", d)
                    for tile in range(2):
                        last = mm(b3[:, tile * D:(tile + 1) * D], hT[:, k % 2, tile * P:(tile + 1) * P], Wv[:], start=True, stop=True)
                    last.then_inc(S["v_mm"], 1)
                if live(b):
                    need(pe, "s_masked", b)
                    need(pe, "wk_tok_rdy", b)
                    need(pe, "x1_rdy", e)
                    for pair in range(2):
                        for ch in range(2):
                            for half in range(2):
                                h = 2 * pair + half
                                w = wk_tok[:, kb % 2, ch, h * M:(h + 1) * M]
                                o = b7[half * M:(half + 1) * M, pair * T + ch * P:(pair + 1) * T]
                                r = S_sb[:, pair, half * T:(half + 1) * T] if ch == 0 else \
                                    S_sb[:, 2, h * P:(h + 1) * P]
                                last = mm(o, w, r, start=ch == 0, stop=ch == 1)
                    last.then_inc(S["lg_mm"], 1)
                if live(c):
                    need(pe, "px_rdy", c)
                    need(pe, "s_copied", b)
                    for pair in range(2):
                        mm(banks[pair][:], wvT[:, kc, pair, 0:P], Px[:, kc % 2, 2 * pair:2 * pair + 2, :], start=True, stop=True)
                        last = mm(banks[2][:, pair * T:(pair + 1) * T], wvT[:, kc, pair, P:T],
                                  Px[:, kc % 2, 2 * pair:2 * pair + 2, P:T], start=True, stop=True)
                    last.then_inc(S["a_mm"], 1)
                if live(a):
                    need(pe, "v_rdy", a)
                    need(pe, "rlog_rdy", d)
                    mm(b3[0:2 * LOW, T:2 * T], low1[:], hT[:, k % 2, :], start=True, stop=True)
                    mm(b3[:, 0:T], Wg[:], hT[:, k % 2, :], start=True, stop=True).then_inc(S["glt_mm"], 1)
                if live(b):
                    need(pe, "lg2_rdy", b)
                    need(pe, "px_rdy", c)
                    for tile in range(2):
                        for pair in range(2):
                            last = tp(b6[:, tile * T + pair * P:tile * T + (pair + 1) * P],
                                      lg2[:, kb % 2, pair, tile * P:(tile + 1) * P], ident[:])
                    last.then_inc(S["lgtok_tp"], 1)
                if live(c):
                    need(pe, "a_masked", c)
                    need(pe, "lg2_rdy", b)
                    need(pe, "x1_rdy", e)
                    for ch in range(2):
                        for h in range(H):
                            r = A_sb[:, h // 2, (h % 2) * T:(h % 2 + 1) * T] if ch == 0 else A_sb[:, 2, h * P:(h + 1) * P]
                            last = mm(b7[h * HD:(h + 1) * HD, ch * P:T], v_tok[:, kc, ch, h * HD:(h + 1) * HD], r,
                                      start=ch == 0, stop=ch == 1)
                    last.then_inc(S["oT_mm"], 1)
                if live(a):
                    need(pe, "lT_rdy", a)
                    need(pe, "ropemul_rdy", a)
                    for n in range(4):
                        last = mm((b4, b5)[n // 2][:, (n % 2) * T:(n % 2 + 1) * T], low2[:, n, :], lT[:, k % 2, :], start=True, stop=True)
                    last.then_inc(S["skv_mm"], 1)
                if live(c):
                    need(pe, "sq_rdy", c)
                    need(pe, "lgsub_rdy", b)
                    need(pe, "px_rdy", c)
                    mm(b6[:, 0:T], headmean[:], sq[:], start=True, stop=True).then_inc(S["ms_mm"], 1)

            pipeline(pe, iteration)

        ctx.close()
        ctx = outer
        NC2 = 2 * NT
        STEPS = 8
        NS = -(-(NC2 + NE - 1) // STEPS) * STEPS
        NROUND = NS // STEPS
        LAG_T, LAG_U, LAG_D = 3, 4, 5
        RING = 4
        GROUP = 4
        NG = NT // GROUP
        I32 = mybir.dt.int32
        b1T = sb("b1T", [P, NE * NC])
        b2b = sb("b2b", [P, NE, D])
        olw, olb = sb("olw", [P, D]), sb("olb", [P, D])
        gbb = sb("gbb", [P, NB, D])
        outw = sb("outw", [P, NB, D])
        iota_e = sb("iota_e", [P, NE])
        iota_lo = sb("iota_lo", [P, P])
        iota_hi = sb("iota_hi", [P, NS])
        dest1 = sb("dest1", [P, NC2])
        spare = sb("spare", [P, NS])
        upper = sb("upper", [P, P])
        top, topi = sb("top", [P, NT, 8]), sb("topi", [P, NT, 8], U32)
        topf = sb("topf", [P, NT, 2])
        pw = sb("pw", [P, NT, 4])
        onehot = sb("onehot", [P, NE, NC2])
        tot = sb("tot", [P, NE, NC2])
        cum = sb("cum", [P, NE, NC2])
        ones_c = sb("ones_c", [P, NE * NC2])
        cnt = sb("cnt", [P, NE]); cnt_i = sb("cnt_i", [P, NE], I32); ntile = sb("ntile", [P, NE]); tend = sb("tend", [P, NE])
        shift = sb("shift", [P, NE])
        slot_f = sb("slot_f", [P, NC2]); slot_i = sb("slot_i", [P, NC2], I32)
        hi_i = sb("hi_i", [P, NC2], I32); lo_i = sb("lo_i", [P, NC2], I32)
        hi_f = sb("hi_f", [P, NC2]); lo_f = sb("lo_f", [P, NC2])
        ohlo = sb("ohlo", [P, NC2, P]); ohhi = sb("ohhi", [P, NC2, NS])
        past = sb("past", [P, NE - 1, NS])
        exp_f = sb("exp_f", [P, NS]); exp_i = sb("exp_i", [P, NS], I32)
        code = sb("code", [P, NS]); empty = sb("empty", [P, NS])
        idx = sb("idx", [P, NS, 2], U32)
        idxr = sb("idxr", [P, STEPS, 2], U32)
        xg = sb("xg", [P, RING, D])
        waited = sb("waited", [1, 1])
        xgT = sb("xgT", [P, 2, P])
        w1c = sb("w1c", [P, 2, FF]); b1c = sb("b1c", [P, 2, NC])
        hid = sb("hid", [P, 2, NC, P])
        y = sb("y", [P, RING, D])
        ROWS = P * NC2 + P * NS
        y_dram = nc.dram_tensor("y_dram", [ROWS, D], F32, kind="Internal").ap()
        yk = sb("yk", [P, 3, GROUP, 2, D])
        y0 = sb("y0", [P, 2, GROUP, D])
        acc = sb("acc", [P, 2, GROUP, D])
        st4, mv4, ve4, rs4 = sb("st4", [P, GROUP, 6]), sb("mv4", [P, 2, GROUP, 2]), sb("ve4", [P, GROUP]), sb("rs4", [P, GROUP])
        halves4 = sb("halves4", [P, GROUP])
        yn = sb("yn", [P, GROUP, D]); yo = sb("yo", [P, GROUP, D])
        names = """f_ld f_ops f_w1 f_b1mm f_b1 f_iota f_s0 f_s f_oh f_count slot_rdy inv_rdy inv_mm idx_set f_fin waits_done
            idxr_rdy gath0 gath1 gath2 gath3 tile_tp xgT_rdy w1c_rdy up_mm hid_rdy down_mm y_rdy scat0 scat1 scat2 scat3
            yk_ld0 yk_ld1 yk_ld2 y0_rdy acc_rdy st4_rdy mv4_rdy ve4_rdy rs4_rdy yn_rdy yo_rdy out_rdy out_st""".split()
        S.update({n: sem(n) for n in names})
        block = ctx.enter_context(nc.Block())
        up_bank, down_bank, tile_bank = banks[0:2], banks[2:4], banks[4:6]
        NF_OPS = 3

        def need_tile(eng, name, n, k):
            if isinstance(n, int) and not 0 <= n * STEPS + k < NS:
                return
            eng.wait_ge(S[name], n * STEPS + k + 1)

        def need_ring(eng, name, n, k):
            if isinstance(n, int) and not 0 <= n * STEPS + k < NS:
                return
            eng.wait_ge(S[f"{name}{k % RING}"], (n * (STEPS // RING) + k // RING + 1) * 16)

        def has_tile(n, k):
            return not isinstance(n, int) or 0 <= n * STEPS + k < NS

        def tiles(eng, step):
            for k in range(STEPS):
                step(0, k)
            with eng.Fori(1, NROUND) as n:
                for k in range(STEPS):
                    step(n, k)
            for k in range(LAG_D + 1):
                step(NROUND, k)

        def groups(eng, step, lag):
            step(0, True)
            with eng.Fori(1, NG) as g:
                step(g, True)
            if lag:
                step(NG, False)

        @block.sync
        def _(sp):
            sp.dma_start(b2b[:], inp["b2"].rearrange("e d -> (e d)").partition_broadcast(P).rearrange("p (e d) -> p e d", e=NE)).then_inc(S["f_ld"], 16)
            sp.dma_start(olw[:], inp["out_ln_w"].partition_broadcast(P)).then_inc(S["f_ld"], 16)
            sp.dma_start(olb[:], inp["out_ln_b"].partition_broadcast(P)).then_inc(S["f_ld"], 16)
            sp.dma_start(gbb[:], mod_dram[:, GB * D:(GB + 1) * D].partition_broadcast(P)).then_inc(S["f_ld"], 16)
            for r in range(RING):
                sp.wait_ge(S[f"scat{r}"], 16 * (NS // RING))
            yv = y_dram[0:P * NC2, :].rearrange("(p g c) d -> p g (c d)", p=P, g=NG)
            ov = out.rearrange("b (c p) d -> p (b c) d", p=P)

            def load(g, r):
                sp.dma_start(yk[:, r, :, :, :].rearrange("p t k d -> p (t k d)"), yv[:, g, :]).then_inc(S[f"yk_ld{r}"], 16)

            for g in range(NG):
                if g >= 3:
                    sp.wait_ge(S["acc_rdy"], g - 2)
                load(g, g % 3)
            for g in range(NG):
                sp.wait_ge(S["out_rdy"], g + 1)
                sp.dma_start(ov[:, g * GROUP:(g + 1) * GROUP, :], x_sb[:, g * GROUP:(g + 1) * GROUP, :]).then_inc(S["out_st"], 16)
            sp.wait_ge(S["out_st"], 16 * NG)

        @block.gpsimd
        def _(pool):
            small = dict(allow_small_or_imprecise_dtypes=True)
            nc.gpsimd.iota(iota_e[:], pattern=[[1, NE]], base=0, channel_multiplier=0, **small)
            nc.gpsimd.iota(iota_lo[:], pattern=[[1, P]], base=0, channel_multiplier=0, **small)
            nc.gpsimd.iota(iota_hi[:], pattern=[[1, NS]], base=0, channel_multiplier=0, **small)
            nc.gpsimd.iota(dest1[:], pattern=[[1, NC2]], base=1, channel_multiplier=NC2, **small)
            nc.gpsimd.iota(spare[:], pattern=[[P, NS]], base=P * NC2 + 1, channel_multiplier=1, **small)
            nc.gpsimd.memset(ones_c[:], 1.0)
            nc.gpsimd.memset(upper[:], 1.0).then_inc(S["f_iota"], 1)
            pool.wait_ge(S["f_iota"], 1)
            nc.gpsimd.affine_select(out=upper[:], in_=upper[:], compare_op=ALU.is_ge, fill=0.0, base=-1,
                                    pattern=[[1, P]], channel_multiplier=-1)
            nc.gpsimd.memset(halves4[:], -0.5).then_inc(S["f_iota"], 1)
            for r in range(2):
                pool.wait_ge(S[f"xhat_st{r}"], 16 * NB // 2)

            def step(n, k):
                kk = (k - LAG_D) % STEPS
                need_tile(pool, "tile_tp", n, k - RING)
                need_tile(pool, "idxr_rdy", n, k)
                need_tile(pool, "y_rdy", n, k - LAG_D)
                if has_tile(n, k):
                    need_tile(pool, "waits_done", n, k - 1)
                    nc.gpsimd.tensor_tensor(waited[:], halves4[0:1, 0:1], halves4[0:1, 0:1], ALU.mult).then_inc(S["waits_done"], 1)
                if has_tile(n, k):
                    nc.gpsimd.indirect_dma_start(xg[:, k % RING, :], None, xhat_dram,
                                                 bass.IndirectOffsetOnAxis(idxr[:, k, 0:1], 0)).then_inc(S[f"gath{k % RING}"], 16)
                if has_tile(n, k - LAG_D):
                    nc.gpsimd.indirect_dma_start(y_dram, bass.IndirectOffsetOnAxis(idxr[:, kk, 1:2], 0),
                                                 y[:, kk % RING, :], None).then_inc(S[f"scat{kk % RING}"], 16)
            tiles(pool, step)
            with pool.Fori(0, NG) as g:
                pool.wait_ge(S["ve4_rdy"], g + 1)
                nc.gpsimd.tensor_tensor(rs4[:], ve4[:], halves4[:], ALU.pow).then_inc(S["rs4_rdy"], 1)

        @block.scalar
        def _(act):
            act.wait_ge(S["f_s0"], 1)
            nc.scalar.activation(pw[:, :, 1], pw[:, :, 0], ACT.Exp).then_inc(S["f_s"], 1)
            act.wait_ge(S["f_b1"], 1)

            def step(n, k):
                if has_tile(n, k - LAG_U):
                    r = (k - LAG_U) % 2
                    need_tile(act, "w1c_rdy", n, k - LAG_U)
                    need_tile(act, "down_mm", n, k - LAG_U - 2)
                    need_tile(act, "up_mm", n, k - LAG_U)
                    for j in range(NC):
                        last = nc.scalar.activation(hid[:, r, j, :], up_bank[r][:, j * P:(j + 1) * P], ACT.Gelu, bias=b1c[:, r, j:j + 1])
                    last.then_inc(S["hid_rdy"], 1)
            tiles(act, step)
            for g in range(NG):
                act.wait_ge(S[f"yk_ld{g % 3}"], 16 * (g // 3 + 1))
                if g >= 2:
                    act.wait_ge(S["acc_rdy"], g - 1)
                for t in range(GROUP):
                    last = nc.scalar.activation(y0[:, g % 2, t, :], yk[:, g % 3, t, 0, :], ACT.Copy, scale=pw[:, g * GROUP + t, 2:3])
                last.then_inc(S["y0_rdy"], 1)

        @block.vector
        def _(dve):
            n_ops = [0]

            def link(ins):
                n_ops[0] += 1
                ins.then_inc(S["f_ops"], 1)
                dve.wait_ge(S["f_ops"], n_ops[0])

            tt, ts = nc.vector.tensor_tensor, nc.vector.tensor_scalar
            dve.wait_ge(S["ld_ffn"], 32)
            dve.wait_ge(S["f_b1mm"], 1)
            tt(b1T[:], banks[6][:, 0:NE * NC], vecT[:, R_B1:R_B1 + NE * NC], ALU.add)
            tt(rbias[:], banks[7][:, 0:NE], rbias[:], ALU.add).then_inc(S["f_b1"], 1)
            for e in range(NE):
                last = ts(w1s[:, e, :], w1s[:, e, :], vecT[:, R_LNW + e:R_LNW + e + 1], None, ALU.mult)
            last.then_inc(S["f_w1"], 1)
            dve.wait_ge(S["f_b1"], 1)
            link(tt(rlog[:], rlog[:], rbias[:].unsqueeze(1).broadcast_to([P, NT, NE]), ALU.add))
            for j in range(NT):
                last = nc.vector.max(top[:, j, :], rlog[:, j, :])
            link(last)
            for j in range(NT):
                last = nc.vector.max_index(topi[:, j, :], top[:, j, :], rlog[:, j, :])
            link(last)
            tt(pw[:, :, 0], top[:, :, 1], top[:, :, 0], ALU.subtract).then_inc(S["f_s0"], 1)
            link(nc.vector.tensor_copy(topf[:], topi[:, :, 0:2]))
            dve.wait_ge(S["f_iota"], 2)
            tt(onehot[:].rearrange("p e (t k) -> p e t k", k=2), iota_e[:].unsqueeze(2).unsqueeze(3).broadcast_to([P, NE, NT, 2]),
               topf[:].unsqueeze(1).broadcast_to([P, NE, NT, 2]), ALU.is_equal).then_inc(S["f_oh"], 1)
            dve.wait_ge(S["f_s"], 1)
            link(ts(pw[:, :, 2], pw[:, :, 1], 1.0, None, ALU.add))
            link(nc.vector.reciprocal(pw[:, :, 2], pw[:, :, 2]))
            link(tt(pw[:, :, 3], pw[:, :, 1], pw[:, :, 2], ALU.mult))
            dve.wait_ge(S["f_count"], 2)
            link(nc.vector.tensor_copy(tot[:], banks[1][:].rearrange("p (e c) -> p e c", e=NE)))
            link(nc.vector.tensor_tensor_scan(cum[:].rearrange("p e c -> p (e c)"), ones_c[:], tot[:].rearrange("p e c -> p (e c)"), 0.0, ALU.mult, ALU.add))
            nc.vector.tensor_copy(cnt[:, 0:1], cum[:, 0, NC2 - 1:NC2])
            link(tt(cnt[:, 1:NE], cum[:, 1:NE, NC2 - 1], cum[:, 0:NE - 1, NC2 - 1], ALU.subtract))
            link(ts(cnt_i[:], cnt[:], float(P - 1), None, ALU.add))
            link(ts(cnt_i[:], cnt_i[:], 7, None, ALU.logical_shift_right))
            link(nc.vector.tensor_copy(ntile[:], cnt_i[:]))
            link(nc.vector.tensor_tensor_scan(tend[:], ones_c[:, 0:NE], ntile[:], 0.0, ALU.mult, ALU.add))
            link(tt(shift[:], tend[:], ntile[:], ALU.subtract))
            link(ts(shift[:], shift[:], float(P), None, ALU.mult))
            link(tt(shift[:], shift[:], cum[:, :, NC2 - 1], ALU.subtract))
            link(tt(shift[:], shift[:], cnt[:], ALU.add))
            link(tt(cum[:], cum[:], tot[:], ALU.subtract))
            link(tt(cum[:], cum[:], banks[0][:].rearrange("p (e c) -> p e c", e=NE), ALU.add))
            link(tt(cum[:], cum[:], shift[:].unsqueeze(2).broadcast_to([P, NE, NC2]), ALU.add))
            link(tt(tot[:], cum[:], onehot[:], ALU.mult))
            link(nc.vector.tensor_reduce(slot_f[:], tot[:].rearrange("p e c -> p c e"), AX.X, ALU.add))
            link(nc.vector.tensor_copy(slot_i[:], slot_f[:]))
            link(ts(hi_i[:], slot_i[:], 7, None, ALU.logical_shift_right))
            link(ts(lo_i[:], slot_i[:], P - 1, None, ALU.bitwise_and))
            nc.vector.tensor_copy(hi_f[:], hi_i[:])
            link(nc.vector.tensor_copy(lo_f[:], lo_i[:]))
            for c in range(NC2):
                ts(ohlo[:, c, :], iota_lo[:], lo_f[:, c:c + 1], None, ALU.is_equal)
                ts(ohhi[:, c, :], iota_hi[:], hi_f[:, c:c + 1], dest1[:, c:c + 1], ALU.is_equal, ALU.mult).then_inc(S["slot_rdy"], 1)
            link(tt(past[:], iota_hi[:].unsqueeze(1).broadcast_to([P, NE - 1, NS]), tend[:, 0:NE - 1].unsqueeze(2).broadcast_to([P, NE - 1, NS]), ALU.is_ge))
            link(nc.vector.tensor_reduce(exp_f[:], past[:].rearrange("p e s -> p s e"), AX.X, ALU.add))
            nc.vector.tensor_copy(exp_i[:], exp_f[:])
            dve.wait_ge(S["inv_mm"], 1)
            link(ts(empty[:], banks[2][:, 0:NS], 1.0, None, ALU.is_lt))
            link(tt(code[:], empty[:], spare[:], ALU.mult))
            link(tt(code[:], code[:], banks[2][:, 0:NS], ALU.add))
            link(ts(idx[:, :, 1], code[:], -1.0, None, ALU.add))
            link(ts(idx[:, :, 0], idx[:, :, 1], 1, None, ALU.logical_shift_right))
            link(ts(idx[:, :, 0], idx[:, :, 0], P * NT - 1, None, ALU.min))
            nc.vector.memset(ve4[:], 1.0).then_inc(S["idx_set"], 1)
            dve.wait_ge(S["idx_set"], 1)
            dve.wait_ge(S["f_ld"], 64)

            def expert_of(n, k):
                if isinstance(n, int):
                    j = n * STEPS + k
                    return dve.value_load(exp_i[0:1, j:j + 1], min_val=0, max_val=NE - 1)
                return dve.value_load(exp_i[0:1, bass.ds(n * STEPS + k, 1)], min_val=0, max_val=NE - 1)

            def step(n, k):
                if has_tile(n, k):
                    need_ring(dve, "scat", n, k - STEPS)
                    nc.vector.tensor_copy(idxr[:, k, :], idx[:, bass.ds(n * STEPS + k, 1), :].squeeze(1)).then_inc(S["idxr_rdy"], 1)
                if has_tile(n, k - LAG_T):
                    kk = k - LAG_T
                    e = expert_of(n, kk)
                    need_tile(dve, "hid_rdy", n, kk - 2)
                    nc.vector.tensor_copy(w1c[:, kk % 2, :], w1s[:, bass.ds(e, 1), :].squeeze(1))
                    nc.vector.tensor_copy(b1c[:, kk % 2, :], b1T[:, bass.ds(e * NC, NC)]).then_inc(S["w1c_rdy"], 1)
                    need_tile(dve, "tile_tp", n, kk)
                    nc.vector.tensor_copy(xgT[:, kk % 2, :], tile_bank[kk % 2][:, 0:P]).then_inc(S["xgT_rdy"], 1)
                if has_tile(n, k - LAG_D):
                    kk = k - LAG_D
                    e = expert_of(n, kk)
                    need_ring(dve, "scat", n, kk - RING)
                    need_tile(dve, "down_mm", n, kk)
                    tt(y[:, kk % RING, :], down_bank[kk % 2][:, 0:D], b2b[:, bass.ds(e, 1), :].squeeze(1), ALU.add).then_inc(S["y_rdy"], 1)
            tiles(dve, step)
            tt(outw[:], gbb[:], olw[:].unsqueeze(1).broadcast_to([P, NB, D]), ALU.mult)
            tt(gbb[:], gbb[:], olb[:].unsqueeze(1).broadcast_to([P, NB, D]), ALU.mult).then_inc(S["f_fin"], 1)
            dve.wait_ge(S["f_fin"], 1)
            xv = x_sb[:].rearrange("p (b c) d -> p b c d", c=2)
            tt(xv, xv, gbb[:].unsqueeze(2).broadcast_to([P, NB, 2, D]), ALU.add).then_inc(S["f_fin"], 1)
            dve.wait_ge(S["f_fin"], 2)
            for g in range(NG + 1):
                if g < NG:
                    dve.wait_ge(S["y0_rdy"], g + 1)
                    for t in range(GROUP):
                        last = nc.vector.scalar_tensor_tensor(out=acc[:, g % 2, t, :], in0=yk[:, g % 3, t, 1, :], scalar=pw[:, g * GROUP + t, 3:4],
                                                              in1=y0[:, g % 2, t, :], op0=ALU.mult, op1=ALU.add)
                    last.then_inc(S["acc_rdy"], 1)
                if g >= 1:
                    dve.wait_ge(S["rs4_rdy"], g)
                    for t in range(GROUP):
                        last = ts(yn[:, t, :], acc[:, (g - 1) % 2, t, :], mv4[:, (g - 1) % 2, t, 0:1], rs4[:, t:t + 1], ALU.subtract, ALU.mult)
                    last.then_inc(S["yn_rdy"], 1)
                if g < NG:
                    dve.wait_ge(S["acc_rdy"], g + 1)
                    for t in range(GROUP):
                        last = nc.vector.bn_stats(st4[:, t, :], acc[:, g % 2, t, :])
                    last.then_inc(S["st4_rdy"], 1)
                if g >= 1:
                    dve.wait_ge(S["yn_rdy"], g)
                    b0 = (g - 1) * GROUP // 2
                    v = lambda a: a.rearrange("p (b c) d -> p b c d", c=2)
                    tt(v(yo[:]), v(yn[:]), outw[:, b0:b0 + GROUP // 2, :].unsqueeze(2).broadcast_to([P, GROUP // 2, 2, D]), ALU.mult).then_inc(S["yo_rdy"], 1)
                if g < NG:
                    dve.wait_ge(S["st4_rdy"], g + 1)
                    for t in range(GROUP):
                        last = nc.vector.bn_aggr(mv4[:, g % 2, t, :], st4[:, t, :])
                    last.then_inc(S["mv4_rdy"], 1)
                    dve.wait_ge(S["mv4_rdy"], g + 1)
                    ts(ve4[:], mv4[:, g % 2, :, 1], EPS, None, ALU.add).then_inc(S["ve4_rdy"], 1)
                if g >= 1:
                    dve.wait_ge(S["yo_rdy"], g)
                    xg_ = x_sb[:, (g - 1) * GROUP:g * GROUP, :]
                    tt(xg_, xg_, yo[:], ALU.add).then_inc(S["out_rdy"], 1)

        @block.tensor
        def _(pe):
            mm = nc.tensor.matmul
            pe.wait_ge(S["ld_ffn"], 32)
            mm(banks[7][:, 0:NE], vecT[:, R_RB:R_RB + 1].broadcast_to([P, P]), routw[:], start=True, stop=True)
            for e in range(NE):
                for j in range(NC):
                    last = mm(banks[6][:, e * NC + j:e * NC + j + 1], w1s[:, e, j * P:(j + 1) * P], vecT[:, R_LNB + e:R_LNB + e + 1], start=True, stop=True)
            last.then_inc(S["f_b1mm"], 1)
            pe.wait_ge(S["f_oh"], 1)
            oh = onehot[:].rearrange("p e c -> p (e c)")
            mm(banks[1][:], ones_c[:, 0:P], oh, start=True, stop=True).then_inc(S["f_count"], 1)
            mm(banks[0][:], upper[:], oh, start=True, stop=True).then_inc(S["f_count"], 1)
            for c in range(NC2):
                pe.wait_ge(S["slot_rdy"], c + 1)
                last = mm(banks[2][:, 0:NS], ohlo[:, c, :], ohhi[:, c, :], start=c == 0, stop=c == NC2 - 1)
            last.then_inc(S["inv_mm"], 1)
            pe.wait_ge(S["idx_set"], 1)
            pe.wait_ge(S["f_w1"], 1)

            def step(n, k):
                if has_tile(n, k - LAG_T):
                    kk = k - LAG_T
                    need_tile(pe, "xgT_rdy", n, kk - 2)
                    need_ring(pe, "gath", n, kk)
                    nc.tensor.transpose(tile_bank[kk % 2][:, 0:P], xg[:, kk % RING, :], ident[:]).then_inc(S["tile_tp"], 1)
                if has_tile(n, k - LAG_U):
                    kk = k - LAG_U
                    need_tile(pe, "hid_rdy", n, kk - 2)
                    need_tile(pe, "xgT_rdy", n, kk)
                    for j in range(NC):
                        last = mm(up_bank[kk % 2][:, j * P:(j + 1) * P], w1c[:, kk % 2, j * P:(j + 1) * P], xgT[:, kk % 2, :], start=True, stop=True)
                    last.then_inc(S["up_mm"], 1)
                if has_tile(n, k - LAG_D):
                    kk = k - LAG_D
                    if isinstance(n, int):
                        e = pe.value_load(exp_i[0:1, n * STEPS + kk:n * STEPS + kk + 1], min_val=0, max_val=NE - 1)
                    else:
                        e = pe.value_load(exp_i[0:1, bass.ds(n * STEPS + kk, 1)], min_val=0, max_val=NE - 1)
                    need_tile(pe, "y_rdy", n, kk - 2)
                    need_tile(pe, "hid_rdy", n, kk)
                    for j in range(NC):
                        last = mm(down_bank[kk % 2][:, 0:D], hid[:, kk % 2, j, :], w2s[:, bass.ds(e, 1), j, :].squeeze(1), start=j == 0, stop=j == NC - 1)
                    last.then_inc(S["down_mm"], 1)
            tiles(pe, step)


_INS = dict(x="L0_attn_hidden_states", Wq="L0_attn_Wq", Wk="L0_attn_Wk", Wv="L0_attn_Wv", Wg="L0_attn_Wg", Wo="L0_attn_Wo",
            sk_w1="L0_attn_sk_w1", sk_w2="L0_attn_sk_w2", sk_b2="L0_attn_sk_b2", sv_w1="L0_attn_sv_w1", sv_w2="L0_attn_sv_w2",
            sv_b2="L0_attn_sv_b2", gnorm_w="L0_attn_gnorm_w", router_ln_w="L0_ffn_router_ln_w", router_ln_b="L0_ffn_router_ln_b",
            router_w="L0_ffn_router_w", router_b="L0_ffn_router_b", exp_ln_w="L0_ffn_exp_ln_w", exp_ln_b="L0_ffn_exp_ln_b",
            w1="L0_ffn_w1", b1="L0_ffn_b1", w2="L0_ffn_w2", b2="L0_ffn_b2", out_ln_w="L0_ffn_out_ln_w", out_ln_b="L0_ffn_out_ln_b",
            c="L0_c", wmod="L0_wmod")


def rope_tables():
    half = HD // 2
    inv_freq = (1.0 / 10000.0 ** (np.arange(half, dtype=np.float32) / half)).astype(np.float32)
    ang = np.arange(T, dtype=np.float32)[None, :] * inv_freq[:, None]
    cos, sin = np.cos(ang), np.sin(ang)
    return (np.ascontiguousarray(np.tile(np.concatenate([cos, cos]), (H, 1))),
            np.ascontiguousarray(np.tile(np.concatenate([-sin, sin]), (H, 1))))


def kernel(**inputs):
    import concourse.bacc as bacc
    from concourse.bass_utils import run_bass_kernel_spmd

    nc = bacc.Bacc("TRN2", target_bir_lowering=False, num_devices=1)
    arrays = {n: np.ascontiguousarray(inputs[full]) for n, full in _INS.items()}
    arrays["cosT"], arrays["sinT"] = rope_tables()
    aps = {n: nc.dram_tensor(f"in_{n}", a.shape, F32, kind="ExternalInput").ap() for n, a in arrays.items()}
    out = nc.dram_tensor("out", [NB, T, D], F32, kind="ExternalOutput").ap()
    build(nc, aps, out)
    r = run_bass_kernel_spmd(nc, [{f"in_{n}": a for n, a in arrays.items()}], core_ids=[0])
    return r.results[0]["out"]
```

```python
import numpy as np
from contextlib import ExitStack

import concourse.bass as bass
from concourse import mybir

F32 = mybir.dt.float32
BF16 = mybir.dt.bfloat16
U32 = mybir.dt.uint32
ACT = mybir.ActivationFunctionType
ALU = mybir.AluOpType
AX = mybir.AxisListType

P = 128
NB = 16
T = 256
D = 128
H = 4
HD = D // H
M = 64
LOW = 16
NE = 8
FF = 512
NC = FF // P
NT = NB * T // P
EPS = 1e-5
CLAMP = 32.0
UNROLL = 4
PEEL = 4
LAST_LAG = 4


def build(nc, inp, out):
    with ExitStack() as ctx:
        def sb(name, shape, dt=F32):
            return ctx.enter_context(nc.sbuf_tensor(name, shape, dt))

        def sem(name):
            return ctx.enter_context(nc.semaphore(name))

        banks = [ctx.enter_context(nc.psum_tensor(f"bank{i}", [P, 512], F32)) for i in range(8)]
        b3, b4, b5, b6, b7 = banks[3:]

        x_sb = sb("x_sb", [P, NT, D])
        Wq, Wqr, Wk, Wkr, Wv, Wg, Wo, Wog = [sb(n, [P, D]) for n in ("Wq", "Wqr", "Wk", "Wkr", "Wv", "Wg", "Wo", "Wog")]
        low1 = sb("low1", [P, 2 * LOW])
        low2 = sb("low2", [P, 4, P])
        cosT, sinT = sb("cosT", [P, T]), sb("sinT", [P, T])
        ident = sb("ident", [P, P])
        headmean = sb("headmean", [P, P])
        ones = sb("ones", [P, T])
        halves = sb("halves", [P, 2])
        vec_rows = sb("vec_rows", [P, D])
        vecT = sb("vecT", [P, 96])
        cT = sb("cT", [P, 4, NB])
        wmod = sb("wmod", [P, 6 * D])
        saT, caT = sb("saT", [P, NB]), sb("caT", [P, NB])
        mod_rows = sb("mod_rows", [NB, 4 * D])
        mod_tmp = sb("mod_tmp", [NB, 2, 2, D])
        modb = sb("modb", [P, 4, 3 * D])
        routw = sb("routw", [P, NE])
        routwg = sb("routwg", [P, NE])
        mod_dram = nc.dram_tensor("mod_dram", [NB, 4 * D], F32, kind="Internal").ap()
        R_LNW, R_LNB, R_RW, R_RB, R_GN, R_C, R_B1 = 0, 8, 16, 17, 18, 32, 48
        NROW = R_B1 + NE * NC
        GA, SB_, CB, GB = 0, 1, 2, 3

        w1s = sb("w1s", [P, NE, FF])
        w2s = sb("w2s", [P, NE, NC, D])
        rbias = sb("rbias", [P, NE])
        b1T = sb("b1T", [P, NE * NC])
        rlog = sb("rlog", [P, NT, NE])
        xhat_dram = nc.dram_tensor("xhat_dram", [P * NT, D], F32, kind="Internal").ap()
        top, topi = sb("top", [P, NT, 8]), sb("topi", [P, NT, 8], U32)
        b1_rows = sb("b1_rows", [NE, FF])
        outer, ctx = ctx, ExitStack()
        lnb_x = sb("lnb_x", [P, NE, NE])
        mv1 = sb("mv1", [P, 2, 2]); st1 = sb("st1", [P, 2, 6]); ve1 = sb("ve1", [P, 2]); rs1 = sb("rs1", [P, 2])
        mv2 = sb("mv2", [P, 2, 2]); st2 = sb("st2", [P, 2, 6]); ve2 = sb("ve2", [P, 2]); rs2 = sb("rs2", [P, 2])
        mv3 = sb("mv3", [P, 2, 2]); st3 = sb("st3", [P, 2, 6]); ve3 = sb("ve3", [P, 2]); rs3 = sb("rs3", [P, 2])
        xn = sb("xn", [P, 2, 2, D])
        hT = sb("hT", [P, 2, T])
        rot = sb("rot", [P, 2, 4, T])
        Qx = sb("Qx", [P, 2, H, T])
        qT = sb("qT", [P, T])
        headmask = sb("headmask", [P, H, 2])
        kT = sb("kT", [P, 2, T])
        lT = sb("lT", [P, 2, T])
        v_tok = sb("v_tok", [P, 4, 2, D])
        g_sb, eg = sb("g_sb", [P, 2, T]), sb("eg", [P, 2, T])
        gate = sb("gate", [P, 4, T])
        wkT = sb("wkT", [P, 2, 2, T])
        wvT = sb("wvT", [P, 4, 2, T])
        z = sb("z", [P, 2, 4, T])
        r0 = sb("r0", [P, 4, T])
        rz = sb("rz", [P, 2, 4, T])
        wk_tok = sb("wk_tok", [P, 2, 2, H * M])
        S_sb = sb("S_sb", [P, 3, 512])
        A_sb = sb("A_sb", [P, 3, 512])
        eps_col = sb("eps_col", [P, 1])[:]
        lg2 = sb("lg2", [P, 2, 2, T])
        mx = sb("mx", [P, 2, H]); rsum = sb("rsum", [P, 2, H])
        lgs = sb("lgs", [P, 2, 2, H * M])
        Px = sb("Px", [P, 2, H, T])
        sq = sb("sq", [P, T]); rs = sb("rs", [P, T]); onT1 = sb("onT1", [P, T]); onT = sb("onT", [P, 2, T])
        Wob = sb("Wob", [P, 2, D])
        xn2 = sb("xn2", [P, 2, D]); h2 = sb("h2", [P, 2, D]); h2a = sb("h2a", [P, 2, D])
        xhat = sb("xhat", [P, 2, 2, D])
        xhatT = sb("xhatT", [P, 2, T])

        names = """ld_x0 ld_x ld_qk ld_w ld_c ld_wmod ld_rows ld_ffn set_pool set_dve set_zero low2_ld vec_tp vec_rdy silu_e silu_rdy mod_mm mod_rdy mod_st q_rdy modb_ld0 modb_ld1 modb_ld2 modb_ld3
            wkT_tp out_mm pT_tp s_mm s_mm01 a_mm01 wkexp_rdy wkclip_rdy s_copied01 a_copied01 xT_tp xhatT_tp qk_mm v_mm rlog_mm lg_mm a_mm glt_mm lgtok_tp oT_mm skv_mm ms_mm
            lnz_rdy r0_rdy wk_tok_rdy s_copied hT_rdy xhatT_rdy v_rdy rlog_rdy a_copied lT_rdy eg_rdy sq_rdy wexp_rdy pexp_rdy
            ffn_mm ffn_bias top_step top_rdy rsln_rdy rs_rdy sigln_rdy sig_rdy
            st1_rdy mv1_rdy ve1_rdy xn_rdy px_rdy nu_rdy rz_rdy x1_rdy st2_rdy mv2_rdy ve2_rdy xn2_rdy h2a_rdy h2_rdy st3_rdy mv3_rdy ve3_rdy
            xhat_rdy ropemul_rdy lg2_rdy mx_rdy lgsub_rdy t1_rdy on_rdy sum_rdy rsum_rdy clip_rdy z_rdy
            rstd1_rdy gate_rdy wob_rdy rstd2_rdy s_masked rope_rdy rstd3_rdy a_masked egc_rdy pnorm_rdy xhat_st0 xhat_st1 dve_chain""".split()
        S = {n: sem(n) for n in names}

        def need(eng, name, batch):
            if isinstance(batch, int) and not 0 <= batch < NB:
                return
            eng.wait_ge(S[name], batch + 1)

        def need_apart(eng, name, batch):
            eng.wait_ge(S["vec_tp"], 1)
            need(eng, name, batch)

        def live(batch):
            return not isinstance(batch, int) or 0 <= batch < NB

        def pipeline(eng, iteration):
            for i in range(PEEL):
                iteration(i, i % UNROLL)
            with eng.Fori(PEEL // UNROLL, NB // UNROLL) as n:
                for k in range(UNROLL):
                    iteration(n * UNROLL + k, k)
            for i in range(NB, NB + LAST_LAG):
                iteration(i, i % UNROLL)

        def slot_loads(batch, slot):
            if isinstance(batch, int):
                return 16 * (batch // 4 + 1)
            return (batch - slot + 4) * 4

        block = ctx.enter_context(nc.Block())

        @block.sync
        def _(sp):
            xv = inp["x"].rearrange("b (c p) d -> p (b c) d", p=P)
            sp.dma_start(x_sb[:, 0:4, :], xv[:, 0:4, :]).then_inc(S["ld_x0"], 16)
            sp.wait_ge(S["ld_c"], 16)
            for dst, name in ((Wq, "Wq"), (Wk, "Wk")):
                sp.dma_start(dst[:], inp[name]).then_inc(S["ld_qk"], 16)
            for dst, name in ((Wqr, "Wq"), (Wkr, "Wk")):
                dv = dst[:].rearrange("p (h two c) -> p h two c", h=H, two=2)
                sv = inp[name].rearrange("p (h two c) -> p h two c", h=H, two=2)
                for half in range(2):
                    sp.dma_start(dv[:, :, half, :], sv[:, :, 1 - half, :]).then_inc(S["ld_qk"], 16)
            for dst, name in ((Wv, "Wv"), (Wg, "Wg"), (Wo, "Wo"), (cosT, "cosT"), (sinT, "sinT"), (routw, "router_w")):
                sp.dma_start(dst[:], inp[name]).then_inc(S["ld_w"], 16)
            sp.dma_start(low1[:, 0:LOW], inp["sk_w1"]).then_inc(S["ld_w"], 16)
            sp.dma_start(low1[:, LOW:2 * LOW], inp["sv_w1"]).then_inc(S["ld_w"], 16)
            sp.dma_start(rbias[:], inp["router_b"].partition_broadcast(P)).then_inc(S["ld_w"], 16)
            sp.dma_start(x_sb[:, 4:NT, :], xv[:, 4:NT, :]).then_inc(S["ld_x"], 16)
            sp.dma_start(w1s[:], inp["w1"].rearrange("e d i -> d e i")).then_inc(S["ld_ffn"], 16)
            sp.dma_start(w2s[:], inp["w2"].rearrange("e (c p) d -> p e c d", p=P)).then_inc(S["ld_ffn"], 16)
            sp.wait_ge(S["mod_rdy"], 2)
            sp.dma_start(mod_dram, mod_rows[:]).then_inc(S["mod_st"], 16)
            sp.wait_ge(S["mod_st"], 16)
            xrows = xhat_dram.rearrange("(p b c) d -> p b (c d)", p=P, c=2)

            def iteration(i, k):
                if live(i):
                    need(sp, "h2_rdy", i - 4)
                    if isinstance(i, int):
                        src = mod_dram[i, 0:3 * D]
                    else:
                        src = mod_dram[bass.ds(i, 1), 0:3 * D].squeeze(0)
                    sp.dma_start(modb[:, k, :], src.partition_broadcast(P)).then_inc(S[f"modb_ld{k}"], 16)
                if live(i - 4):
                    need(sp, "xhat_rdy", i - 4)
                    sp.dma_start(xrows[:, bass.ds(i - 4, 1), :].squeeze(1), xhat[:, k % 2, :, :].rearrange("p c d -> p (c d)")).then_inc(S[f"xhat_st{k % 2}"], 16)
            pipeline(sp, iteration)
            for r in range(2):
                sp.wait_ge(S[f"xhat_st{r}"], 16 * NB // 2 + 16)
        N_QK, N_W = 6, 9

        @block.gpsimd
        def _(pool):
            def gate_step(a, k):
                need(pool, "sig_rdy", a)
                nc.gpsimd.tensor_tensor(gate[:, k, :], g_sb[:, k % 2, :], eg[:, k % 2, :], ALU.mult).then_inc(S["gate_rdy"], 1)

            nc.gpsimd.memset(ident[:], 1.0).then_inc(S["set_pool"], 1)
            nc.gpsimd.memset(headmean[:], 1.0 / HD).then_inc(S["set_pool"], 1)
            nc.gpsimd.memset(halves[:], -0.5).then_inc(S["set_pool"], 1)
            nc.gpsimd.memset(headmask[:], 1.0).then_inc(S["set_pool"], 1)
            pool.wait_ge(S["set_pool"], 4)
            nc.gpsimd.affine_select(out=ident[:], in_=ident[:], compare_op=ALU.is_equal, fill=0.0, base=0,
                                    pattern=[[-1, P]], channel_multiplier=1).then_inc(S["set_pool"], 1)
            for n, hm in enumerate((headmean[:].rearrange("p (h c) -> p h c", h=H), headmask[:])):
                w = hm.shape[2]
                nc.gpsimd.affine_select(out=hm, in_=hm, compare_op=ALU.is_ge, fill=0.0, base=0,
                                        pattern=[[-HD, H], [0, w]], channel_multiplier=1).then_inc(S["set_pool"], 1)
                pool.wait_ge(S["set_pool"], 6 + 2 * n)
                nc.gpsimd.affine_select(out=hm, in_=hm, compare_op=ALU.is_ge, fill=0.0, base=HD - 1,
                                        pattern=[[HD, H], [0, w]], channel_multiplier=-1).then_inc(S["set_pool"], 1)

            def iteration(i, k):
                a, b, c, e, d = i, i - 1, i - 2, i - 3, i - 4
                kb, kc, ke, kd = (k - 1) % 4, (k - 2) % 4, (k - 3) % 4, (k - 4) % 4
                if live(a):
                    need(pool, "ve1_rdy", a)
                    nc.gpsimd.tensor_tensor(rs1[:], ve1[:], halves[:], ALU.pow).then_inc(S["rstd1_rdy"], 1)
                if live(b):
                    gate_step(b, kb)
                if live(c):
                    pool.wait_ge(S[f"modb_ld{kc}"], slot_loads(c, kc))
                    if isinstance(c, int) and c == 0:
                        pool.wait_ge(S["vec_rdy"], 2)
                    need(pool, "out_mm", c - 2)
                    nc.gpsimd.tensor_tensor(Wob[:, kc % 2, :], Wog[:], modb[:, kc, GA * D:(GA + 1) * D],
                                            ALU.mult).then_inc(S["wob_rdy"], 1)
                if live(b):
                    need_apart(pool, "s_copied01", b)
                    causal01(S_sb)
                    need_apart(pool, "s_copied", b)
                    causal2(S_sb, "s_masked")
                if live(e):
                    need(pool, "ve2_rdy", e)
                    nc.gpsimd.tensor_tensor(rs2[:], ve2[:], halves[:], ALU.pow).then_inc(S["rstd2_rdy"], 1)
                if live(a):
                    need(pool, "ropemul_rdy", a)
                    need(pool, "s_mm", a - 2)
                    nc.gpsimd.tensor_tensor(qT[:], rot[:, k % 2, 0, :], rot[:, k % 2, 1, :], ALU.add).then_inc(S["q_rdy"], 1)
                if live(a):
                    need_apart(pool, "q_rdy", a)
                    for h in range(H):
                        nc.gpsimd.tensor_scalar(Qx[:, k % 2, h, :], qT[:], headmask[:, h, 0:1], 1.0, ALU.mult, ALU.mult)
                    nc.gpsimd.tensor_tensor(kT[:, k % 2, :], rot[:, k % 2, 2, :], rot[:, k % 2, 3, :],
                                            ALU.add).then_inc(S["rope_rdy"], 1)
                if live(e):
                    need(pool, "ve3_rdy", e)
                    nc.gpsimd.tensor_tensor(rs3[:], ve3[:], halves[:], ALU.pow).then_inc(S["rstd3_rdy"], 1)
                if live(c):
                    need_apart(pool, "a_copied01", c)
                    causal01(A_sb)
                    need_apart(pool, "a_copied", c)
                    causal2(A_sb, "a_masked")
                if live(b):
                    need(pool, "rsum_rdy", b)
                    for tile in range(2):
                        v = lgs[:, kb % 2, tile, :].rearrange("p (h m) -> p h m", h=H)
                        last = nc.gpsimd.tensor_tensor(v, v, rsum[:, tile, :].unsqueeze(2).broadcast_to([P, H, M]), ALU.mult)
                    last.then_inc(S["pnorm_rdy"], 1)

            def causal01(buf):
                d = buf[:, 0:2, :].rearrange("p two (h t) -> p (two h) t", h=2)[:, :, 0:P]
                nc.gpsimd.affine_select(out=d, in_=d, compare_op=ALU.is_ge, fill=0.0, base=0, pattern=[[0, H], [1, P]], channel_multiplier=-1)

            def causal2(buf, name):
                d = buf[:, 2, :].rearrange("p (h t) -> p h t", h=H)
                nc.gpsimd.affine_select(out=d, in_=d, compare_op=ALU.is_ge, fill=0.0, base=0, pattern=[[0, H], [1, P]],
                                        channel_multiplier=-1).then_inc(S[name], 1)

            pipeline(pool, iteration)

        @block.scalar
        def _(act):
            act.wait_ge(S["set_zero"], 1)
            rows = ((R_C, NB, "c"), (R_LNW, NE, "exp_ln_w"), (R_LNB, NE, "exp_ln_b"), (R_B1, NE * NC, "b1"), (R_RW, 1, "router_ln_w"), (R_RB, 1, "router_ln_b"))
            for r, n, name in rows:
                src = inp[name] if n > 1 else inp[name].unsqueeze(0)
                if name == "b1":
                    src = src.rearrange("e (c p) -> (e c) p", p=P)
                act.dma_start(vec_rows[r:r + n, :], src).then_inc(S["ld_c" if name == "c" else "ld_rows"], 16)
            act.dma_start(vec_rows[R_GN:R_GN + 1, :].rearrange("o (h c) -> o h c", h=H),
                          inp["gnorm_w"].unsqueeze(0).unsqueeze(1).broadcast_to([1, H, HD])).then_inc(S["ld_rows"], 16)
            act.dma_start(wmod[:], inp["wmod"]).then_inc(S["ld_wmod"], 16)
            nc.scalar.preload_act_table_set("natural_log_exp_and_others")
            act.wait_ge(S["vec_rdy"], 1)
            nc.scalar.activation(cT[:, 1, :], cT[:, 0, :], ACT.Exp, scale=-1.0).then_inc(S["silu_e"], 1)
            for n, w2, bias in ((0, "sk_w2", "sk_b2"), (1, "sv_w2", "sv_b2")):
                act.dma_start(low2[n * LOW:(n + 1) * LOW, 2 * n:2 * n + 2, :],
                              inp[w2].rearrange("r (a c) -> r a c", a=2)).then_inc(S["low2_ld"], 16)
                act.dma_start(low2[2 * LOW:2 * LOW + 1, 2 * n:2 * n + 2, :],
                              inp[bias].unsqueeze(0).rearrange("o (a c) -> o a c", a=2)).then_inc(S["low2_ld"], 16)

            def iteration(i, k):
                a, b, c, e, d = i, i - 1, i - 2, i - 3, i - 4
                kb, kc, kd = (k - 1) % 4, (k - 2) % 4, (k - 4) % 4
                if live(b):
                    need(act, "wkT_tp", b)
                    need(act, "lg_mm", b - 2)
                    nc.scalar.copy(wk_tok[:, kb % 2, :, :], b3[:].rearrange("p (c n) -> p c n", c=2)).then_inc(S["wk_tok_rdy"], 1)
                if live(e):
                    need(act, "ms_mm", e)
                    need(act, "t1_rdy", e - 1)
                    nc.scalar.activation(rs[:], b6[:, 0:T], ACT.Ln, bias=eps_col).then_inc(S["rsln_rdy"], 1)
                    need(act, "rsln_rdy", e)
                    nc.scalar.activation(rs[:], rs[:], ACT.Exp, scale=-0.5).then_inc(S["rs_rdy"], 1)
                if live(b):
                    need(act, "z_rdy", b)
                    need(act, "rz_rdy", b - 1)
                    nc.scalar.activation(r0[:], z[:, kb % 2, :, :], ACT.Ln).then_inc(S["lnz_rdy"], 1)
                if live(b):
                    need(act, "lnz_rdy", b)
                    nc.scalar.activation(r0[:], r0[:], ACT.Exp, scale=-1.0).then_inc(S["r0_rdy"], 1)
                if live(a):
                    if isinstance(a, int) and a == 0:
                        act.wait_ge(S["mod_rdy"], 1)
                    need(act, "xT_tp", a)
                    need(act, "glt_mm", a - 2)
                    nc.scalar.activation(hT[:, k % 2, :], b3[:, 0:T], ACT.Identity, bias=saT[:, bass.ds(a, 1)],
                                         scale=caT[:, bass.ds(a, 1)]).then_inc(S["hT_rdy"], 1)
                if live(d):
                    need(act, "xhatT_tp", d)
                    nc.scalar.copy(xhatT[:, kd % 2, :], b3[:, T:2 * T]).then_inc(S["xhatT_rdy"], 1)
                if live(b):
                    need(act, "s_mm01", b)
                    for n in range(2):
                        last = nc.scalar.copy(S_sb[:, n, :], banks[n][:])
                    last.then_inc(S["s_copied01"], 1)
                    need(act, "s_mm", b)
                    nc.scalar.copy(S_sb[:, 2, :], banks[2][:]).then_inc(S["s_copied"], 1)
                if live(a):
                    need(act, "v_mm", a)
                    need(act, "oT_mm", a - 4)
                    nc.scalar.copy(v_tok[:, k, :, :], b3[:, 0:T].rearrange("p (c n) -> p c n", c=2)).then_inc(S["v_rdy"], 1)
                if live(d):
                    need(act, "rlog_mm", d)
                    nc.scalar.copy(rlog[:, bass.ds(d * 2, 2), :], b3[:, T:T + 2 * NE].rearrange("p (c n) -> p c n", c=2)).then_inc(S["rlog_rdy"], 1)
                if live(a):
                    need(act, "glt_mm", a)
                    need(act, "skv_mm", a - 2)
                    nc.scalar.copy(lT[0:2 * LOW, k % 2, :], b3[0:2 * LOW, T:2 * T]).then_inc(S["lT_rdy"], 1)
                if live(a):
                    need(act, "gate_rdy", a - 2)
                    nc.scalar.copy(g_sb[:, k % 2, :], b3[:, 0:T])
                    nc.scalar.activation(eg[:, k % 2, :], b3[:, 0:T], ACT.Exp, scale=-1.0).then_inc(S["eg_rdy"], 1)
                if live(c):
                    need(act, "a_mm01", c)
                    need(act, "oT_mm", c - 2)
                    for n in range(2):
                        last = nc.scalar.copy(A_sb[:, n, :], banks[n][:])
                    last.then_inc(S["a_copied01"], 1)
                    need(act, "a_mm", c)
                    nc.scalar.copy(A_sb[:, 2, :], banks[2][:]).then_inc(S["a_copied"], 1)
                if live(b):
                    need(act, "lgsub_rdy", b)
                    nc.scalar.activation(lgs[:, kb % 2, :, :], lgs[:, kb % 2, :, :], ACT.Exp).then_inc(S["pexp_rdy"], 1)
                if live(a):
                    need(act, "skv_mm", a)
                    need(act, "a_mm", a - 4)
                    nc.scalar.activation(wkT[:, k % 2, :, :], b4[:].rearrange("p (c n) -> p c n", c=2), ACT.Exp).then_inc(S["wkexp_rdy"], 1)
                    nc.scalar.activation(wvT[:, k, :, :], b5[:].rearrange("p (c n) -> p c n", c=2), ACT.Exp).then_inc(S["wexp_rdy"], 1)
                if live(c):
                    need(act, "oT_mm", c)
                    need(act, "ms_mm", c - 1)
                    nc.scalar.activation(sq[:], b7[:, 0:T], ACT.Square).then_inc(S["sq_rdy"], 1)
                if live(a):
                    need(act, "egc_rdy", a)
                    nc.scalar.activation(eg[:, k % 2, :], eg[:, k % 2, :], ACT.Ln, bias=1.0).then_inc(S["sigln_rdy"], 1)
                    need(act, "sigln_rdy", a)
                    nc.scalar.activation(eg[:, k % 2, :], eg[:, k % 2, :], ACT.Exp, scale=-1.0).then_inc(S["sig_rdy"], 1)

            pipeline(act, iteration)

        @block.vector
        def _(dve):
            chain = [0]

            def link(ins):
                chain[0] += 1
                ins.then_inc(S["dve_chain"], 1)
                dve.wait_ge(S["dve_chain"], chain[0])

            link(nc.vector.memset(vec_rows[:], 0.0))
            nc.vector.memset(low2[:], 0.0).then_inc(S["set_zero"], 1)
            nc.vector.memset(ones[:], 1.0).then_inc(S["xhat_st0"], 16)
            nc.vector.memset(sq[:], 1.0).then_inc(S["xhat_st1"], 16)
            nc.vector.memset(eps_col, EPS)
            nc.vector.memset(lnb_x[:], 0.0)
            nc.vector.memset(Qx[:], 0.0)
            nc.vector.memset(Px[:], 0.0)
            link(nc.vector.memset(lT[:], 0.0))
            nc.vector.memset(lT[2 * LOW:2 * LOW + 1, :, :], 1.0).then_inc(S["set_dve"], 1)
            dve.wait_ge(S["vec_tp"], 1)
            link(nc.vector.tensor_copy(vecT[:, 0:NROW], b3[:, 0:NROW]))
            nc.vector.tensor_copy(lnb_x[:].rearrange("p e m -> p (e m)")[:, 0:NE * NE:NE + 1], vecT[:, R_LNB:R_LNB + NE])
            nc.vector.tensor_copy(cT[:, 0, :], vecT[:, R_C:R_C + NB]).then_inc(S["vec_rdy"], 1)
            dve.wait_ge(S["silu_e"], 1)
            link(nc.vector.tensor_scalar(cT[:, 1, :], cT[:, 1, :], 1.0, None, ALU.add))
            link(nc.vector.reciprocal(cT[:, 2, :], cT[:, 1, :]))
            nc.vector.tensor_tensor(cT[:, 3, :], cT[:, 0, :], cT[:, 2, :], ALU.mult).then_inc(S["silu_rdy"], 1)
            dve.wait_ge(S["mod_mm"], 1)
            nc.vector.tensor_copy(saT[:], b3[:, 0:NB])
            nc.vector.tensor_scalar(caT[:], b3[:, NB:2 * NB], 1.0, None, ALU.add).then_inc(S["mod_rdy"], 1)
            def modulation_rows():
                for n, m in ((0, GA), (1, GB)):
                    g = b7[0:NB, m * D:(m + 1) * D]
                    link(nc.vector.tensor_copy(mod_tmp[:, n, 0, :], g))
                    link(nc.vector.scalar_tensor_tensor(out=mod_tmp[:, n, 1, :], in0=mod_tmp[:, n, 0, :], scalar=-1.0,
                                                        in1=mod_tmp[:, n, 0, :], op0=ALU.mult, op1=ALU.max))
                    nc.vector.tensor_scalar(mod_tmp[:, n, 1, :], mod_tmp[:, n, 1, :], 0.25, None, ALU.max)
                    link(nc.vector.tensor_scalar(mod_tmp[:, n, 0, :], mod_tmp[:, n, 0, :], 0.0, 2.0, ALU.is_ge, ALU.mult))
                    nc.vector.scalar_tensor_tensor(out=mod_rows[:, m * D:(m + 1) * D], in0=mod_tmp[:, n, 0, :], scalar=-1.0,
                                                   in1=mod_tmp[:, n, 1, :], op0=ALU.add, op1=ALU.mult)
                nc.vector.tensor_copy(mod_rows[:, SB_ * D:(SB_ + 1) * D], b7[0:NB, SB_ * D:(SB_ + 1) * D])
                nc.vector.tensor_scalar(mod_rows[:, CB * D:(CB + 1) * D], b7[0:NB, CB * D:(CB + 1) * D], 1.0, None,
                                        ALU.add).then_inc(S["mod_rdy"], 1)

            def ln_sums(src2, st, n):
                for tile in range(2):
                    last = nc.vector.bn_stats(st[:, tile, :], src2[tile])
                last.then_inc(S[f"st{n}_rdy"], 1)

            def ln_moments(st, mv, ve, b, n):
                for tile in range(2):
                    last = nc.vector.bn_aggr(mv[:, tile, :], st[:, tile, :])
                last.then_inc(S[f"mv{n}_rdy"], 1)
                need(dve, f"mv{n}_rdy", b)
                nc.vector.tensor_scalar(ve[:], mv[:, :, 1], EPS, None, ALU.add).then_inc(S[f"ve{n}_rdy"], 1)

            def ln_stats(src2, st, mv, ve, b, n):
                ln_sums(src2, st, n)
                need_apart(dve, f"st{n}_rdy", b)
                ln_moments(st, mv, ve, b, n)

            def normalize(dst2, src2, mv, r, name):
                for tile in range(2):
                    last = nc.vector.tensor_scalar(dst2[tile], src2[tile], mv[:, tile, 0:1], r[:, tile:tile + 1],
                                                   ALU.subtract, ALU.mult)
                last.then_inc(S[name], 1)

            def x_tile(b, tile):
                return x_sb[:, bass.ds(b * 2 + tile, 1), :].squeeze(1) if not isinstance(b, int) else x_sb[:, b * 2 + tile, :]

            top_count = [0]

            def best_two(b0, b1):
                dve.wait_ge(S["rlog_rdy"], b1)
                tiles = slice(2 * b0, 2 * b1)
                nc.vector.tensor_tensor(rlog[:, tiles, :], rlog[:, tiles, :], rbias[:].unsqueeze(1).broadcast_to([P, 2 * (b1 - b0), NE]),
                                        ALU.add).then_inc(S["top_step"], 1)
                top_count[0] += 1
                dve.wait_ge(S["top_step"], top_count[0])
                for j in range(2 * b0, 2 * b1):
                    last = nc.vector.max(top[:, j, :], rlog[:, j, :])
                last.then_inc(S["top_step"], 1)
                top_count[0] += 1
                dve.wait_ge(S["top_step"], top_count[0])
                for j in range(2 * b0, 2 * b1):
                    last = nc.vector.max_index(topi[:, j, :], top[:, j, :], rlog[:, j, :])
                last.then_inc(S["top_rdy"], 1)

            def iteration(i, k):
                a, b, c, e = i, i - 1, i - 2, i - 3
                kb, kc, ke = (k - 1) % 4, (k - 2) % 4, (k - 3) % 4
                if live(a):
                    if isinstance(a, int) and a == 0:
                        dve.wait_ge(S["ld_x0"], 16)
                    if isinstance(a, int) and a == 2:
                        dve.wait_ge(S["ld_x"], 16)
                    ln_sums([x_tile(a, 0), x_tile(a, 1)], st1, 1)
                    need(dve, "st1_rdy", a)
                if live(b):
                    need(dve, "clip_rdy", b)
                    for j in range(4):
                        w = wkT[:, kb % 2, j, :] if j < 2 else wvT[:, kb, j - 2, :]
                        last = nc.vector.tensor_tensor_scan(z[:, kb % 2, j, :], ones[:], w, 0.0, ALU.mult, ALU.add)
                    last.then_inc(S["z_rdy"], 1)
                if live(a):
                    ln_moments(st1, mv1, ve1, a, 1)
                if live(e):
                    need(dve, "rs_rdy", e)
                    nc.vector.tensor_tensor(onT1[:], b7[:, 0:T], rs[:], ALU.mult).then_inc(S["t1_rdy"], 1)
                if live(e):
                    need(dve, "t1_rdy", e)
                    need(dve, "gate_rdy", e)
                    nc.vector.tensor_tensor(onT[:, ke % 2, :], onT1[:], gate[:, ke, :], ALU.mult).then_inc(S["on_rdy"], 1)
                if live(a):
                    need(dve, "rstd1_rdy", a)
                    need(dve, "xT_tp", a - 2)
                    normalize([xn[:, k % 2, t, :] for t in range(2)], [x_tile(a, 0), x_tile(a, 1)], mv1, rs1, "xn_rdy")
                    if isinstance(a, int) and a == 0:
                        modulation_rows()
                        dve.wait_ge(S["ld_w"], 16 * N_W)
                        nc.vector.tensor_scalar(Wog[:], Wo[:], vecT[:, R_GN:R_GN + 1], None, ALU.mult)
                        nc.vector.tensor_scalar(routwg[:], routw[:], vecT[:, R_RW:R_RW + 1], None, ALU.mult).then_inc(S["vec_rdy"], 1)
                        dve.wait_ge(S["ffn_mm"], 1)
                        nc.vector.tensor_tensor(rbias[:], b6[:, 0:NE], rbias[:], ALU.add).then_inc(S["ffn_bias"], 1)
                if live(b):
                    need(dve, "r0_rdy", b)
                    nc.vector.tensor_tensor(z[:, kb % 2, :, :], z[:, kb % 2, :, :], r0[:], ALU.mult).then_inc(S["nu_rdy"], 1)
                if live(e):
                    need(dve, "out_mm", e)
                    xe = x_sb[:, bass.ds(e * 2, 2), :]
                    nc.vector.tensor_tensor(xe, xe, b7[:, 0:T].rearrange("p (c n) -> p c n", c=2), ALU.add).then_inc(S["x1_rdy"], 1)
                if live(c):
                    need(dve, "pT_tp", c)
                    need(dve, "a_mm", c - 2)
                    for pair in range(2):
                        for half in range(2):
                            q = slice(half * M, (half + 1) * M)
                            last = nc.vector.scalar_tensor_tensor(
                                out=Px[q, kc % 2, 2 * pair + half, :], in0=b6[q, pair * T:(pair + 1) * T], scalar=-1.0,
                                in1=rz[q, kc % 2, 2 + pair, :], op0=ALU.mult, op1=ALU.mult)
                    last.then_inc(S["px_rdy"], 1)
                if live(e):
                    need_apart(dve, "x1_rdy", e)
                    ln_stats([x_tile(e, 0), x_tile(e, 1)], st2, mv2, ve2, e, 2)
                if live(a):
                    need(dve, "qk_mm", a)
                    need(dve, "rope_rdy", a - 2)
                    for n, bank in ((0, b4), (2, b5)):
                        nc.vector.tensor_tensor(rot[:, k % 2, n, :], bank[:, 0:T], cosT[:], ALU.mult)
                        last = nc.vector.tensor_tensor(rot[:, k % 2, n + 1, :], bank[:, T:2 * T], sinT[:], ALU.mult)
                    last.then_inc(S["ropemul_rdy"], 1)
                if live(b):
                    need(dve, "nu_rdy", b)
                    nc.vector.scalar_tensor_tensor(out=rz[:, kb % 2, :, :], in0=z[:, kb % 2, :, :], scalar=-2.0, in1=r0[:],
                                                   op0=ALU.add, op1=ALU.mult).then_inc(S["rz_rdy"], 1)
                if live(e):
                    need(dve, "rstd2_rdy", e)
                    normalize([xn2[:, t, :] for t in range(2)], [x_tile(e, 0), x_tile(e, 1)], mv2, rs2, "xn2_rdy")
                    need(dve, "xn2_rdy", e)
                    cb = modb[:, ke, CB * D:(CB + 1) * D].unsqueeze(1).broadcast_to([P, 2, D])
                    sbb = modb[:, ke, SB_ * D:(SB_ + 1) * D].unsqueeze(1).broadcast_to([P, 2, D])
                    nc.vector.tensor_tensor(h2a[:], xn2[:], cb, ALU.mult).then_inc(S["h2a_rdy"], 1)
                    need(dve, "h2a_rdy", e)
                    nc.vector.tensor_tensor(h2[:], h2a[:], sbb, ALU.add).then_inc(S["h2_rdy"], 1)
                if live(b):
                    need(dve, "lg_mm", b)
                    need(dve, "lgtok_tp", b - 2)
                    need(dve, "rz_rdy", b)
                    nc.vector.scalar_tensor_tensor(out=lg2[:, kb % 2, :, :], in0=b7[:].rearrange("p (c n) -> p c n", c=2),
                                                   scalar=-float(HD) ** -0.5, in1=rz[:, kb % 2, 0:2, :],
                                                   op0=ALU.mult, op1=ALU.mult).then_inc(S["lg2_rdy"], 1)
                if live(e):
                    need_apart(dve, "h2_rdy", e)
                    ln_stats([h2[:, t, :] for t in range(2)], st3, mv3, ve3, e, 3)
                if live(b):
                    need(dve, "lgtok_tp", b)
                    need(dve, "pT_tp", b - 2)
                    lgv = b6[:].rearrange("p (g m) -> p g m", m=M)
                    nc.vector.tensor_reduce(mx[:].rearrange("p c h -> p (c h)"), lgv, AX.X, ALU.max).then_inc(S["mx_rdy"], 1)
                if live(b):
                    need(dve, "mx_rdy", b)
                    nc.vector.tensor_tensor(lgs[:, kb % 2, :, :].rearrange("p c (h m) -> p (c h) m", h=H), lgv,
                                            mx[:].rearrange("p c h -> p (c h)").unsqueeze(2).broadcast_to([P, 2 * H, M]),
                                            ALU.subtract).then_inc(S["lgsub_rdy"], 1)
                if live(a):
                    need(dve, "eg_rdy", a)
                    nc.vector.tensor_scalar(eg[:, k % 2, :], eg[:, k % 2, :], 1e18, 0.0, ALU.min, ALU.max).then_inc(S["egc_rdy"], 1)
                if isinstance(i, int) and i == NB + 1:
                    dve.wait_ge(S["ffn_bias"], 1)
                    best_two(0, NB - 4)
                if live(e):
                    need(dve, "rstd3_rdy", e)
                    if not (isinstance(e, int) and e < 2):
                        dve.wait_ge(S[f"xhat_st{ke % 2}"], (e - ke % 2) * 8 + 16)
                    normalize([xhat[:, ke % 2, t, :] for t in range(2)], [h2[:, t, :] for t in range(2)], mv3, rs3, "xhat_rdy")
                if isinstance(i, int) and i == NB + 2:
                    best_two(NB - 4, NB - 2)
                if live(b):
                    need(dve, "pexp_rdy", b)
                    need(dve, "pnorm_rdy", b - 1)
                    nc.vector.tensor_reduce(mx[:].rearrange("p c h -> p (c h)"),
                                            lgs[:, kb % 2, :, :].rearrange("p c (h m) -> p (c h) m", h=H), AX.X,
                                            ALU.add).then_inc(S["sum_rdy"], 1)
                if live(a):
                    for w, exp_done, done in ((wkT[:, k % 2, :, :], "wkexp_rdy", "wkclip_rdy"), (wvT[:, k, :, :], "wexp_rdy", "clip_rdy")):
                        need(dve, exp_done, a)
                        nc.vector.tensor_scalar(w, w, float(np.exp(CLAMP)), float(np.exp(-CLAMP)), ALU.min, ALU.max).then_inc(S[done], 1)
                if live(b):
                    need(dve, "sum_rdy", b)
                    nc.vector.reciprocal(rsum[:], mx[:]).then_inc(S["rsum_rdy"], 1)

            pipeline(dve, iteration)
            dve.wait_ge(S["ffn_mm"], 2)
            nc.vector.tensor_copy(b1_rows[:], b4[0:NE, :]).then_inc(S["ffn_bias"], 1)
            best_two(NB - 2, NB)

        @block.tensor
        def _(pe):
            mm, tp = nc.tensor.matmul, nc.tensor.transpose
            pe.wait_ge(S["set_pool"], 9)
            pe.wait_ge(S["ld_c"], 16)
            pe.wait_ge(S["ld_rows"], 16 * 6)
            tp(b3[:, 0:P], vec_rows[:], ident[:]).then_inc(S["vec_tp"], 1)
            pe.wait_ge(S["silu_rdy"], 1)
            pe.wait_ge(S["ld_wmod"], 16)
            mm(b3[:, 0:NB], wmod[:, 0:D], cT[:, 3, :], start=True, stop=True)
            mm(b3[:, NB:2 * NB], wmod[:, D:2 * D], cT[:, 3, :], start=True, stop=True)
            mm(b7[0:NB, :], cT[:, 3, :], wmod[:, 2 * D:6 * D], start=True, stop=True).then_inc(S["mod_mm"], 1)
            pe.wait_ge(S["ld_qk"], 16 * N_QK)
            pe.wait_ge(S["set_dve"], 1)
            pe.wait_ge(S["mod_rdy"], 1)

            def iteration(i, k):
                a, b, c, e, d = i, i - 1, i - 2, i - 3, i - 4
                kb, kc, ke, kd = (k - 1) % 4, (k - 2) % 4, (k - 3) % 4, (k - 4) % 4
                if live(b):
                    need(pe, "wkclip_rdy", b)
                    need(pe, "eg_rdy", b)
                    for ch in range(2):
                        for pair in range(2):
                            last = tp(b3[:, ch * T + pair * P:ch * T + (pair + 1) * P],
                                      wkT[:, kb % 2, pair, ch * P:(ch + 1) * P], ident[:])
                    last.then_inc(S["wkT_tp"], 1)
                if live(e):
                    need(pe, "sq_rdy", e)
                    need(pe, "lgsub_rdy", c)
                    need(pe, "px_rdy", e)
                    mm(b6[:, 0:T], headmean[:], sq[:], start=True, stop=True).then_inc(S["ms_mm"], 1)
                if live(b):
                    need(pe, "rope_rdy", b)
                    need(pe, "a_copied", b - 2)
                    kk = kT[:, kb % 2, :]
                    for n in range(2):
                        last = mm(banks[n][:], kk[:, 0:P], Qx[:, kb % 2, 2 * n:2 * n + 2, :], start=True, stop=True)
                    last.then_inc(S["s_mm01"], 1)
                    mm(banks[2][:], kk[:, P:T], Qx[:, kb % 2, :, P:T], start=True, stop=True).then_inc(S["s_mm"], 1)
                if live(d):
                    need(pe, "xhat_rdy", d)
                    need(pe, "wk_tok_rdy", b)
                    if isinstance(d, int):
                        need(pe, "rlog_rdy", d - 1)
                    for tile in range(2):
                        last = tp(b3[:, T + tile * P:T + (tile + 1) * P], xhat[:, kd % 2, tile, :], ident[:])
                    last.then_inc(S["xhatT_tp"], 1)
                if live(a):
                    need(pe, "xn_rdy", a)
                    need(pe, "wk_tok_rdy", b)
                    for tile in range(2):
                        last = tp(b3[:, tile * P:(tile + 1) * P], xn[:, k % 2, tile, :], ident[:])
                    last.then_inc(S["xT_tp"], 1)
                if live(e):
                    need(pe, "on_rdy", e)
                    need(pe, "wob_rdy", e)
                    for tile in range(2):
                        last = mm(b7[:, tile * D:(tile + 1) * D], onT[:, ke % 2, tile * P:(tile + 1) * P], Wob[:, ke % 2, :],
                                  start=True, stop=True)
                    last.then_inc(S["out_mm"], 1)
                if live(c):
                    need(pe, "pnorm_rdy", c)
                    need(pe, "rsln_rdy", c - 1)
                    for pair in range(2):
                        for tile in range(2):
                            last = tp(b6[:, pair * T + tile * P:pair * T + (tile + 1) * P],
                                      lgs[:, kc % 2, tile, pair * P:(pair + 1) * P], ident[:])
                    last.then_inc(S["pT_tp"], 1)
                if live(a):
                    need(pe, "hT_rdy", a)
                    need(pe, "wexp_rdy", a - 1)
                    hh = hT[:, k % 2, :]
                    for bank, w, wr in ((b4, Wq, Wqr), (b5, Wk, Wkr)):
                        mm(bank[:, 0:T], w[:], hh, start=True, stop=True)
                        last = mm(bank[:, T:2 * T], wr[:], hh, start=True, stop=True)
                    last.then_inc(S["qk_mm"], 1)
                if live(d):
                    need(pe, "xhatT_rdy", d)
                    for tile in range(2):
                        last = mm(b3[:, T + tile * NE:T + (tile + 1) * NE], xhatT[:, kd % 2, tile * P:(tile + 1) * P], routwg[:],
                                  start=True, stop=True)
                    last.then_inc(S["rlog_mm"], 1)
                if live(a):
                    if isinstance(a, int) and a == 0:
                        pe.wait_ge(S["ld_w"], 16 * N_W)
                        pe.wait_ge(S["low2_ld"], 64)
                        mm(b6[:, 0:NE], vecT[:, R_RB:R_RB + 1].broadcast_to([P, P]), routw[:], start=True, stop=True).then_inc(S["ffn_mm"], 1)
                    need(pe, "xhatT_rdy", d)
                    for tile in range(2):
                        last = mm(b3[:, tile * D:(tile + 1) * D], hT[:, k % 2, tile * P:(tile + 1) * P], Wv[:], start=True, stop=True)
                    last.then_inc(S["v_mm"], 1)
                if live(b):
                    need(pe, "s_masked", b)
                    need(pe, "wk_tok_rdy", b)
                    need(pe, "x1_rdy", e)
                    for pair in range(2):
                        for ch in range(2):
                            for half in range(2):
                                h = 2 * pair + half
                                w = wk_tok[:, kb % 2, ch, h * M:(h + 1) * M]
                                o = b7[half * M:(half + 1) * M, pair * T + ch * P:(pair + 1) * T]
                                r = S_sb[:, pair, half * T:(half + 1) * T] if ch == 0 else \
                                    S_sb[:, 2, h * P:(h + 1) * P]
                                last = mm(o, w, r, start=ch == 0, stop=ch == 1)
                    last.then_inc(S["lg_mm"], 1)
                if live(a):
                    need(pe, "v_rdy", a)
                    need(pe, "rlog_rdy", d)
                    mm(b3[0:2 * LOW, T:2 * T], low1[:], hT[:, k % 2, :], start=True, stop=True)
                    mm(b3[:, 0:T], Wg[:], hT[:, k % 2, :], start=True, stop=True).then_inc(S["glt_mm"], 1)
                if live(c):
                    need(pe, "px_rdy", c)
                    need(pe, "s_copied", b)
                    for pair in range(2):
                        last = mm(banks[pair][:], wvT[:, kc, pair, 0:P], Px[:, kc % 2, 2 * pair:2 * pair + 2, :], start=True, stop=True)
                    last.then_inc(S["a_mm01"], 1)
                    for pair in range(2):
                        last = mm(banks[2][:, pair * T:(pair + 1) * T], wvT[:, kc, pair, P:T],
                                  Px[:, kc % 2, 2 * pair:2 * pair + 2, P:T], start=True, stop=True)
                    last.then_inc(S["a_mm"], 1)
                if live(b):
                    need(pe, "lg2_rdy", b)
                    need(pe, "px_rdy", c)
                    for tile in range(2):
                        for pair in range(2):
                            last = tp(b6[:, tile * T + pair * P:tile * T + (pair + 1) * P],
                                      lg2[:, kb % 2, pair, tile * P:(tile + 1) * P], ident[:])
                    last.then_inc(S["lgtok_tp"], 1)
                if live(a):
                    need(pe, "lT_rdy", a)
                    need(pe, "ropemul_rdy", a)
                    for n in range(4):
                        last = mm((b4, b5)[n // 2][:, (n % 2) * T:(n % 2 + 1) * T], low2[:, n, :], lT[:, k % 2, :], start=True, stop=True)
                    last.then_inc(S["skv_mm"], 1)
                if live(c):
                    need(pe, "a_masked", c)
                    need(pe, "lg2_rdy", b)
                    need(pe, "x1_rdy", e)
                    for ch in range(2):
                        for h in range(H):
                            r = A_sb[:, h // 2, (h % 2) * T:(h % 2 + 1) * T] if ch == 0 else A_sb[:, 2, h * P:(h + 1) * P]
                            last = mm(b7[h * HD:(h + 1) * HD, ch * P:T], v_tok[:, kc, ch, h * HD:(h + 1) * HD], r,
                                      start=ch == 0, stop=ch == 1)
                    last.then_inc(S["oT_mm"], 1)
                if isinstance(i, int):
                    if i == 0:
                        pe.wait_ge(S["mod_rdy"], 2)
                    if i == NB + 2:
                        pe.wait_ge(S["ld_ffn"], 32)
                        for x in range(NE):
                            last = mm(b4[0:NE, :], lnb_x[:, x, :], w1s[:, x, :], start=x == 0, stop=x == NE - 1)
                        last.then_inc(S["ffn_mm"], 1)

            pipeline(pe, iteration)

        ctx.close()
        ctx = outer
        NC2 = 2 * NT
        STEPS = 12
        NS = -(-(NC2 + NE - 1) // STEPS) * STEPS
        NROUND = NS // STEPS
        LAG_T, LAG_U, LAG_D, LAG_S = 3, 4, 5, 7
        RING = dict(gath=4, scat=6)
        PAIR = NB // (NROUND - 1)
        GROUP = 4
        NG = NT // GROUP
        I32 = mybir.dt.int32
        b2b = sb("b2b", [P, NE, D])
        olw, olb = sb("olw", [P, D]), sb("olb", [P, D])
        gbb = sb("gbb", [P, NB, D])
        outw = sb("outw", [P, NB, D])
        iota_e = sb("iota_e", [P, NE])
        iota_lo = sb("iota_lo", [P, P], BF16)
        iota_hi = sb("iota_hi", [P, NS], BF16)
        token = sb("token", [P, 1]); column = sb("column", [P, NC2])
        spare = sb("spare", [P, NS])
        upper = sb("upper", [P, P], BF16); ones_b = sb("ones_b", [P, P], BF16)
        topf = sb("topf", [P, NT, 2])
        pw = sb("pw", [P, NT, 4])
        onehot = sb("onehot", [P, NE, NC2], BF16)
        tot = sb("tot", [P, NE, NC2])
        cum = sb("cum", [P, NE, NC2])
        ones_c = sb("ones_c", [P, NE * NC2])
        cnt = sb("cnt", [P, NE]); cnt_i = sb("cnt_i", [P, NE], I32); ntile = sb("ntile", [P, NE]); tend = sb("tend", [P, NE])
        shift = sb("shift", [P, NE])
        slot_f = sb("slot_f", [P, NC2]); slot_i = sb("slot_i", [P, NC2], I32)
        hi_i = sb("hi_i", [P, NC2], I32); lo_i = sb("lo_i", [P, NC2], I32)
        hi_f = sb("hi_f", [P, NC2], BF16); lo_f = sb("lo_f", [P, NC2], BF16)
        ohlo = sb("ohlo", [P, NC2, P], BF16)
        ohhi = sb("ohhi", [P, NC2, NS], BF16)
        ohcode = sb("ohcode", [P, NC2, 2, NS], BF16)
        CH = 8
        past = sb("past", [P, NE - 1, NS])
        exp_f = sb("exp_f", [P, NS]); exp_i = sb("exp_i", [P, NS], I32)
        colnum = sb("colnum", [P, NS]); code = sb("code", [P, NS]); empty = sb("empty", [P, NS])
        idx = sb("idx", [P, NS, 2], U32)
        idxr = sb("idxr", [P, STEPS, 2], U32)
        xg = sb("xg", [P, RING["gath"], D])
        gelu_out = sb("gelu_out", [P, 1])
        waited = sb("waited", [1, 1])
        xgT = sb("xgT", [P, 2, P])
        w1c = sb("w1c", [P, 2, FF]); b1c = sb("b1c", [P, 2, NC])
        hid = sb("hid", [P, 2, NC, P])
        y = sb("y", [P, RING["scat"], D])
        ROWS = P * NC2 + P * NS
        y_dram = nc.dram_tensor("y_dram", [ROWS, D], F32, kind="Internal").ap()
        yk = sb("yk", [P, 3, GROUP, 2, D])
        y0 = sb("y0", [P, 2, GROUP, D])
        acc = sb("acc", [P, 2, GROUP, D])
        st4, mv4, ve4, rs4 = sb("st4", [P, GROUP, 6]), sb("mv4", [P, 2, GROUP, 2]), sb("ve4", [P, GROUP]), sb("rs4", [P, 2, GROUP])
        nmr = sb("nmr", [P, 2, GROUP])
        halves4 = sb("halves4", [P, GROUP])
        yn = sb("yn", [P, GROUP, D]); yo = sb("yo", [P, 2, GROUP, D])
        names = """f_ld f_ops f_iota f_s0 f_s f_oh f_count ohlo_rdy ohcol_rdy ohhi_rdy ohtok_rdy inv_mm idx_set f_fin outb_rdy waits_done
            idxr_rdy gath0 gath1 gath2 gath3 tile_tp xgT_rdy w1c_rdy up_mm hid_rdy down_mm y_rdy scat0 scat1 scat2 scat3 scat4 scat5
            yk_ld0 yk_ld1 yk_ld2 y0_rdy acc_rdy st4_rdy mv4_rdy ve4_rdy rs4_rdy nmr_rdy yn_rdy yo_rdy out_rdy out_st""".split()
        S.update({n: sem(n) for n in names})
        block = ctx.enter_context(nc.Block())
        up_bank, down_bank, tile_bank = banks[0:2], banks[2:4], banks[4:6]

        def need_tile(eng, name, n, k):
            if isinstance(n, int) and not 0 <= n * STEPS + k < NS:
                return
            eng.wait_ge(S[name], n * STEPS + k + 1)

        def need_ring(eng, name, n, k):
            if isinstance(n, int) and not 0 <= n * STEPS + k < NS:
                return
            ring = RING[name]
            eng.wait_ge(S[f"{name}{k % ring}"], (n * (STEPS // ring) + k // ring + 1) * 16)

        def has_tile(n, k):
            return not isinstance(n, int) or 0 <= n * STEPS + k < NS

        def tiles(eng, step):
            for k in range(STEPS):
                step(0, k)
            with eng.Fori(1, NROUND) as n:
                for k in range(STEPS):
                    step(n, k)
            for k in range(LAG_S + 1):
                step(NROUND, k)

        @block.sync
        def _(sp):
            sp.dma_start(b2b[:], inp["b2"].rearrange("e d -> (e d)").partition_broadcast(P).rearrange("p (e d) -> p e d", e=NE)).then_inc(S["f_ld"], 16)
            sp.dma_start(olw[:], inp["out_ln_w"].partition_broadcast(P)).then_inc(S["f_ld"], 16)
            sp.dma_start(olb[:], inp["out_ln_b"].partition_broadcast(P)).then_inc(S["f_ld"], 16)
            sp.dma_start(gbb[:], mod_dram[:, GB * D:(GB + 1) * D].partition_broadcast(P)).then_inc(S["f_ld"], 16)
            for r in range(RING["scat"]):
                sp.wait_ge(S[f"scat{r}"], 16 * (NS // RING["scat"]))
            yv = y_dram[0:P * NC2, :].rearrange("(p g c) d -> p g (c d)", p=P, g=NG)
            ov = out.rearrange("b (c p) d -> p (b c) d", p=P)

            def load(g, r):
                sp.dma_start(yk[:, r, :, :, :].rearrange("p t k d -> p (t k d)"), yv[:, g, :]).then_inc(S[f"yk_ld{r}"], 16)

            for g in range(NG):
                if g >= 3:
                    sp.wait_ge(S["acc_rdy"], g - 2)
                load(g, g % 3)
            for g in range(NG):
                sp.wait_ge(S["out_rdy"], g + 1)
                sp.dma_start(ov[:, g * GROUP:(g + 1) * GROUP, :], x_sb[:, g * GROUP:(g + 1) * GROUP, :]).then_inc(S["out_st"], 16)
            sp.wait_ge(S["out_st"], 16 * NG)

        @block.gpsimd
        def _(pool):
            small = dict(allow_small_or_imprecise_dtypes=True)
            nc.gpsimd.iota(iota_e[:], pattern=[[1, NE]], base=0, channel_multiplier=0, **small).then_inc(S["f_iota"], 1)
            nc.gpsimd.memset(upper[:], -1.0)
            nc.gpsimd.memset(ones_b[:], 1.0).then_inc(S["f_iota"], 1)
            pool.wait_ge(S["f_iota"], 2)
            nc.gpsimd.affine_select(out=upper[:], in_=upper[:], compare_op=ALU.is_ge, fill=0.0, base=0,
                                    pattern=[[-1, P]], channel_multiplier=1)
            nc.gpsimd.memset(ones_c[:], 1.0).then_inc(S["f_iota"], 1)
            nc.gpsimd.iota(iota_lo[:], pattern=[[1, P]], base=0, channel_multiplier=0, **small)
            nc.gpsimd.iota(iota_hi[:], pattern=[[1, NS]], base=0, channel_multiplier=0, **small)
            nc.gpsimd.iota(token[:], pattern=[[0, 1]], base=0, channel_multiplier=1, **small)
            nc.gpsimd.iota(column[:], pattern=[[1, NC2]], base=1, channel_multiplier=0, **small)
            nc.gpsimd.iota(spare[:], pattern=[[P, NS]], base=P * NC2 + 1, channel_multiplier=1, **small)
            nc.gpsimd.memset(halves4[:], -0.5).then_inc(S["f_iota"], 1)
            for c in range(0, NC2, CH):
                pool.wait_ge(S["ohhi_rdy"], c // CH + 1)
                nc.gpsimd.tensor_tensor(ohcode[:, c:c + CH, 1, :], ohhi[:, c:c + CH, :], column[:, c:c + CH].unsqueeze(2).broadcast_to([P, CH, NS]),
                                        ALU.mult).then_inc(S["ohcol_rdy"], 1)

            def step(n, k):
                kk = (k - LAG_S) % STEPS
                if k % 2 == 0:
                    for name, back in (("tile_tp", RING["gath"]), ("idxr_rdy", 0), ("y_rdy", LAG_S)):
                        need_tile(pool, name, n, k - back + (has_tile(n, k + 1 - back)))
                if has_tile(n, k) and k % 2 == 0:
                    if not (isinstance(n, int) and n == 0 and k == 0):
                        pool.wait_ge(S["waits_done"], (n * STEPS + k) // 2 if isinstance(n, int) else n * (STEPS // 2) + k // 2)
                    nc.gpsimd.tensor_tensor(waited[:], halves4[0:1, 0:1], halves4[0:1, 0:1], ALU.mult).then_inc(S["waits_done"], 1)
                if has_tile(n, k):
                    nc.gpsimd.indirect_dma_start(xg[:, k % RING["gath"], :], None, xhat_dram,
                                                 bass.IndirectOffsetOnAxis(idxr[:, k, 0:1], 0)).then_inc(S[f"gath{k % RING['gath']}"], 16)
                if has_tile(n, k - LAG_S):
                    nc.gpsimd.indirect_dma_start(y_dram, bass.IndirectOffsetOnAxis(idxr[:, kk, 1:2], 0),
                                                 y[:, kk % RING["scat"], :], None).then_inc(S[f"scat{kk % RING['scat']}"], 16)
            tiles(pool, step)
            for g in range(NG + 2):
                if g < NG:
                    pool.wait_ge(S["ve4_rdy"], g + 1)
                    if g >= 2:
                        pool.wait_ge(S["yn_rdy"], g - 1)
                    nc.gpsimd.tensor_tensor(rs4[:, g % 2, :], ve4[:], halves4[:], ALU.pow).then_inc(S["rs4_rdy"], 1)
                if g >= 2:
                    pool.wait_ge(S["f_fin"], NROUND)
                    pool.wait_ge(S["yo_rdy"], g - 1)
                    xg_ = x_sb[:, (g - 2) * GROUP:(g - 1) * GROUP, :]
                    nc.gpsimd.tensor_tensor(xg_, xg_, yo[:, g % 2], ALU.add).then_inc(S["out_rdy"], 1)

        @block.scalar
        def _(act):
            act.wait_ge(S["f_s0"], 1)
            nc.scalar.activation(pw[:, :, 1], pw[:, :, 0], ACT.Exp).then_inc(S["f_s"], 1)
            act.wait_ge(S["f_s"], 1)
            for c in range(0, NC2, CH):
                act.wait_ge(S["ohhi_rdy"], c // CH + 1)
                nc.scalar.activation(ohcode[:, c:c + CH, 0, :], ohhi[:, c:c + CH, :], ACT.Copy, scale=token[:, 0:1]).then_inc(S["ohtok_rdy"], 1)
            nc.scalar.activation(gelu_out[:], pw[:, 0, 1:2], ACT.Gelu)

            def step(n, k):
                if has_tile(n, k - LAG_U):
                    r = (k - LAG_U) % 2
                    need_tile(act, "w1c_rdy", n, k - LAG_U)
                    need_tile(act, "down_mm", n, k - LAG_U - 2)
                    need_tile(act, "up_mm", n, k - LAG_U)
                    for j in range(NC):
                        last = nc.scalar.activation(hid[:, r, j, :], up_bank[r][:, j * P:(j + 1) * P], ACT.Gelu, bias=b1c[:, r, j:j + 1])
                    last.then_inc(S["hid_rdy"], 1)
            tiles(act, step)
            def first_choice(g):
                act.wait_ge(S[f"yk_ld{g % 3}"], 16 * (g // 3 + 1))
                if g >= 2:
                    act.wait_ge(S["acc_rdy"], g - 1)
                for t in range(GROUP):
                    last = nc.scalar.activation(y0[:, g % 2, t, :], yk[:, g % 3, t, 0, :], ACT.Copy, scale=pw[:, g * GROUP + t, 2:3])
                last.then_inc(S["y0_rdy"], 1)

            first_choice(0)
            first_choice(1)
            for g in range(NG):
                if g + 2 < NG:
                    first_choice(g + 2)
                act.wait_ge(S["nmr_rdy"], g + 1)
                if g >= 1:
                    act.wait_ge(S["yo_rdy"], g)
                for t in range(GROUP):
                    last = nc.scalar.activation(yn[:, t, :], acc[:, g % 2, t, :], ACT.Identity, scale=rs4[:, g % 2, t:t + 1], bias=nmr[:, g % 2, t:t + 1])
                last.then_inc(S["yn_rdy"], 1)

        @block.vector
        def _(dve):
            n_ops = [0]

            def link(ins):
                n_ops[0] += 1
                ins.then_inc(S["f_ops"], 1)
                dve.wait_ge(S["f_ops"], n_ops[0])

            tt, ts = nc.vector.tensor_tensor, nc.vector.tensor_scalar
            dve.wait_ge(S["top_rdy"], 3)
            tt(pw[:, :, 0], top[:, :, 1], top[:, :, 0], ALU.subtract).then_inc(S["f_s0"], 1)
            link(nc.vector.tensor_copy(topf[:], topi[:, :, 0:2]))
            dve.wait_ge(S["f_iota"], 1)
            tt(onehot[:].rearrange("p e (t k) -> p e t k", k=2), iota_e[:].unsqueeze(2).unsqueeze(3).broadcast_to([P, NE, NT, 2]),
               topf[:].unsqueeze(1).broadcast_to([P, NE, NT, 2]), ALU.is_equal).then_inc(S["f_oh"], 1)
            dve.wait_ge(S["f_s"], 1)
            link(ts(pw[:, :, 2], pw[:, :, 1], 1.0, None, ALU.add))
            link(nc.vector.reciprocal(pw[:, :, 2], pw[:, :, 2]))
            link(tt(pw[:, :, 3], pw[:, :, 1], pw[:, :, 2], ALU.mult))
            dve.wait_ge(S["f_count"], 2)
            dve.wait_ge(S["f_iota"], 3)
            link(nc.vector.tensor_tensor_scan(cum[:].rearrange("p e c -> p (e c)"), ones_c[:], banks[1][:], 0.0, ALU.mult, ALU.add))
            nc.vector.tensor_copy(cnt[:, 0:1], cum[:, 0, NC2 - 1:NC2])
            link(tt(cnt[:, 1:NE], cum[:, 1:NE, NC2 - 1], cum[:, 0:NE - 1, NC2 - 1], ALU.subtract))
            link(ts(cnt_i[:], cnt[:], float(P - 1), None, ALU.add))
            link(ts(cnt_i[:], cnt_i[:], 7, None, ALU.logical_shift_right))
            link(nc.vector.tensor_copy(ntile[:], cnt_i[:]))
            link(nc.vector.tensor_tensor_scan(tend[:], ones_c[:, 0:NE], ntile[:], 0.0, ALU.mult, ALU.add))
            link(tt(shift[:], tend[:], ntile[:], ALU.subtract))
            link(ts(shift[:], shift[:], float(P), None, ALU.mult))
            link(tt(shift[:], shift[:], cum[:, :, NC2 - 1], ALU.subtract))
            link(tt(shift[:], shift[:], cnt[:], ALU.add))
            link(tt(cum[:], cum[:], banks[0][:].rearrange("p (e c) -> p e c", e=NE), ALU.add))
            link(tt(cum[:], cum[:], shift[:].unsqueeze(2).broadcast_to([P, NE, NC2]), ALU.add))
            link(tt(tot[:], cum[:], onehot[:], ALU.mult))
            link(nc.vector.tensor_reduce(slot_f[:], tot[:].rearrange("p e c -> p c e"), AX.X, ALU.add))
            link(nc.vector.tensor_copy(slot_i[:], slot_f[:]))
            link(ts(hi_i[:], slot_i[:], 7, None, ALU.logical_shift_right))
            link(ts(lo_i[:], slot_i[:], P - 1, None, ALU.bitwise_and))
            nc.vector.tensor_copy(hi_f[:], hi_i[:])
            link(nc.vector.tensor_copy(lo_f[:], lo_i[:]))
            dve.wait_ge(S["f_iota"], 4)
            for c in range(0, NC2, CH):
                tt(ohhi[:, c:c + CH, :], iota_hi[:].unsqueeze(1).broadcast_to([P, CH, NS]),
                   hi_f[:, c:c + CH].unsqueeze(2).broadcast_to([P, CH, NS]), ALU.is_equal).then_inc(S["ohhi_rdy"], 1)
                tt(ohlo[:, c:c + CH, :], iota_lo[:].unsqueeze(1).broadcast_to([P, CH, P]),
                   lo_f[:, c:c + CH].unsqueeze(2).broadcast_to([P, CH, P]), ALU.is_equal).then_inc(S["ohlo_rdy"], 1)
            link(tt(past[:], iota_hi[:].unsqueeze(1).broadcast_to([P, NE - 1, NS]), tend[:, 0:NE - 1].unsqueeze(2).broadcast_to([P, NE - 1, NS]), ALU.is_ge))
            link(nc.vector.tensor_reduce(exp_f[:], past[:].rearrange("p e s -> p s e"), AX.X, ALU.add))
            nc.vector.tensor_copy(exp_i[:], exp_f[:])
            dve.wait_ge(S["ffn_mm"], 3)
            nc.vector.tensor_tensor(b1T[:].rearrange("p (e c) -> p e c", c=NC), banks[6][:, 0:NE * NC].rearrange("p (c e) -> p e c", e=NE),
                                    vecT[:, R_B1:R_B1 + NE * NC].rearrange("p (e c) -> p e c", c=NC), ALU.add)
            dve.wait_ge(S["inv_mm"], 1)
            nc.vector.tensor_copy(colnum[:], banks[2][:, NS:2 * NS])
            link(ts(empty[:], banks[2][:, NS:2 * NS], 1.0, None, ALU.is_lt))
            link(tt(code[:], empty[:], spare[:], ALU.mult))
            link(tt(code[:], code[:], colnum[:], ALU.add))
            link(nc.vector.scalar_tensor_tensor(out=code[:], in0=banks[2][:, 0:NS], scalar=float(NC2), in1=code[:], op0=ALU.mult, op1=ALU.add))
            link(ts(idx[:, :, 1], code[:], -1.0, None, ALU.add))
            link(ts(idx[:, :, 0], idx[:, :, 1], 1, None, ALU.logical_shift_right))
            link(ts(idx[:, :, 0], idx[:, :, 0], P * NT - 1, None, ALU.min))
            nc.vector.memset(ve4[:], 1.0).then_inc(S["idx_set"], 1)
            dve.wait_ge(S["idx_set"], 1)
            dve.wait_ge(S["f_ld"], 64)

            def expert_of(n, k):
                if isinstance(n, int):
                    j = n * STEPS + k
                    return dve.value_load(exp_i[0:1, j:j + 1], min_val=0, max_val=NE - 1)
                return dve.value_load(exp_i[0:1, bass.ds(n * STEPS + k, 1)], min_val=0, max_val=NE - 1)

            def step(n, k):
                if has_tile(n, k):
                    need_ring(dve, "scat", n, k - STEPS)
                    nc.vector.tensor_copy(idxr[:, k, :], idx[:, bass.ds(n * STEPS + k, 1), :].squeeze(1)).then_inc(S["idxr_rdy"], 1)
                if has_tile(n, k - LAG_T):
                    kk = k - LAG_T
                    e = expert_of(n, kk)
                    need_tile(dve, "hid_rdy", n, kk - 2)
                    nc.vector.tensor_scalar(w1c[:, kk % 2, :], w1s[:, bass.ds(e, 1), :].squeeze(1), vecT[:, bass.ds(e + R_LNW, 1)], None, ALU.mult)
                    nc.vector.tensor_copy(b1c[:, kk % 2, :], b1T[:, bass.ds(e * NC, NC)]).then_inc(S["w1c_rdy"], 1)
                    need_tile(dve, "tile_tp", n, kk)
                    nc.vector.tensor_copy(xgT[:, kk % 2, :], tile_bank[kk % 2][:, 0:P]).then_inc(S["xgT_rdy"], 1)
                if has_tile(n, k - LAG_D):
                    kk = k - LAG_D
                    e = expert_of(n, kk)
                    need_ring(dve, "scat", n, kk - RING["scat"])
                    need_tile(dve, "down_mm", n, kk)
                    tt(y[:, kk % RING["scat"], :], down_bank[kk % 2][:, 0:D], b2b[:, bass.ds(e, 1), :].squeeze(1), ALU.add).then_inc(S["y_rdy"], 1)
            def output_factors(n, b0, w):
                gv = gbb[:, bass.ds(b0, w), :]
                tt(outw[:, bass.ds(b0, w), :], gv, olw[:].unsqueeze(1).broadcast_to([P, w, D]), ALU.mult)
                tt(gv, gv, olb[:].unsqueeze(1).broadcast_to([P, w, D]), ALU.mult).then_inc(S["outb_rdy"], 1)
                dve.wait_ge(S["outb_rdy"], n)
                xv = x_sb[:, bass.ds(b0 * 2, 2 * w), :].rearrange("p (b c) d -> p b c d", c=2)
                tt(xv, xv, gv.unsqueeze(2).broadcast_to([P, w, 2, D]), ALU.add).then_inc(S["f_fin"], 1)

            for k in range(STEPS):
                step(0, k)
            with dve.Fori(1, NROUND) as n:
                for k in range(STEPS):
                    step(n, k)
                    if k == 0:
                        output_factors(n, (n - 1) * PAIR, PAIR)
            for k in range(LAG_S + 1):
                step(NROUND, k)
                if k == 0:
                    output_factors(NROUND, (NROUND - 1) * PAIR, NB - (NROUND - 1) * PAIR)
            for g in range(NG + 1):
                if g < NG:
                    dve.wait_ge(S["y0_rdy"], g + 1)
                    if g >= 2:
                        dve.wait_ge(S["yn_rdy"], g - 1)
                    for t in range(GROUP):
                        last = nc.vector.scalar_tensor_tensor(out=acc[:, g % 2, t, :], in0=yk[:, g % 3, t, 1, :], scalar=pw[:, g * GROUP + t, 3:4],
                                                              in1=y0[:, g % 2, t, :], op0=ALU.mult, op1=ALU.add)
                    last.then_inc(S["acc_rdy"], 1)
                if g >= 1:
                    dve.wait_ge(S["rs4_rdy"], g)
                    nc.vector.scalar_tensor_tensor(out=nmr[:, (g - 1) % 2, :], in0=mv4[:, (g - 1) % 2, :, 0], scalar=-1.0, in1=rs4[:, (g - 1) % 2, :],
                                                   op0=ALU.mult, op1=ALU.mult).then_inc(S["nmr_rdy"], 1)
                if g < NG:
                    dve.wait_ge(S["acc_rdy"], g + 1)
                    for t in range(GROUP):
                        last = nc.vector.bn_stats(st4[:, t, :], acc[:, g % 2, t, :])
                    last.then_inc(S["st4_rdy"], 1)
                if g < NG:
                    dve.wait_ge(S["st4_rdy"], g + 1)
                    for t in range(GROUP):
                        last = nc.vector.bn_aggr(mv4[:, g % 2, t, :], st4[:, t, :])
                    last.then_inc(S["mv4_rdy"], 1)
                    dve.wait_ge(S["mv4_rdy"], g + 1)
                    ts(ve4[:], mv4[:, g % 2, :, 1], EPS, None, ALU.add).then_inc(S["ve4_rdy"], 1)
                if g >= 1:
                    dve.wait_ge(S["yn_rdy"], g)
                    if g >= 3:
                        dve.wait_ge(S["out_rdy"], g - 2)
                    b0 = (g - 1) * GROUP // 2
                    v = lambda a: a.rearrange("p (b c) d -> p b c d", c=2)
                    tt(v(yo[:, (g - 1) % 2]), v(yn[:]), outw[:, b0:b0 + GROUP // 2, :].unsqueeze(2).broadcast_to([P, GROUP // 2, 2, D]), ALU.mult).then_inc(S["yo_rdy"], 1)

        @block.tensor
        def _(pe):
            mm = nc.tensor.matmul
            pe.wait_ge(S["ffn_bias"], 2)
            for j in range(NC):
                last = nc.tensor.transpose(banks[6][:, j * NE:(j + 1) * NE], b1_rows[:, j * P:(j + 1) * P], ident[0:NE, 0:NE])
            last.then_inc(S["ffn_mm"], 1)
            pe.wait_ge(S["f_oh"], 1)
            pe.wait_ge(S["f_iota"], 3)
            oh = onehot[:].rearrange("p e c -> p (e c)")
            mm(banks[1][:], ones_b[:], oh, start=True, stop=True).then_inc(S["f_count"], 1)
            mm(banks[0][:], upper[:], oh, start=True, stop=True).then_inc(S["f_count"], 1)
            for c in range(NC2):
                if c % CH == 0:
                    pe.wait_ge(S["ohlo_rdy"], c // CH + 1)
                    pe.wait_ge(S["ohcol_rdy"], c // CH + 1)
                    pe.wait_ge(S["ohtok_rdy"], c // CH + 1)
                last = mm(banks[2][:, 0:2 * NS], ohlo[:, c, :], ohcode[:, c, :, :], start=c == 0, stop=c == NC2 - 1)
            last.then_inc(S["inv_mm"], 1)
            pe.wait_ge(S["idx_set"], 1)

            def step(n, k):
                if has_tile(n, k - LAG_T):
                    kk = k - LAG_T
                    need_tile(pe, "xgT_rdy", n, kk - 2)
                    need_ring(pe, "gath", n, kk)
                    nc.tensor.transpose(tile_bank[kk % 2][:, 0:P], xg[:, kk % RING["gath"], :], ident[:]).then_inc(S["tile_tp"], 1)
                if has_tile(n, k - LAG_U):
                    kk = k - LAG_U
                    need_tile(pe, "hid_rdy", n, kk - 2)
                    need_tile(pe, "xgT_rdy", n, kk)
                    for j in range(NC):
                        last = mm(up_bank[kk % 2][:, j * P:(j + 1) * P], w1c[:, kk % 2, j * P:(j + 1) * P], xgT[:, kk % 2, :], start=True, stop=True)
                    last.then_inc(S["up_mm"], 1)
                if has_tile(n, k - LAG_D):
                    kk = k - LAG_D
                    if isinstance(n, int):
                        e = pe.value_load(exp_i[0:1, n * STEPS + kk:n * STEPS + kk + 1], min_val=0, max_val=NE - 1)
                    else:
                        e = pe.value_load(exp_i[0:1, bass.ds(n * STEPS + kk, 1)], min_val=0, max_val=NE - 1)
                    need_tile(pe, "y_rdy", n, kk - 2)
                    need_tile(pe, "hid_rdy", n, kk)
                    for j in range(NC):
                        last = mm(down_bank[kk % 2][:, 0:D], hid[:, kk % 2, j, :], w2s[:, bass.ds(e, 1), j, :].squeeze(1), start=j == 0, stop=j == NC - 1)
                    last.then_inc(S["down_mm"], 1)
            tiles(pe, step)


_INS = dict(x="L0_attn_hidden_states", Wq="L0_attn_Wq", Wk="L0_attn_Wk", Wv="L0_attn_Wv", Wg="L0_attn_Wg", Wo="L0_attn_Wo",
            sk_w1="L0_attn_sk_w1", sk_w2="L0_attn_sk_w2", sk_b2="L0_attn_sk_b2", sv_w1="L0_attn_sv_w1", sv_w2="L0_attn_sv_w2",
            sv_b2="L0_attn_sv_b2", gnorm_w="L0_attn_gnorm_w", router_ln_w="L0_ffn_router_ln_w", router_ln_b="L0_ffn_router_ln_b",
            router_w="L0_ffn_router_w", router_b="L0_ffn_router_b", exp_ln_w="L0_ffn_exp_ln_w", exp_ln_b="L0_ffn_exp_ln_b",
            w1="L0_ffn_w1", b1="L0_ffn_b1", w2="L0_ffn_w2", b2="L0_ffn_b2", out_ln_w="L0_ffn_out_ln_w", out_ln_b="L0_ffn_out_ln_b",
            c="L0_c", wmod="L0_wmod")


def rope_tables():
    half = HD // 2
    inv_freq = (1.0 / 10000.0 ** (np.arange(half, dtype=np.float32) / half)).astype(np.float32)
    ang = np.arange(T, dtype=np.float32)[None, :] * inv_freq[:, None]
    cos, sin = np.cos(ang), np.sin(ang)
    return (np.ascontiguousarray(np.tile(np.concatenate([cos, cos]), (H, 1))),
            np.ascontiguousarray(np.tile(np.concatenate([-sin, sin]), (H, 1))))


def kernel(**inputs):
    import concourse.bacc as bacc
    from concourse.bass_utils import run_bass_kernel_spmd

    nc = bacc.Bacc("TRN2", target_bir_lowering=False, num_devices=1)
    arrays = {n: np.ascontiguousarray(inputs[full]) for n, full in _INS.items()}
    arrays["cosT"], arrays["sinT"] = rope_tables()
    aps = {n: nc.dram_tensor(f"in_{n}", a.shape, F32, kind="ExternalInput").ap() for n, a in arrays.items()}
    out = nc.dram_tensor("out", [NB, T, D], F32, kind="ExternalOutput").ap()
    build(nc, aps, out)
    r = run_bass_kernel_spmd(nc, [{f"in_{n}": a for n, a in arrays.items()}], core_ids=[0])
    return r.results[0]["out"]
```
